# Optimizing a Trainium2 kernel written in Bass

```python
import numpy as np
import jax
import jax.numpy as jnp

def _softmax(x, axis=-1):
    return jax.nn.softmax(x, axis=axis)

def _gelu(x):
    return jax.nn.gelu(x, approximate=True)

def _silu(x):
    return jax.nn.silu(x)

def _sigmoid(x):
    return jax.nn.sigmoid(x)

def _layernorm(x, axis=-1, eps=1e-05):
    m = jnp.mean(x, axis=axis, keepdims=True)
    v = jnp.var(x, axis=axis, keepdims=True)
    return (x - m) / jnp.sqrt(v + eps)

def _scatter_add(tgt, idx, src, axis=0):
    return tgt.at[idx].add(src)

def _segment_sum(src, seg, n):
    return jax.ops.segment_sum(src, seg, n)
kernel_name = 'mk_seq_preln_d2_jaxref_r8_31c526'

def setup_inputs(seed: int=0):
    np.random.seed(seed)
    _w = jnp.asarray

    def _L0_attn_setup():
        import jax, jax.numpy as jnp
        import numpy as np
        B, T, D, H = (4, 256, 128, 16)
        HD = D // H
        ROPE_BASE = 10000.0

        def rotate_half(x):
            x1 = x[..., ::2]
            x2 = x[..., 1::2]
            return jnp.stack((-x2, x1), axis=-1).reshape(x.shape)

        def rope_tables(seq_len, dim, dtype=jnp.float32):
            inv = 1.0 / ROPE_BASE ** (jnp.arange(0, dim, 2, dtype=jnp.float32) / dim)
            t = jnp.arange(seq_len, dtype=jnp.float32)
            freqs = jnp.einsum('i,j->ij', t, inv)
            emb = jnp.concatenate((freqs, freqs), axis=-1)
            return (jnp.cos(emb).astype(dtype)[None, None], jnp.sin(emb).astype(dtype)[None, None])
        key = jax.random.key(seed)
        ks = jax.random.split(key, 9)
        s = 0.02
        return {'x': jax.random.normal(ks[0], (B, T, D), jnp.float32), 'Wq': jax.random.normal(ks[1], (D, D), jnp.float32) * s, 'bq': jnp.zeros((D,), jnp.float32), 'Wk': jax.random.normal(ks[2], (D, D), jnp.float32) * s, 'bk': jnp.zeros((D,), jnp.float32), 'Wv': jax.random.normal(ks[3], (D, D), jnp.float32) * s, 'bv': jnp.zeros((D,), jnp.float32), 'Wo': jax.random.normal(ks[4], (D, D), jnp.float32) * s, 'bo': jnp.zeros((D,), jnp.float32)}
    _L0_attn_in = _L0_attn_setup()

    def _L0_ffn_setup():
        import jax, jax.numpy as jnp
        import numpy as np
        BLOCK = 16
        _GRID = jnp.array([0.0, 0.5, 1.0, 1.5, 2.0, 3.0, 4.0, 6.0], dtype=jnp.float32)
        _MID = jnp.array([0.25, 0.75, 1.25, 1.75, 2.5, 3.5, 5.0], dtype=jnp.float32)

        def fp4_quant_dequant(x):
            shape = x.shape
            xb = x.reshape(shape[:-1] + (shape[-1] // BLOCK, BLOCK))
            scale = jnp.max(jnp.abs(xb), axis=-1, keepdims=True) / 6.0
            scale = jnp.maximum(scale, jnp.float32(1e-12))
            xn = xb / scale
            idx = jnp.searchsorted(_MID, jnp.abs(xn))
            q = _GRID[idx] * jnp.sign(xn) * scale
            return q.reshape(shape)

        def fp4_linear(x, w):
            xq = fp4_quant_dequant(x)
            wq = fp4_quant_dequant(w)
            return jnp.einsum('bsk,nk->bsn', xq, wq)
        key = jax.random.key(seed)
        k1, k2, k3, k4 = jax.random.split(key, 4)
        H, I = (128, 352)
        x = jax.random.normal(k1, (4, 512, H), dtype=jnp.float32)
        w_gate = jax.random.normal(k2, (I, H), dtype=jnp.float32) * 0.02
        w_up = jax.random.normal(k3, (I, H), dtype=jnp.float32) * 0.02
        w_down = jax.random.normal(k4, (H, I), dtype=jnp.float32) * 0.02
        return {'x': x, 'w_gate': w_gate, 'w_up': w_up, 'w_down': w_down}
    _L0_ffn_in = _L0_ffn_setup()

    def _L1_attn_setup():
        import jax, jax.numpy as jnp
        import numpy as np
        BATCH, SEQ, DIM, DSTATE = (4, 256, 128, 32)
        key = jax.random.key(seed)
        ks = jax.random.split(key, 6)
        x = jax.random.normal(ks[0], (BATCH, SEQ, DIM), dtype=jnp.float32)
        log_A = jax.random.normal(ks[1], (DIM, DSTATE), dtype=jnp.float32) * 0.01 - 4.0
        B_w = jax.random.normal(ks[2], (DSTATE, DIM), dtype=jnp.float32) / np.sqrt(DIM)
        B_b = jnp.zeros((DSTATE,), jnp.float32)
        C_w = jax.random.normal(ks[3], (DSTATE, DIM), dtype=jnp.float32) / np.sqrt(DIM)
        C_b = jnp.zeros((DSTATE,), jnp.float32)
        D_skip = jnp.ones((DIM,), jnp.float32)
        dt_w = jax.random.normal(ks[4], (DIM, DIM), dtype=jnp.float32) / np.sqrt(DIM)
        dt_b = jnp.zeros((DIM,), jnp.float32)
        return dict(x=x, log_A=log_A, B_w=B_w, B_b=B_b, C_w=C_w, C_b=C_b, D_skip=D_skip, dt_w=dt_w, dt_b=dt_b)
    _L1_attn_in = _L1_attn_setup()

    def _L1_ffn_setup():
        import jax, jax.numpy as jnp
        import numpy as np
        N_EMBD = 128
        N_EXPERTS = 8
        HIDDEN = 4 * N_EMBD
        B, T = (4, 256)
        key = jax.random.key(seed)
        kx, kg, k1, kb1, k2, kb2 = jax.random.split(key, 6)
        s_in = 1.0 / np.sqrt(N_EMBD)
        s_hid = 1.0 / np.sqrt(HIDDEN)
        return {'x': jax.random.normal(kx, (B, T, N_EMBD), dtype=jnp.float32), 'gate_w': jax.random.normal(kg, (N_EMBD, N_EXPERTS), dtype=jnp.float32) * s_in, 'w1': jax.random.normal(k1, (N_EXPERTS, N_EMBD, HIDDEN), dtype=jnp.float32) * s_in, 'b1': jnp.zeros((N_EXPERTS, HIDDEN), dtype=jnp.float32), 'w2': jax.random.normal(k2, (N_EXPERTS, HIDDEN, N_EMBD), dtype=jnp.float32) * s_hid, 'b2': jnp.zeros((N_EXPERTS, N_EMBD), dtype=jnp.float32)}
    _L1_ffn_in = _L1_ffn_setup()
    _d = {'L0_attn_x': _L0_attn_in['x'], 'L0_attn_Wq': _L0_attn_in['Wq'], 'L0_attn_bq': _L0_attn_in['bq'], 'L0_attn_Wk': _L0_attn_in['Wk'], 'L0_attn_bk': _L0_attn_in['bk'], 'L0_attn_Wv': _L0_attn_in['Wv'], 'L0_attn_bv': _L0_attn_in['bv'], 'L0_attn_Wo': _L0_attn_in['Wo'], 'L0_attn_bo': _L0_attn_in['bo'], 'L0_ffn_w_gate': _L0_ffn_in['w_gate'], 'L0_ffn_w_up': _L0_ffn_in['w_up'], 'L0_ffn_w_down': _L0_ffn_in['w_down'], 'L1_attn_log_A': _L1_attn_in['log_A'], 'L1_attn_B_w': _L1_attn_in['B_w'], 'L1_attn_B_b': _L1_attn_in['B_b'], 'L1_attn_C_w': _L1_attn_in['C_w'], 'L1_attn_C_b': _L1_attn_in['C_b'], 'L1_attn_D_skip': _L1_attn_in['D_skip'], 'L1_attn_dt_w': _L1_attn_in['dt_w'], 'L1_attn_dt_b': _L1_attn_in['dt_b'], 'L1_ffn_gate_w': _L1_ffn_in['gate_w'], 'L1_ffn_w1': _L1_ffn_in['w1'], 'L1_ffn_b1': _L1_ffn_in['b1'], 'L1_ffn_w2': _L1_ffn_in['w2'], 'L1_ffn_b2': _L1_ffn_in['b2']}
    _x0 = _d['L0_attn_x']
    _d['L0_attn_x'] = jax.random.normal(jax.random.fold_in(jax.random.key(seed), 1), (2, 1024, 128), dtype=_x0.dtype)
    del _x0
    return _d

def reference(L0_attn_x, L0_attn_Wq, L0_attn_bq, L0_attn_Wk, L0_attn_bk, L0_attn_Wv, L0_attn_bv, L0_attn_Wo, L0_attn_bo, L0_ffn_w_gate, L0_ffn_w_up, L0_ffn_w_down, L1_attn_log_A, L1_attn_B_w, L1_attn_B_b, L1_attn_C_w, L1_attn_C_b, L1_attn_D_skip, L1_attn_dt_w, L1_attn_dt_b, L1_ffn_gate_w, L1_ffn_w1, L1_ffn_b1, L1_ffn_w2, L1_ffn_b2):

    def _L0_attn_ref(x, Wq, bq, Wk, bk, Wv, bv, Wo, bo):
        import jax, jax.numpy as jnp
        import numpy as np
        B, T, D, H = (4, 256, 128, 16)
        HD = D // H
        ROPE_BASE = 10000.0

        def rotate_half(x):
            x1 = x[..., ::2]
            x2 = x[..., 1::2]
            return jnp.stack((-x2, x1), axis=-1).reshape(x.shape)

        def rope_tables(seq_len, dim, dtype=jnp.float32):
            inv = 1.0 / ROPE_BASE ** (jnp.arange(0, dim, 2, dtype=jnp.float32) / dim)
            t = jnp.arange(seq_len, dtype=jnp.float32)
            freqs = jnp.einsum('i,j->ij', t, inv)
            emb = jnp.concatenate((freqs, freqs), axis=-1)
            return (jnp.cos(emb).astype(dtype)[None, None], jnp.sin(emb).astype(dtype)[None, None])
        b, t, d = x.shape

        def proj(W, bias):
            return (x @ W.T + bias).reshape(b, t, H, HD).transpose(0, 2, 1, 3)
        q, k, v = (proj(Wq, bq), proj(Wk, bk), proj(Wv, bv))
        cos, sin = rope_tables(t, HD, x.dtype)
        q = q * cos + rotate_half(q) * sin
        k = k * cos + rotate_half(k) * sin
        scale = 1.0 / jnp.sqrt(jnp.asarray(HD, x.dtype))
        attn = jnp.einsum('bhqd,bhkd->bhqk', q, k) * scale
        attn = jax.nn.softmax(attn, axis=-1)
        out = jnp.einsum('bhqk,bhkd->bhqd', attn, v)
        out = out.transpose(0, 2, 1, 3).reshape(b, t, d)
        return out @ Wo.T + bo

    def _L0_ffn_ref(x, w_gate, w_up, w_down):
        import jax, jax.numpy as jnp
        import numpy as np
        BLOCK = 16
        _GRID = jnp.array([0.0, 0.5, 1.0, 1.5, 2.0, 3.0, 4.0, 6.0], dtype=jnp.float32)
        _MID = jnp.array([0.25, 0.75, 1.25, 1.75, 2.5, 3.5, 5.0], dtype=jnp.float32)

        def fp4_quant_dequant(x):
            shape = x.shape
            xb = x.reshape(shape[:-1] + (shape[-1] // BLOCK, BLOCK))
            scale = jnp.max(jnp.abs(xb), axis=-1, keepdims=True) / 6.0
            scale = jnp.maximum(scale, jnp.float32(1e-12))
            xn = xb / scale
            idx = jnp.searchsorted(_MID, jnp.abs(xn))
            q = _GRID[idx] * jnp.sign(xn) * scale
            return q.reshape(shape)

        def fp4_linear(x, w):
            xq = fp4_quant_dequant(x)
            wq = fp4_quant_dequant(w)
            return jnp.einsum('bsk,nk->bsn', xq, wq)
        gate = fp4_linear(x, w_gate)
        y = fp4_linear(x, w_up)
        h = jax.nn.silu(gate) * y
        return fp4_linear(h, w_down)

    def _L1_attn_ref(x, log_A, B_w, B_b, C_w, C_b, D_skip, dt_w, dt_b):
        import jax, jax.numpy as jnp
        import numpy as np
        BATCH, SEQ, DIM, DSTATE = (4, 256, 128, 32)
        Bsz, S, D = x.shape
        N = log_A.shape[1]
        dt = jax.nn.softplus(jnp.einsum('bsd,ed->bse', x, dt_w) + dt_b)
        A = -jnp.exp(log_A)
        b = jnp.einsum('bsd,nd->bsn', x, B_w) + B_b
        c = jnp.einsum('bsd,nd->bsn', x, C_w) + C_b

        def step(h, inp):
            x_t, dt_t, b_t, c_t = inp
            A_bar = jnp.exp(A[None] * dt_t[..., None])
            h = A_bar * h + (dt_t * x_t)[..., None] * b_t[:, None, :]
            y = jnp.einsum('bdn,bn->bd', h, c_t) + D_skip * x_t
            return (h, y)
        h0 = jnp.zeros((Bsz, D, N), x.dtype)
        xs = (jnp.swapaxes(x, 0, 1), jnp.swapaxes(dt, 0, 1), jnp.swapaxes(b, 0, 1), jnp.swapaxes(c, 0, 1))
        _, ys = jax.lax.scan(step, h0, xs)
        return jnp.swapaxes(ys, 0, 1)

    def _L1_ffn_ref(x, gate_w, w1, b1, w2, b2):
        import jax, jax.numpy as jnp
        import numpy as np
        N_EMBD = 128
        N_EXPERTS = 8
        HIDDEN = 4 * N_EMBD
        B, T = (4, 256)
        Bb, Tt, C = x.shape
        xf = x.reshape(Bb * Tt, C)
        logits = xf @ gate_w
        topk_vals, topk_idx = jax.lax.top_k(logits, 2)
        gates = jax.nn.softmax(topk_vals, axis=-1)
        h = jnp.einsum('nc,ech->neh', xf, w1) + b1[None]
        h = jax.nn.gelu(h, approximate=False)
        eo = jnp.einsum('neh,ehc->nec', h, w2) + b2[None]
        onehot = jax.nn.one_hot(topk_idx, N_EXPERTS, dtype=xf.dtype)
        comb = jnp.einsum('nk,nke->ne', gates, onehot)
        out = jnp.einsum('ne,nec->nc', comb, eo)
        return out.reshape(Bb, Tt, C)
    x = L0_attn_x
    x = x + _L0_attn_ref(_layernorm(x, axis=-1), L0_attn_Wq, L0_attn_bq, L0_attn_Wk, L0_attn_bk, L0_attn_Wv, L0_attn_bv, L0_attn_Wo, L0_attn_bo)
    x = x + _L0_ffn_ref(_layernorm(x, axis=-1), L0_ffn_w_gate, L0_ffn_w_up, L0_ffn_w_down)
    x = x + _L1_attn_ref(_layernorm(x, axis=-1), L1_attn_log_A, L1_attn_B_w, L1_attn_B_b, L1_attn_C_w, L1_attn_C_b, L1_attn_D_skip, L1_attn_dt_w, L1_attn_dt_b)
    x = x + _L1_ffn_ref(_layernorm(x, axis=-1), L1_ffn_gate_w, L1_ffn_w1, L1_ffn_b1, L1_ffn_w2, L1_ffn_b2)
    return x

_drawn_inputs = setup_inputs


def setup_inputs(seed=0):
    import zlib

    import numpy as np

    out = dict(_drawn_inputs(seed))
    spreads = {'L0_attn_bq': (0.0, 0.8),
     'L0_attn_bk': (0.0, 0.8),
     'L0_attn_bv': (0.0, 0.1),
     'L0_attn_bo': (0.0, 0.1),
     'L1_attn_B_b': (0.0, 0.1),
     'L1_attn_C_b': (0.0, 0.1),
     'L1_attn_D_skip': (1.0, 0.6),
     'L1_attn_dt_b': (0.0, 0.273),
     'L1_ffn_b1': (0.0, 0.8),
     'L1_ffn_b2': (0.0, 0.8)}
    factors = {'L0_attn_Wq': 8.0,
     'L0_attn_Wk': 8.0,
     'L0_attn_Wv': 8.0,
     'L0_ffn_w_gate': 3.606,
     'L0_ffn_w_up': 3.445,
     'L0_ffn_w_down': 3.407,
     'L1_attn_log_A': 7.014,
     'L1_ffn_gate_w': 5.328,
     'L1_ffn_w1': 5.368,
     'L1_ffn_w2': 4.779}
    for name, (base, spread) in spreads.items():
        noise = np.random.default_rng([zlib.crc32(name.encode()), seed]).standard_normal(out[name].shape)
        drawn = base * np.exp(spread * noise) if base else spread * noise
        out[name] = jnp.asarray(drawn.astype(out[name].dtype))
    for name, factor in factors.items():
        out[name] = (out[name] * factor).astype(out[name].dtype)
    return out
```

```python
from contextlib import ExitStack

import numpy as np

import concourse.bass as bass
from concourse import mybir

F32 = mybir.dt.float32
BF16 = mybir.dt.bfloat16
U32 = mybir.dt.uint32
ALU = mybir.AluOpType
ACT = mybir.ActivationFunctionType
AX = mybir.AxisListType

P = 128
BATCH = 2
SEQ = 1024
TOKENS = BATCH * SEQ
D = 128
TILES = TOKENS // P
BANK = 512
CHUNKS = TOKENS // BANK
EPS = 1e-5

HEADS = 16
HD = D // HEADS
QUAD = 4
PASSES = BATCH * HEADS // QUAD
QC = QUAD * HD
KT = SEQ // P
PARTS = 3
PROD = PARTS * PARTS * HD
ROWS = 96
ATT_SCALE = 1.0 / float(np.sqrt(np.float32(HD)))
VW = 16
STEPS = 2 * KT
MAX_TILES = 2
SETS = 3

MIDS = [0.25, 0.75, 1.25, 1.75, 2.5, 3.5, 5.0]
JUMPS = [0.5, 0.5, 0.5, 0.5, 1.0, 1.0, 2.0]
FFN = 352
QB = 16
NSTATE = 32
EXPERTS = 8
HIDDEN = 512
HT = HIDDEN // P

WF = 6 * D + FFN
QMAX = 4 * FFN


def build_kernel(nc, i, out):
    ctx = ExitStack()

    def sb(name, shape, dt=F32, stack=ctx):
        return stack.enter_context(nc.sbuf_tensor(name, shape, dt))

    def sem(name):
        return ctx.enter_context(nc.semaphore(name))

    with ctx:
        ps = ctx.enter_context(nc.psum_tensor("ps", [P, 8, BANK], F32))

        x = sb("x", [P, TILES, D])
        xc = sb("xc", [P, TILES, D])
        sq = sb("sq", [P, TILES, D])
        xt = sb("xt", [P, TOKENS])
        ident = sb("ident", [P, P])
        stat = sb("stat", [P, 4, TILES])

        expo = sb("expo", [P, TILES])

        wf = sb("wf", [P, WF])
        wfq = sb("wfq", [P, WF])
        wgu_t = sb("wgu_t", [P, 2, FFN])
        wd_t = sb("wd_t", [P, 3, D])

        wdt = sb("wdt", [P, D])
        wbc = sb("wbc", [P, 2, D])
        cols = sb("cols", [P, 4])
        log_a = sb("log_a", [P, NSTATE])
        sel = sb("sel", [P, NSTATE])
        sel_b = sb("sel_b", [P, NSTATE], BF16)
        wgate = sb("wgate", [P, EXPERTS])
        b1r = sb("b1r", [EXPERTS * HT, P])
        b2 = sb("b2", [EXPERTS, D])
        tri = sb("tri", [P, EXPERTS, EXPERTS])
        ssm_t = sb("ssm_t", [P, 3, D])
        b1t = sb("b1t", [P, (EXPERTS + 2) * HT])
        b1_now = sb("b1_now", [P, 2, HT])

        phase = ExitStack()

        def sb(name, shape, dt=F32):
            return phase.enter_context(nc.sbuf_tensor(name, shape, dt))

        w4 = sb("w4", [P, 4, D])
        perm = sb("perm", [P, 2, P])
        wt = sb("wt", [P, 6, D])
        bqk = sb("bqk", [P, 2])
        bperm = sb("bperm", [P, 2, 2])
        cos = sb("cos", [P, SEQ])
        sin = sb("sin", [P, SEQ])
        bv_all = sb("bv_all", [P, D])
        bo_all = sb("bo_all", [P, D])
        rot = sb("rot", [P, 2, 3, BANK])
        rest = sb("rest", [P, 2, BANK])
        parts = sb("parts", [P, 2, PARTS, BANK], BF16)
        v = sb("v", [P, PASSES, KT, QC])
        qs = [sb(f"qs{n}", [ROWS, 2, QUAD, BANK], BF16) for n in range(SETS)]
        ks = [sb(f"ks{n}", [ROWS, 2, QUAD, BANK], BF16) for n in range(SETS)]
        vq = [sb(f"vq{n}", [P, KT, QUAD, VW]) for n in range(SETS)]
        zrow = sb("zrow", [2, 2 * QUAD * BANK], BF16)
        prob = sb("prob", [P, 8, BANK])
        nmax = sb("nmax", [P, 2, 16])
        nmax_p = sb("nmax_p", [P, 32], BF16)
        nmax_t = sb("nmax_t", [P, 2, 32], BF16)
        o_sb = sb("o_sb", [P, 2, BANK])
        den = sb("den", [P, BATCH, HEADS * SEQ // P])
        rden = sb("rden", [P, BATCH, SEQ])
        num = sb("num", [P, TOKENS])

        phase.close()

        silu = sb("silu", [P, 2, FFN])
        hid = sb("hid", [P, 2, 4 * FFN])
        hid_q = sb("hid_q", [P, 2, 4 * FFN])
        hid_t = sb("hid_t", [P, 3, BANK])
        fa = sb("fa", [P, 2, QMAX])
        fx = sb("fx", [P, 2, QMAX])
        fs = sb("fs", [P, 2, QMAX], BF16)
        fg = sb("fg", [P, 7, QMAX], BF16)
        fblk = sb("fblk", [P, 2, 3, QMAX // QB])
        phase.close()

        a_neg = sb("a_neg", [P, NSTATE])
        dt = sb("dt", [P, TOKENS])
        dtx = sb("dtx", [P, TOKENS])
        zt = sb("zt", [P, TOKENS])
        bc32 = sb("bc32", [P, 2, TOKENS])
        bcp = sb("bcp", [P, 2, TOKENS], BF16)
        abar = sb("abar", [P, 2, SEQ])
        dbx = sb("dbx", [P, 2, SEQ])
        hst = sb("hst", [P, 2, SEQ])
        cbr = sb("cbr", [P, 2, SEQ])
        hc = sb("hc", [P, 2, SEQ])
        phase.close()

        w1 = sb("w1", [P, 2, HIDDEN])
        w2 = sb("w2", [P, 2, HT, D])
        act_t = sb("act_t", [P, 2, HT, BANK])
        lg = sb("lg", [P, TILES, EXPERTS])
        gt = sb("gt", [P, TILES, EXPERTS, EXPERTS])
        eq = sb("eq", [P, TILES, EXPERTS, EXPERTS])
        rank = sb("rank", [P, TILES, EXPERTS])
        is01 = sb("is01", [P, 2, TILES, EXPERTS])
        top = sb("top", [P, 6, TILES])
        comb = sb("comb", [P, TILES, EXPERTS])
        comb_t = sb("comb_t", [EXPERTS, TOKENS])
        phase.close()

        q_dram = nc.dram_tensor("q_dram", (PASSES, 2, PARTS, QC, BANK), BF16, kind="Internal").ap()
        k_dram = nc.dram_tensor("k_dram", (PASSES, 2, PARTS, QC, BANK), BF16, kind="Internal").ap()
        o_dram = nc.dram_tensor("o_dram", (PASSES, P, SEQ), F32, kind="Internal").ap()
        r_dram = nc.dram_tensor("r_dram", (BATCH, HEADS, SEQ), F32, kind="Internal").ap()

        s_x = [sem(f"s_x{n}") for n in range(2)]
        s_const = sem("s_const")
        s_centred = sem("s_centred")
        s_squared = sem("s_squared")
        s_var = sem("s_var")
        s_rstd = sem("s_rstd")
        s_normed = sem("s_normed")
        s_turned = sem("s_turned")
        s_xt = sem("s_xt")
        s_v1 = sem("s_v1")
        s_p1 = sem("s_p1")
        s_wt_ps = sem("s_wt_ps")
        s_wt = sem("s_wt")
        s_proj = sem("s_proj")
        s_rope_read = sem("s_rope_read")
        s_rope = sem("s_rope")
        s_part1 = sem("s_part1")
        s_rest = sem("s_rest")
        s_part2 = sem("s_part2")
        s_part3 = sem("s_part3")
        s_parts_out = [sem(f"s_parts_out{n}") for n in range(2)]
        s_v_ps = sem("s_v_ps")
        s_v = sem("s_v")
        s_set = sem("s_set")
        s_qk = [sem(f"s_qk{n}") for n in range(SETS)]
        s_score = sem("s_score")
        s_max = sem("s_max")
        s_nmax = sem("s_nmax")
        s_nrow = [sem(f"s_nrow{n}") for n in range(2)]
        s_st = sem("s_st")
        s_exp = sem("s_exp")
        s_pv = sem("s_pv")
        s_o = sem("s_o")
        s_o_out = [sem(f"s_o_out{n}") for n in range(2)]
        s_vq = sem("s_vq")
        s_od = [sem(f"s_od{n}") for n in range(2)]
        s_num = sem("s_num")
        s_rden = sem("s_rden")
        s_ready = sem("s_ready")
        s_att = sem("s_att")
        s_y = sem("s_y")
        s_res = sem("s_res")
        s_out = sem("s_out")
        s_wf = sem("s_wf")
        s_wfz = sem("s_wfz")
        s_qx = sem("s_qx")
        s_qa = sem("s_qa")
        s_quant = sem("s_quant")
        s_wft_ps = sem("s_wft_ps")
        s_wft = sem("s_wft")
        s_gu = sem("s_gu")
        s_silu = sem("s_silu")
        s_hid = sem("s_hid")
        s_ht_ps = sem("s_ht_ps")
        s_ht = sem("s_ht")
        s_down = sem("s_down")
        s_skip = sem("s_skip")
        s_b1_now = sem("s_b1_now")
        s_w12 = [sem(f"s_w12_{n}") for n in range(2)]
        s_w34 = sem("s_w34")
        s_dtw_ps = sem("s_dtw_ps")
        s_dtw = sem("s_dtw")
        s_zps = sem("s_zps")
        s_z = sem("s_z")
        s_e = sem("s_e")
        s_u = sem("s_u")
        s_ln = sem("s_ln")
        s_dt = sem("s_dt")
        s_bp = sem("s_bp")
        s_bp2 = sem("s_bp2")
        s_bp3 = sem("s_bp3")
        s_rest3 = sem("s_rest3")
        s_a = sem("s_a")
        s_abar = sem("s_abar")
        s_bb = sem("s_bb")
        s_cb = sem("s_cb")
        s_dbx = sem("s_dbx")
        s_scan = sem("s_scan")
        s_cs = sem("s_cs")
        s_hc = sem("s_hc")
        s_y3 = sem("s_y3")
        s_yt = sem("s_yt")
        s_selb = sem("s_selb")
        s_lgps = sem("s_lgps")
        s_lg = sem("s_lg")
        s_diff = sem("s_diff")
        s_ediff = sem("s_ediff")
        s_comb = sem("s_comb")
        s_combt_ps = sem("s_combt_ps")
        s_combt = sem("s_combt")
        s_b2 = sem("s_b2")
        s_l1 = sem("s_l1")
        s_gelu = sem("s_gelu")
        s_l2 = sem("s_l2")
        s_moe = sem("s_moe")
        s_acc = sem("s_acc")
        s_mstep = sem("s_mstep")

        block = ctx.enter_context(nc.Block())

        count = {"dve": 0, "pool": 0}

        def dve_step(ins):
            count["dve"] += 1
            ins.then_inc(s_v1, 1)
            nc.vector.wait_ge(s_v1, count["dve"])

        def pool_step(ins):
            count["pool"] += 1
            ins.then_inc(s_p1, 1)
            nc.gpsimd.wait_ge(s_p1, count["pool"])

        def bc(ap2, n):
            return ap2.unsqueeze(2).to_broadcast([ap2.shape[0], ap2.shape[1], n])

        def norm_dve_a(k, h):
            a, b = h * TILES // 2, (h + 1) * TILES // 2
            dve_step(nc.vector.tensor_reduce(stat[:, 0, a:b], x[:, a:b, :], AX.X, ALU.add))
            dve_step(nc.vector.tensor_scalar(stat[:, 1, a:b], stat[:, 0, a:b], 1.0 / D, None, ALU.mult))
            if k:
                nc.vector.wait_ge(s_turned, 4 * k)
            nc.vector.tensor_tensor(xc[:, a:b, :], x[:, a:b, :], bc(stat[:, 1, a:b], D),
                                    ALU.subtract).then_inc(s_centred, 1)

        def norm_dve_b(k, h):
            a, b = h * TILES // 2, (h + 1) * TILES // 2
            u = 2 * k + h
            nc.vector.wait_ge(s_squared, u + 1)
            nc.vector.tensor_reduce(stat[:, 2, a:b], sq[:, a:b, :], AX.X, ALU.add).then_inc(s_var, 1)
            nc.vector.wait_ge(s_rstd, u + 1)
            nc.vector.wait_ge(s_centred, u + 1)
            nc.vector.tensor_tensor(xc[:, a:b, :], xc[:, a:b, :], bc(stat[:, 3, a:b], D),
                                    ALU.mult).then_inc(s_normed, 1)

        def norm_act(k, h):
            a, b = h * TILES // 2, (h + 1) * TILES // 2
            u = 2 * k + h
            nc.scalar.wait_ge(s_centred, u + 1)
            if k:
                nc.scalar.wait_ge(s_var, u - 1)
            if k == 2:
                nc.scalar.wait_ge(s_turned, 8)
            nc.scalar.activation(sq[:, a:b, :], xc[:, a:b, :], ACT.Square).then_inc(s_squared, 1)

        def norm_pool(k, h):
            a, b = h * TILES // 2, (h + 1) * TILES // 2
            u = 2 * k + h
            nc.gpsimd.wait_ge(s_var, u + 1)
            if k:
                nc.gpsimd.wait_ge(s_normed, u - 1)
            pool_step(nc.gpsimd.tensor_scalar(stat[:, 3, a:b], stat[:, 2, a:b], 1.0 / D, EPS, ALU.mult, ALU.add))
            nc.gpsimd.tensor_tensor(stat[:, 3, a:b], stat[:, 3, a:b], expo[:, a:b], ALU.pow).then_inc(s_rstd, 1)

        def turn_pe(k, g):
            if k == 1:
                nc.tensor.wait_ge(s_quant, 1 + g // 2 + 1)
            else:
                nc.tensor.wait_ge(s_normed, 2 * k + g // 2 + 1)
            if k:
                nc.tensor.wait_ge(s_xt, 4 * (k - 1) + g + 1)
            for j in range(4):
                mm = nc.tensor.transpose(ps[:, g, j * P:(j + 1) * P], (sq if k == 1 else xc)[:, 4 * g + j, :], ident[:])
            mm.then_inc(s_turned, 1)

        def turn_act(k, g):
            nc.scalar.wait_ge(s_turned, 4 * k + g + 1)
            if k == 1:
                nc.scalar.wait_ge(s_v_ps, 4)
            if k == 2:
                nc.scalar.wait_ge(s_gu, TILES)
            if k == 3:
                nc.scalar.wait_ge(s_skip, BATCH)
            nc.scalar.activation(xt[:, g * BANK:(g + 1) * BANK], ps[:, g, :], ACT.Copy).then_inc(s_xt, 1)

        def quant_scale(n, src, ready=None):
            w = src.shape[1]
            blk = fblk[:, n % 2, :, 0:w // QB]
            cols = src.rearrange("p (b k) -> p b k", k=QB)
            if ready:
                nc.vector.wait_ge(*ready)
            if n >= 2:
                nc.vector.wait_ge(s_quant, n - 1)
            dve_step(nc.vector.tensor_reduce(blk[:, 0], cols, AX.X, ALU.max, apply_absolute_value=True))
            dve_step(nc.vector.tensor_scalar(blk[:, 1], blk[:, 0], 1.0 / 6.0, 1e-12, ALU.mult, ALU.max))
            dve_step(nc.vector.reciprocal(blk[:, 2], blk[:, 1]))
            if n >= 2:
                nc.vector.wait_ge(s_qa, 2 * (n - 1))
            nc.vector.tensor_tensor(fx[:, n % 2, 0:w].rearrange("p (b k) -> p b k", k=QB), cols,
                                    bc(blk[:, 2], QB), ALU.mult).then_inc(s_qx, 1)

        def quant_act(n, w):
            nc.scalar.wait_ge(s_qx, n + 1)
            if n >= 2:
                nc.scalar.wait_ge(s_quant, n - 1)
            nc.scalar.activation(fa[:, n % 2, 0:w], fx[:, n % 2, 0:w], ACT.Abs).then_inc(s_qa, 1)
            nc.scalar.activation(fs[:, n % 2, 0:w], fx[:, n % 2, 0:w], ACT.Sign).then_inc(s_qa, 1)

        def quant_grid(n, dst, free=None):
            w = dst.shape[1]
            a = fa[:, n % 2, 0:w]
            g = [fg[:, m, 0:w] for m in range(7)]
            nc.vector.wait_ge(s_qa, 2 * (n + 1))
            if n:
                nc.vector.wait_ge(s_quant, n)
            for m in range(7):
                ins = nc.vector.tensor_scalar(g[m], a, MIDS[m], JUMPS[m], ALU.is_gt, ALU.mult)
            dve_step(ins)
            for m in (0, 2, 4):
                ins = nc.vector.tensor_tensor(g[m], g[m], g[m + 1], ALU.add)
            dve_step(ins)
            dve_step(nc.vector.tensor_tensor(g[0], g[0], g[2], ALU.add))
            dve_step(nc.vector.tensor_tensor(g[4], g[4], g[6], ALU.add))
            dve_step(nc.vector.tensor_tensor(g[0], g[0], g[4], ALU.add))
            dve_step(nc.vector.tensor_tensor(g[0], g[0], fs[:, n % 2, 0:w], ALU.mult))
            if free:
                nc.vector.wait_ge(*free)
            nc.vector.tensor_tensor(dst.rearrange("p (b k) -> p b k", k=QB), g[0].rearrange("p (b k) -> p b k", k=QB),
                                    bc(fblk[:, n % 2, 1, 0:w // QB], QB), ALU.mult).then_inc(s_quant, 1)

        N_CONST = 6 + 4 + 2
        N_W34 = 3 + 16 + 6

        LOADS = 16 * (2 * (PARTS + 1) + 1)

        @block.sync
        def _(sp):
            xv = i["L0_attn_x"].rearrange("b (t p) c -> p (b t) c", p=P)
            for h in range(2):
                sp.dma_start(x[:, 8 * h:8 * h + 8, :], xv[:, 8 * h:8 * h + 8, :]).then_inc(s_x[h], 16)
            sp.dma_start(ident[:], i["ident"]).then_inc(s_const, 16)
            for n, w in enumerate(("Wq", "Wk", "Wv", "Wo")):
                sp.dma_start(w4[:, n, :], i["L0_attn_" + w]).then_inc(s_const, 16)
            sp.dma_start(perm[:], i["perm"].rearrange("n p c -> p n c")).then_inc(s_const, 16)
            for n, b in enumerate(("bq", "bk")):
                sp.dma_start(bqk[:, n:n + 1], i["L0_attn_" + b].rearrange("(p o) -> p o", o=1)).then_inc(s_const, 16)
            sp.dma_start(cos[:], i["cos"]).then_inc(s_const, 16)
            sp.dma_start(sin[:], i["sin"]).then_inc(s_const, 16)
            for b, t in (("bv", bv_all), ("bo", bo_all)):
                sp.dma_start(t[:], i["L0_attn_" + b].rearrange("(o c) -> o c", o=1).to_broadcast([P, D])).then_inc(s_const, 16)

            sp.wait_ge(s_wfz, 1)
            for n, w in enumerate(("gate", "up")):
                src = i["L0_ffn_w_" + w]
                sp.dma_start(wf[:, 3 * n * D:(3 * n + 2) * D].rearrange("p (t c) -> p t c", c=D),
                             src[0:2 * P].rearrange("(t p) c -> p t c", p=P)).then_inc(s_wf, 16)
                sp.dma_start(wf[0:FFN - 2 * P, (3 * n + 2) * D:(3 * n + 3) * D], src[2 * P:FFN]).then_inc(s_wf, 16)
            sp.dma_start(wf[:, 6 * D:WF], i["L0_ffn_w_down"]).then_inc(s_wf, 16)

            col = lambda name: i["L1_attn_" + name].rearrange("(p o) -> p o", o=1)
            sp.dma_start(wdt[:], i["L1_attn_dt_w"]).then_inc(s_w34, 16)
            sp.dma_start(cols[:, 0:1], col("dt_b")).then_inc(s_w34, 16)
            sp.dma_start(cols[:, 3:4], col("D_skip")).then_inc(s_w34, 16)
            for n in range(4):
                rows = slice(NSTATE * n, NSTATE * (n + 1))
                for m, w in enumerate("BC"):
                    sp.dma_start(wbc[rows, m], i[f"L1_attn_{w}_w"]).then_inc(s_w34, 16)
                    sp.dma_start(cols[rows, 1 + m:2 + m], col(w + "_b")).then_inc(s_w34, 16)
            sp.dma_start(log_a[:], i["L1_attn_log_A"]).then_inc(s_w34, 16)
            sp.dma_start(sel[:], i["sel"]).then_inc(s_w34, 16)
            sp.dma_start(wgate[:], i["L1_ffn_gate_w"]).then_inc(s_w34, 16)
            sp.dma_start(b1r[:], i["L1_ffn_b1"].rearrange("e (h p) -> (e h) p", p=P)).then_inc(s_w34, 16)
            sp.dma_start(b2[:], i["L1_ffn_b2"]).then_inc(s_w34, 16)
            sp.dma_start(tri[:], i["tri"]).then_inc(s_w34, 16)

            def store_parts(u):
                c, kind = divmod(u, 2)
                sp.wait_ge(s_part3, u + 1)
                dst = (q_dram, k_dram)[kind]
                for g in range(QUAD):
                    sp.dma_start(dst[4 * (c // 2) + g, c % 2].rearrange("n c t -> c n t"),
                                 parts[QC * g:QC * g + QC, u % 2]).then_inc(s_parts_out[u % 2], 16)

            def load(it, p):
                for f in range(2):
                    sp.dma_start(qs[p][0:PROD, f], q_dram[bass.ds(it, 1), f].rearrange(
                        "o n (d h) t -> (o n d) (h t)", h=QUAD).unsqueeze(1).to_broadcast([PARTS * HD, PARTS, QUAD * BANK])).then_inc(s_qk[p], 16)
                    for a in range(PARTS):
                        sp.dma_start(ks[p][HD * PARTS * a:HD * PARTS * (a + 1), f], k_dram[bass.ds(it, 1), f].rearrange(
                            "o n (d h) t -> d (o n) (h t)", h=QUAD)).then_inc(s_qk[p], 16)
                sp.dma_start(qs[p][PROD:PROD + 2], zrow[:].rearrange("p (f h t) -> p f h t", f=2, h=QUAD)).then_inc(s_qk[p], 16)

            def store_maxima(it, p, half):
                sp.wait_ge(s_nmax, 2 * it + half + 1)
                for z in range(4):
                    sp.dma_start(
                        qs[p][PROD:PROD + 2, half].rearrange("n h (q t) -> n (h q) t", t=P)[:, :, 32 * z:32 * z + 32],
                        nmax_t[32 * z:32 * z + 32, half, :]).then_inc(s_nrow[half], 16)

            def store_out(it, half):
                sp.wait_ge(s_o, 2 * it + half + 2)
                sp.dma_start(o_dram[bass.ds(it, 1), :, half * BANK:(half + 1) * BANK].rearrange("o r t -> (o r) t"),
                             o_sb[:, half, :]).then_inc(s_o_out[half], 16)

            for u in range(CHUNKS):
                store_parts(u)
            for n in range(2):
                sp.wait_ge(s_parts_out[n], 16 * QUAD * CHUNKS // 2)
            sp.wait_ge(s_set, SETS)
            for p in range(SETS):
                load(p, p)
            for u in range(CHUNKS, 2 * CHUNKS):
                store_parts(u)
            for n in range(2):
                sp.wait_ge(s_parts_out[n], 16 * QUAD * CHUNKS)
            store_maxima(0, 0, 0)
            store_maxima(0, 0, 1)

            def one_pass(it, p, more, again=None):
                if more:
                    store_maxima(it + 1, (p + 1) % SETS, 0)
                store_out(it, 0)
                if again is not None:
                    sp.wait_ge(s_pv, STEPS * (it + 1))
                    load(again, p)
                store_out(it, 1)
                if more:
                    store_maxima(it + 1, (p + 1) % SETS, 1)

            with sp.Fori(0, PASSES // SETS) as r:
                for p in range(SETS):
                    one_pass(SETS * r + p, p, True, (SETS * r + p + SETS) % PASSES)
            one_pass(PASSES - 2, 0, True)

            def sp_pass_7():
                one_pass(PASSES - 1, 1, False)

            def load_out(b):
                sp.wait_ge(s_o_out[0], 16 * (4 * b + 4 + 1))
                sp.wait_ge(s_o_out[1], 16 * (4 * b + 4 + 1))
                rows = o_dram[4 * b:4 * b + 4].rearrange("q (h r) t -> (q h) r t", r=32)
                sp.dma_start(den[:, b], rows[:, HD]).then_inc(s_od[b], 16)
                sp.dma_start(num[:, b * SEQ:(b + 1) * SEQ], rows[:, 0:HD]).then_inc(s_num, 16)
                sp.wait_ge(s_rden, b + 1)
                sp.dma_start(r_dram[b].rearrange("h (c t) -> (h c) t", c=P // HEADS), den[:, b]).then_inc(s_od[b], 16)
                sp.wait_ge(s_od[b], 32)
                sp.dma_start(rden[:, b], r_dram[b].unsqueeze(1).to_broadcast([HEADS, HD, SEQ])).then_inc(s_num, 16)
                sp.wait_ge(s_num, 32 * (b + 1))
                sp.sem_inc(s_ready, 1)

            load_out(0)
            sp.wait_ge(s_qk[SETS - 1], LOADS * (PASSES // SETS + 1))
            sp_pass_7()
            load_out(1)

            def load_expert(e, p):
                sp.dma_start(w1[:, p], i["L1_ffn_w1"][bass.ds(e, 1)].rearrange("o c h -> c (o h)")).then_inc(s_w12[p], 16)
                sp.dma_start(w2[:, p], i["L1_ffn_w2"][bass.ds(e, 1)].rearrange("o (t p) c -> p (o t) c", p=P)).then_inc(s_w12[p], 16)

            sp.wait_ge(s_skip, BATCH)
            sp.wait_ge(s_yt, 4)
            load_expert(0, 0)
            load_expert(1, 1)
            with sp.Fori(1, EXPERTS // 2) as r:
                for p in range(2):
                    sp.wait_ge(s_l2, CHUNKS * (2 * r + p - 1))
                    load_expert(2 * r + p, p)
            sp.wait_ge(s_moe, EXPERTS * CHUNKS)
            ov = out.rearrange("b (t p) c -> p (b t) c", p=P)
            sp.dma_start(ov, x[:]).then_inc(s_out, 16)
            sp.wait_ge(s_out, 16)

        @block.gpsimd
        def _(pool):
            pool_step(nc.gpsimd.memset(expo[:], -0.5))
            for h in range(2):
                norm_pool(0, h)
            pool.wait_ge(s_rstd, 2)
            pool_step(nc.gpsimd.memset(zrow[:], 0.0))
            for n in range(SETS):
                pool_step(nc.gpsimd.memset(qs[n][64:ROWS], 0.0))
                pool_step(nc.gpsimd.memset(ks[n][64:ROWS], 1.0))
            for n in range(SETS):
                nc.gpsimd.memset(vq[n][:], 1.0).then_inc(s_set, 1)
                pool.wait_ge(s_set, n + 1)
            for u in range(2 * CHUNKS):
                b = u % 2
                pool.wait_ge(s_part1, u + 1)
                nc.gpsimd.tensor_tensor(rest[:, b], rot[:, b, 2], parts[:, b, 0], ALU.subtract).then_inc(s_rest, 1)
                pool.wait_ge(s_rest, u + 1)
                pool.wait_ge(s_part2, u + 1)
                nc.gpsimd.tensor_tensor(parts[:, b, 2], rest[:, b], parts[:, b, 1], ALU.subtract).then_inc(s_part3, 1)

            def values(it, p):
                nc.gpsimd.tensor_copy(vq[p][:, :, :, 0:HD], v[:, bass.ds(it, 1)].rearrange(
                    "p o k (h d) -> p (o k) h d", d=HD)).then_inc(s_vq, 1)

            pool.wait_ge(s_v, 4)
            for p in range(SETS):
                values(p, p)
            with pool.Fori(1, PASSES // SETS) as r:
                for p in range(SETS):
                    pool.wait_ge(s_pv, STEPS * (SETS * (r - 1) + p + 1))
                    values(SETS * r + p, p)
            for p in range(PASSES % SETS):
                pool.wait_ge(s_pv, STEPS * (SETS * (PASSES // SETS - 1) + p + 1))
                values(PASSES - PASSES % SETS + p, p)

            norm_pool(1, 0)
            norm_pool(1, 1)

            norm_pool(2, 0)
            norm_pool(2, 1)

            def outflow(b, n, slot):
                m = NSTATE * b + n
                pool.wait_ge(s_scan, m + 1)
                pool.wait_ge(s_cs, m + 1)
                if not (isinstance(m, int) and m < 2):
                    pool.wait_ge(s_y3, m - 1)
                nc.gpsimd.tensor_tensor(hc[:, slot], hst[:, slot], cbr[:, slot], ALU.mult).then_inc(s_hc, 1)

            for b in range(BATCH):
                if b == 0:
                    outflow(0, 0, 0)
                    outflow(0, 1, 1)
                with pool.Fori(1 - b, NSTATE // 2) as k:
                    outflow(b, 2 * k, 0)
                    outflow(b, 2 * k + 1, 1)

            norm_pool(3, 0)
            norm_pool(3, 1)

        @block.scalar
        def _(act):
            for h in range(2):
                norm_act(0, h)
            act.wait_ge(s_wt_ps, 1)
            nc.scalar.activation(wt[:, 0:4, :], ps[:, 4, :], ACT.Copy).then_inc(s_wt, 1)
            nc.scalar.activation(wt[:, 4:6, :], ps[:, 5, 0:2 * D], ACT.Copy).then_inc(s_wt, 1)
            nc.scalar.activation(bperm[:], ps[:, 5, 2 * D:2 * D + 4].rearrange("p (n k) -> p n k", k=2), ACT.Copy).then_inc(s_wt, 1)
            for g in range(4):
                turn_act(0, g)
            for u in range(2 * CHUNKS):
                b = u % 2
                act.wait_ge(s_rope, u + 1)
                if u >= 2:
                    act.wait_ge(s_parts_out[b], 16 * QUAD * (u // 2))
                nc.scalar.activation(parts[:, b, 0], rot[:, b, 2], ACT.Copy).then_inc(s_part1, 1)
                act.wait_ge(s_rest, u + 1)
                nc.scalar.activation(parts[:, b, 1], rest[:, b], ACT.Copy).then_inc(s_part2, 1)

            def one_pass(it, first):
                for s in range(STEPS):
                    for j in range(4):
                        n = 4 * s + j
                        if j == 0 and s >= 2:
                            act.wait_ge(s_pv, STEPS * it + s - 1)
                        act.wait_ge(s_st, 4 * STEPS * it + n + 1)
                        nc.scalar.activation(prob[:, n % 8], ps[:, 4 + (first + n) % 3], ACT.Exp,
                                             scale=ATT_SCALE).then_inc(s_exp, 1)
                    if s == KT:
                        evacuate(it, 0)
                evacuate(it, 1)

            def evacuate(it, half):
                act.wait_ge(s_pv, STEPS * it + KT * (half + 1))
                act.wait_ge(s_o_out[half], 16 * (it + 1))
                nc.scalar.activation(o_sb[:, half], ps[:, 7], ACT.Copy).then_inc(s_o, 1)

            for half in range(2):
                act.sem_inc(s_o_out[half], 16)
            with act.Fori(0, PASSES // SETS) as r:
                for p in range(SETS):
                    one_pass(SETS * r + p, 4 * STEPS * p)
            one_pass(PASSES - 2, 0)
            one_pass(PASSES - 1, 4 * STEPS)

            norm_act(1, 0)
            norm_act(1, 1)
            quant_act(0, WF)
            quant_act(1, TOKENS // 2)
            act.wait_ge(s_wft_ps, 1)
            nc.scalar.activation(wgu_t[:], ps[:, 4:6, 0:FFN], ACT.Copy).then_inc(s_wft, 1)
            nc.scalar.activation(wd_t[:, 0:2], ps[:, 6, 0:2 * D].rearrange("p (t c) -> p t c", c=D), ACT.Copy).then_inc(s_wft, 1)
            nc.scalar.activation(wd_t[0:FFN - 2 * P, 2], ps[0:FFN - 2 * P, 6, 2 * D:3 * D], ACT.Copy).then_inc(s_wft, 1)
            turn_act(1, 0)
            turn_act(1, 1)
            quant_act(2, TOKENS // 2)
            turn_act(1, 2)
            turn_act(1, 3)

            def turned_hidden(g):
                for j in range(3):
                    rows = min(P, FFN - j * P)
                    act.wait_ge(s_ht_ps, 3 * g + j + 1)
                    if g:
                        act.wait_ge(s_down, g)
                    nc.scalar.activation(hid_t[0:rows, j], ps[0:rows, 4 + j], ACT.Copy).then_inc(s_ht, 1)

            for g in range(4):
                for t in range(4 * g, 4 * g + 4):
                    act.wait_ge(s_gu, t + 1)
                    if t >= 2:
                        act.wait_ge(s_hid, t - 1)
                    nc.scalar.activation(silu[:, t % 2], ps[:, 2 * (t % 2), 0:FFN], ACT.Silu).then_inc(s_silu, 1)
                quant_act(3 + g, QMAX)
                if g:
                    turned_hidden(g - 1)
            turned_hidden(3)

            act.wait_ge(s_dtw_ps, 1)
            nc.scalar.activation(ssm_t[:], ps[:, 4, 0:3 * D].rearrange("p (t c) -> p t c", c=D), ACT.Copy).then_inc(s_dtw, 1)
            nc.scalar.activation(b1t[:, 0:EXPERTS * HT], ps[:, 4, 3 * D:3 * D + EXPERTS * HT], ACT.Copy).then_inc(s_dtw, 1)
            nc.scalar.activation(sel_b[:], sel[:], ACT.Copy).then_inc(s_selb, 1)
            norm_act(2, 0)
            norm_act(2, 1)
            nc.scalar.activation(a_neg[:], log_a[:], ACT.Exp).then_inc(s_a, 1)
            for g in range(4):
                turn_act(2, g)
            for c in range(CHUNKS):
                w = slice(c * BANK, (c + 1) * BANK)
                for n, dst in enumerate((zt[:, w], bc32[:, 0, w], bc32[:, 1, w])):
                    act.wait_ge(s_zps, 3 * c + n + 1)
                    nc.scalar.activation(dst, ps[:, 5 + n], ACT.Identity, bias=cols[:, n:n + 1]).then_inc(s_z, 1)
            for b in range(BATCH):
                w = slice(b * SEQ, (b + 1) * SEQ)
                act.wait_ge(s_z, 6 * (b + 1))
                nc.scalar.activation(dt[:, w], zt[:, w], ACT.Abs).then_inc(s_e, 1)
                act.wait_ge(s_e, 2 * b + 1)
                nc.scalar.activation(dt[:, w], dt[:, w], ACT.Exp, scale=-1.0).then_inc(s_e, 1)
                for n in range(2):
                    nc.scalar.activation(bcp[:, n, w], bc32[:, n, w], ACT.Copy).then_inc(s_bp, 1)
                act.wait_ge(s_u, b + 1)
                nc.scalar.activation(cbr[:, b], dtx[:, w], ACT.Ln).then_inc(s_ln, 1)
                for n in range(2):
                    act.wait_ge(s_rest3, 2 * b + n + 1)
                    nc.scalar.activation(bcp[64:P, n, w], bc32[64:P, n, w], ACT.Copy).then_inc(s_bp2, 1)

            def factors(b, n, slot):
                m = NSTATE * b + n
                if not (isinstance(m, int) and m < 2):
                    act.wait_ge(s_scan, m - 1)
                act.wait_ge(s_a, 2)
                nc.scalar.activation(abar[:, slot], dt[:, b * SEQ:(b + 1) * SEQ], ACT.Exp,
                                     scale=a_neg[:, bass.ds(n, 1)]).then_inc(s_abar, 1)
                act.wait_ge(s_cb, m + 1)
                if not (isinstance(m, int) and m < 2):
                    act.wait_ge(s_hc, m - 1)
                nc.scalar.activation(cbr[:, slot], ps[:, 4:6], ACT.Copy).then_inc(s_cs, 1)

            act.wait_ge(s_a, 2)
            act.wait_ge(s_dt, 2 * BATCH)
            for b in range(BATCH):
                if b == 0:
                    factors(0, 0, 0)
                    factors(0, 1, 1)
                with act.Fori(1 - b, NSTATE // 2) as k:
                    factors(b, 2 * k, 0)
                    factors(b, 2 * k + 1, 1)

            norm_act(3, 0)
            norm_act(3, 1)
            for g in range(4):
                turn_act(3, g)
            act.wait_ge(s_diff, 1)
            nc.scalar.activation(top[:, 3], top[:, 2], ACT.Exp).then_inc(s_ediff, 1)
            act.wait_ge(s_combt_ps, 1)
            nc.scalar.activation(comb_t[:].rearrange("e (g t) -> e g t", t=BANK), ps[0:EXPERTS, 0:4], ACT.Copy).then_inc(s_combt, 1)

            with act.Fori(0, EXPERTS // 2) as k:
                for u in range(2 * CHUNKS):
                    m = 2 * CHUNKS * k + u
                    if u >= 2:
                        act.wait_ge(s_l2, m - 1)
                    if u % CHUNKS == 0:
                        act.wait_ge(s_b1_now, 2 * k + u // CHUNKS + 1)
                    for h in range(HT):
                        act.wait_ge(s_l1, HT * m + h + 1)
                        nc.scalar.activation(act_t[:, u % 2, h], ps[:, h], ACT.Gelu,
                                             bias=b1_now[:, u // CHUNKS, h:h + 1]).then_inc(s_gelu, 1)
                act.wait_ge(s_l2, 2 * CHUNKS * (k + 1))

        @block.vector
        def _(dve):
            nc.vector.memset(ps[:, 7], 0.0).then_inc(s_o, 1)
            nc.vector.memset(wf[:], 0.0).then_inc(s_wfz, 1)
            dve_step(nc.vector.memset(b1t[:, EXPERTS * HT:], 0.0))
            for h in range(2):
                dve.wait_ge(s_x[h], 16)
                norm_dve_a(0, h)
            for h in range(2):
                norm_dve_b(0, h)
            dve.wait_ge(s_const, 16 * N_CONST)
            dve.wait_ge(s_wt, 3)
            for u in range(2 * CHUNKS):
                c, kind = divmod(u, 2)
                b = u % 2
                t0 = (c % 2) * BANK
                dve.wait_ge(s_proj, u + 1)
                if u >= 2:
                    dve.wait_ge(s_rest, u - 1)
                nc.vector.scalar_tensor_tensor(rot[:, b, 0], ps[:, 4 + 2 * b], bperm[:, 0, kind:kind + 1],
                                               cos[:, t0:t0 + BANK], ALU.add, ALU.mult)
                ins = nc.vector.scalar_tensor_tensor(rot[:, b, 1], ps[:, 5 + 2 * b], bperm[:, 1, kind:kind + 1],
                                                     sin[:, t0:t0 + BANK], ALU.add, ALU.mult)
                ins.then_inc(s_rope_read, 1)
                dve.wait_ge(s_rope_read, u + 1)
                nc.vector.tensor_tensor(rot[:, b, 2], rot[:, b, 0], rot[:, b, 1], ALU.add).then_inc(s_rope, 1)
            for g in range(4):
                b, k0 = divmod(4 * g, KT)
                dve.wait_ge(s_v_ps, g + 1)
                for j in range(4):
                    ins = nc.vector.tensor_tensor(v[:, 4 * b:4 * b + 4, k0 + j, :],
                                                  ps[:, g, j * P:(j + 1) * P].rearrange("p (q c) -> p q c", c=QC),
                                                  bv_all[:].rearrange("p (q c) -> p q c", c=QC), ALU.add)
                ins.then_inc(s_v, 1)

            def maxima(it):
                for half in range(2):
                    for n in range(16):
                        t = 16 * half + n
                        dve.wait_ge(s_score, 32 * it + t + 1)
                        nc.vector.tensor_reduce(nmax[:, half, n:n + 1], ps[:, 2 * (t % 2):2 * (t % 2) + 2, :],
                                                AX.XY, ALU.max, negate=True).then_inc(s_max, 1)
                    w = 2 * (2 * it + half)
                    dve.wait_ge(s_max, 32 * it + 16 * half + 16)
                    nc.vector.tensor_copy(nmax_p[:, 0:16], nmax[:, half]).then_inc(s_mstep, 1)
                    dve.wait_ge(s_mstep, w + 1)
                    nc.vector.tensor_tensor(nmax_p[:, 16:32], nmax[:, half], nmax_p[:, 0:16], ALU.subtract).then_inc(s_mstep, 1)
                    dve.wait_ge(s_mstep, w + 2)
                    dve.wait_ge(s_nrow[half], 64 * it)
                    nc.vector.transpose(nmax_t[:, half, :], nmax_p[:]).then_inc(s_nmax, 1)

            maxima(0)
            with dve.Fori(1, PASSES) as it:
                maxima(it)

            for b in range(BATCH):
                w = slice(b * SEQ, (b + 1) * SEQ)
                dve.wait_ge(s_od[b], 16)
                nc.vector.reciprocal(den[:, b], den[:, b]).then_inc(s_rden, 1)
                dve.wait_ge(s_ready, b + 1)
                nc.vector.tensor_tensor(num[:, w], num[:, w], rden[:, b], ALU.mult).then_inc(s_att, 1)
            for g in range(4):
                dve_step(nc.vector.tensor_tensor(x[:, 4 * g:4 * g + 4, :], x[:, 4 * g:4 * g + 4, :],
                                                 bo_all[:].unsqueeze(1).to_broadcast([P, 4, D]), ALU.add))
                dve.wait_ge(s_y, g + 1)
                nc.vector.tensor_tensor(x[:, 4 * g:4 * g + 4, :], x[:, 4 * g:4 * g + 4, :],
                                        ps[:, g, :].rearrange("p (t c) -> p t c", c=D), ALU.add).then_inc(s_res, 1)

            dve.wait_ge(s_res, 4)
            norm_dve_a(1, 0)
            norm_dve_a(1, 1)
            quant_scale(0, wf[:], (s_wf, 16 * 5))
            norm_dve_b(1, 0)
            norm_dve_b(1, 1)
            halves = [xc[:, 8 * h:8 * h + 8, :].rearrange("p t c -> p (t c)") for h in range(2)]
            sq_halves = [sq[:, 8 * h:8 * h + 8, :].rearrange("p t c -> p (t c)") for h in range(2)]
            quant_scale(1, halves[0], (s_normed, 3))
            quant_grid(0, wfq[:])
            quant_scale(2, halves[1], (s_normed, 4))
            quant_grid(1, sq_halves[0])
            quant_grid(2, sq_halves[1])

            def hidden(g):
                for t in range(4 * g, 4 * g + 4):
                    dve.wait_ge(s_silu, t + 1)
                    if g >= 2:
                        dve.wait_ge(s_qx, 3 + g - 1)
                    nc.vector.tensor_tensor(hid[:, g % 2, (t % 4) * FFN:(t % 4 + 1) * FFN], silu[:, t % 2],
                                            ps[:, 2 * (t % 2) + 1, 0:FFN], ALU.mult).then_inc(s_hid, 1)
                quant_scale(3 + g, hid[:, g % 2], (s_hid, 4 * g + 4))

            def down(g):
                dve.wait_ge(s_down, g + 1)
                nc.vector.tensor_tensor(x[:, 4 * g:4 * g + 4, :], x[:, 4 * g:4 * g + 4, :],
                                        ps[:, 7].rearrange("p (t c) -> p t c", c=D), ALU.add).then_inc(s_res, 1)

            hidden(0)
            for g in range(4):
                if g < 3:
                    hidden(g + 1)
                quant_grid(3 + g, hid_q[:, g % 2], (s_ht_ps, 3 * (g - 1)) if g >= 2 else None)
                if g:
                    down(g - 1)
            down(3)

            dve.wait_ge(s_res, 8)
            norm_dve_a(2, 0)
            norm_dve_a(2, 1)
            norm_dve_b(2, 0)
            norm_dve_b(2, 1)
            dve.wait_ge(s_a, 1)
            nc.vector.tensor_scalar(a_neg[:], a_neg[:], -1.0, None, ALU.mult).then_inc(s_a, 1)
            for b in range(BATCH):
                w = slice(b * SEQ, (b + 1) * SEQ)
                dve.wait_ge(s_e, 2 * b + 2)
                nc.vector.tensor_scalar(dtx[:, w], dt[:, w], 1.0, None, ALU.add).then_inc(s_u, 1)
                for n in range(2):
                    dve.wait_ge(s_bp, 2 * b + n + 1)
                    nc.vector.tensor_tensor(bc32[64:P, n, w], bc32[64:P, n, w], bcp[64:P, n, w], ALU.subtract).then_inc(s_rest3, 1)
                dve.wait_ge(s_u, b + 1)
                dve_step(nc.vector.scalar_tensor_tensor(dt[:, w], dtx[:, w], 1.0, dt[:, w], ALU.subtract, ALU.subtract))
                dve.wait_ge(s_ln, b + 1)
                dve_step(nc.vector.tensor_tensor(dt[:, w], cbr[:, b], dt[:, w], ALU.subtract))
                nc.vector.scalar_tensor_tensor(dt[:, w], zt[:, w], 0.0, dt[:, w], ALU.max, ALU.add).then_inc(s_dt, 1)
                for n in range(2):
                    dve.wait_ge(s_bp2, 2 * b + n + 1)
                    nc.vector.tensor_tensor(bcp[96:P, n, w], bc32[96:P, n, w], bcp[96:P, n, w], ALU.subtract).then_inc(s_bp3, 1)
                dve.wait_ge(s_dt, 2 * b + 1)
                nc.vector.tensor_tensor(dtx[:, w], dt[:, w], xt[:, w], ALU.mult).then_inc(s_dt, 1)

            def inflow(b, n, slot):
                m = NSTATE * b + n
                dve.wait_ge(s_bb, m + 1)
                if not (isinstance(m, int) and m < 2):
                    dve.wait_ge(s_scan, m - 1)
                nc.vector.tensor_tensor(dbx[:, slot].rearrange("p (k t) -> p k t", k=2),
                                        dtx[:, b * SEQ:(b + 1) * SEQ].rearrange("p (k t) -> p k t", k=2),
                                        ps[:, 2 * slot:2 * slot + 2], ALU.mult).then_inc(s_dbx, 1)

            def scan(b, n, slot):
                m = NSTATE * b + n
                dve.wait_ge(s_dbx, m + 1)
                dve.wait_ge(s_abar, m + 1)
                if not (isinstance(m, int) and m < 2):
                    dve.wait_ge(s_hc, m - 1)
                nc.vector.tensor_tensor_scan(hst[:, slot], abar[:, slot], dbx[:, slot], 0.0, ALU.mult, ALU.add).then_inc(s_scan, 1)

            def scan_pair(b, k):
                inflow(b, 2 * k + 1, 1)
                scan(b, 2 * k, 0)
                inflow(b, 2 * k + 2, 0)
                scan(b, 2 * k + 1, 1)

            dve.wait_ge(s_dt, 2 * BATCH)
            for b in range(BATCH):
                inflow(b, 0, 0)
                if b == 0:
                    scan_pair(0, 0)
                with dve.Fori(1 - b, NSTATE // 2 - 1) as k:
                    scan_pair(b, k)
                inflow(b, NSTATE - 1, 1)
                scan(b, NSTATE - 2, 0)
                scan(b, NSTATE - 1, 1)
                w = slice(b * SEQ, (b + 1) * SEQ)
                dve.wait_ge(s_y3, NSTATE * (b + 1))
                nc.vector.scalar_tensor_tensor(zt[:, w].rearrange("p (k t) -> p k t", k=2),
                                               xt[:, w].rearrange("p (k t) -> p k t", k=2), cols[:, 3:4],
                                               ps[:, 6:8], ALU.mult, ALU.add).then_inc(s_skip, 1)
            for g in range(4):
                dve.wait_ge(s_yt, g + 1)
                nc.vector.tensor_tensor(x[:, 4 * g:4 * g + 4, :], x[:, 4 * g:4 * g + 4, :],
                                        ps[:, g].rearrange("p (t c) -> p t c", c=D), ALU.add).then_inc(s_res, 1)

            dve.wait_ge(s_res, 12)
            norm_dve_a(3, 0)
            norm_dve_a(3, 1)
            norm_dve_b(3, 0)
            norm_dve_b(3, 1)
            dve.wait_ge(s_lgps, 1)
            lg3 = lg[:].rearrange("p t e -> p (t e)")
            dve_step(nc.vector.tensor_copy(lg3, ps[:, 4, 0:TILES * EXPERTS]))
            shape = [P, TILES, EXPERTS, EXPERTS]
            l_e = lg[:].unsqueeze(3).to_broadcast(shape)
            l_j = lg[:].unsqueeze(2).to_broadcast(shape)
            nc.vector.tensor_tensor(gt[:], l_j, l_e, ALU.is_gt)
            dve_step(nc.vector.tensor_tensor(eq[:], l_j, l_e, ALU.is_equal))
            dve_step(nc.vector.tensor_tensor(eq[:], eq[:], tri[:].unsqueeze(1).to_broadcast(shape), ALU.mult))
            dve_step(nc.vector.tensor_tensor(gt[:], gt[:], eq[:], ALU.add))
            dve_step(nc.vector.tensor_reduce(rank[:], gt[:], AX.X, ALU.add))
            nc.vector.tensor_reduce(top[:, 0], lg[:], AX.X, ALU.max)
            nc.vector.tensor_scalar(is01[:, 0], rank[:], 0.0, None, ALU.is_equal)
            dve_step(nc.vector.tensor_scalar(is01[:, 1], rank[:], 1.0, None, ALU.is_equal))
            dve_step(nc.vector.tensor_tensor(rank[:], lg[:], is01[:, 1], ALU.mult))
            dve_step(nc.vector.tensor_reduce(top[:, 1], rank[:], AX.X, ALU.add))
            nc.vector.tensor_tensor(top[:, 2], top[:, 1], top[:, 0], ALU.subtract).then_inc(s_diff, 1)
            dve.wait_ge(s_ediff, 1)
            dve_step(nc.vector.tensor_scalar(top[:, 4], top[:, 3], 1.0, None, ALU.add))
            dve_step(nc.vector.reciprocal(top[:, 4], top[:, 4]))
            dve_step(nc.vector.tensor_tensor(top[:, 5], top[:, 3], top[:, 4], ALU.mult))
            for n in range(2):
                ins = nc.vector.tensor_tensor(is01[:, n], is01[:, n], bc(top[:, 4 + n], EXPERTS), ALU.mult)
            dve_step(ins)
            nc.vector.tensor_tensor(comb[:], is01[:, 0], is01[:, 1], ALU.add).then_inc(s_comb, 1)
            for g in range(4):
                dve.wait_ge(s_b2, g + 1)
                nc.vector.tensor_tensor(x[:, 4 * g:4 * g + 4, :], x[:, 4 * g:4 * g + 4, :],
                                        ps[:, 4 + g].rearrange("p (t c) -> p t c", c=D), ALU.add).then_inc(s_acc, 1)
            dve.wait_ge(s_acc, 4)
            dve.wait_ge(s_comb, 1)

            def next_bias(e, p):
                nc.vector.tensor_scalar(b1_now[:, p], b1t[:, bass.ds(HT * e, HT)], 1.0, None, ALU.mult).then_inc(s_b1_now, 1)

            dve.wait_ge(s_dtw, 2)
            next_bias(0, 0)
            next_bias(1, 1)
            with dve.Fori(0, EXPERTS // 2) as k:
                for u in range(2 * CHUNKS):
                    m = 2 * CHUNKS * k + u
                    dve.wait_ge(s_l2, m + 1)
                    if u:
                        dve.wait_ge(s_moe, m)
                    if u % CHUNKS == CHUNKS - 1:
                        dve.wait_ge(s_gelu, HT * m + HT)
                        next_bias(2 * k + 2 + u // CHUNKS, u // CHUNKS)
                    for j in range(4):
                        t = 4 * (u % CHUNKS) + j
                        ins = nc.vector.scalar_tensor_tensor(x[:, t, :], ps[:, 4 + u % 2, j * D:(j + 1) * D],
                                                             comb[:, t, bass.ds(2 * k + u // CHUNKS, 1)], x[:, t, :],
                                                             ALU.mult, ALU.add)
                    ins.then_inc(s_moe, 1)
                dve.wait_ge(s_moe, 2 * CHUNKS * (k + 1))



        @block.tensor
        def _(pe):
            pe.wait_ge(s_const, 16 * N_CONST)
            for n, (w, order) in enumerate(((0, 0), (0, 1), (1, 0), (1, 1), (2, 2), (3, 2))):
                nc.tensor.matmul(ps[:, 4 + n // 4, (n % 4) * D:(n % 4 + 1) * D], w4[:, w, :],
                                 ident[:] if order == 2 else perm[:, order],
                                 start=True, stop=True, is_transpose=True)
            for n in range(2):
                mm = nc.tensor.matmul(ps[:, 5, 2 * D + 2 * n:2 * D + 2 * n + 2], perm[:, n], bqk[:], start=True, stop=True)
            mm.then_inc(s_wt_ps, 1)
            turn_pe(0, 0)
            turn_pe(0, 1)
            pe.wait_ge(s_wt, 3)
            for u in range(2 * CHUNKS):
                if u == CHUNKS:
                    turn_pe(0, 2)
                    turn_pe(0, 3)
                c, kind = divmod(u, 2)
                pe.wait_ge(s_xt, c + 1)
                if u >= 2:
                    pe.wait_ge(s_rope_read, u - 1)
                for n in range(2):
                    mm = nc.tensor.matmul(ps[:, 4 + 2 * (u % 2) + n], wt[:, 2 * kind + n, :],
                                          xt[:, c * BANK:(c + 1) * BANK], start=True, stop=True)
                mm.then_inc(s_proj, 1)
            for g in range(4):
                pe.wait_ge(s_xt, 4)
                for j in range(4):
                    t = 4 * g + j
                    mm = nc.tensor.matmul(ps[:, g, j * P:(j + 1) * P], xt[:, t * P:(t + 1) * P], wt[:, 4, :],
                                          start=True, stop=True)
                mm.then_inc(s_v_ps, 1)

            def score_half(it, p, t, kk):
                half, h, q = t // 16, t % 16 // 4, t % 4
                if kk == 0 and not (isinstance(it, int) and it == 0 and t < 2):
                    pe.wait_ge(s_max, 32 * it + t - 1)
                mm = nc.tensor.matmul(ps[:, 2 * (t % 2) + kk], qs[p][:, half, h, q * P:(q + 1) * P],
                                      ks[p][:, kk, h, :], start=True, stop=True)
                if kk == 1:
                    mm.then_inc(s_score, 1)

            def one_pass(it, p, first, more, loads=None):
                for s in range(STEPS):
                    half, kt = divmod(s, KT)
                    if kt == 0:
                        pe.wait_ge(s_nrow[half], 64 * (it + 1))
                    if more and s == 0:
                        pe.wait_ge(s_qk[(p + 1) % SETS], LOADS * loads)
                    todo = [(MAX_TILES * s + n // 2, n % 2) for n in range(2 * MAX_TILES)] if more else []
                    for j in range(QUAD):
                        n = 4 * s + j
                        if n >= 3:
                            pe.wait_ge(s_exp, 4 * STEPS * it + n - 2)
                        nc.tensor.matmul(ps[:, 4 + (first + n) % 3], ks[p][:, kt // 4, j, kt % 4 * P:(kt % 4 + 1) * P],
                                         qs[p][:, half, j, :], start=True, stop=True).then_inc(s_st, 1)
                        for t, kk in todo[len(todo) * j // 4:len(todo) * (j + 1) // 4]:
                            score_half(it + 1, (p + 1) % SETS, t, kk)
                    if s >= 1:
                        products(it, p, s - 1)
                products(it, p, STEPS - 1)

            def products(it, p, s):
                half, kt = divmod(s, KT)
                if s == 0:
                    pe.wait_ge(s_vq, it + 1)
                if kt == 0:
                    pe.wait_ge(s_o, 2 * it + half + 1)
                pe.wait_ge(s_exp, 4 * STEPS * it + 4 * s + 4)
                for j in range(QUAD):
                    mm = nc.tensor.matmul(ps[32 * j:32 * j + VW, 7], vq[p][:, kt, j, :], prob[:, (4 * s + j) % 8],
                                          start=(kt == 0), stop=(kt == KT - 1))
                mm.then_inc(s_pv, 1)

            pe.wait_ge(s_qk[0], LOADS)
            pe.wait_ge(s_v, 4)
            for t in range(32):
                score_half(0, 0, t, 0)
                score_half(0, 0, t, 1)
            with pe.Fori(0, PASSES // SETS) as r:
                for p in range(SETS):
                    one_pass(SETS * r + p, p, 4 * STEPS * p, True, r + 1 + (p + 1) // SETS)
            one_pass(PASSES - 2, 0, 0, True, PASSES // SETS + 1)
            one_pass(PASSES - 1, 1, 4 * STEPS, False)

            for g in range(4):
                pe.wait_ge(s_att, g // 2 + 1)
                for j in range(4):
                    t = 4 * g + j
                    mm = nc.tensor.matmul(ps[:, g, j * P:(j + 1) * P], num[:, t * P:(t + 1) * P], wt[:, 5, :],
                                          start=True, stop=True)
                mm.then_inc(s_y, 1)

            pe.wait_ge(s_quant, 1)
            pe.wait_ge(s_exp, 4 * STEPS * PASSES)
            for n in range(2):
                for j in range(3):
                    rows = min(P, FFN - j * P)
                    nc.tensor.transpose(ps[:, 4 + n, j * P:j * P + rows], wfq[0:rows, (3 * n + j) * D:(3 * n + j + 1) * D],
                                        ident[0:rows, 0:rows])
            for j in range(3):
                rows = min(P, FFN - j * P)
                mm = nc.tensor.transpose(ps[0:rows, 6, j * D:(j + 1) * D], wfq[:, 6 * D + j * P:6 * D + j * P + rows], ident[:])
            mm.then_inc(s_wft_ps, 1)
            for g in range(4):
                turn_pe(1, g)
            pe.wait_ge(s_wft, 3)

            def gate_up(g):
                for t in range(4 * g, 4 * g + 4):
                    pe.wait_ge(s_xt, 4 + (4 if t < 2 else g + 1))
                    if t >= 2:
                        pe.wait_ge(s_hid, t - 1)
                    for n in range(2):
                        mm = nc.tensor.matmul(ps[:, 2 * (t % 2) + n, 0:FFN], xt[:, t * P:(t + 1) * P], wgu_t[:, n, :],
                                              start=True, stop=True)
                    mm.then_inc(s_gu, 1)

            gate_up(0)
            for g in range(4):
                if g < 3:
                    gate_up(g + 1)
                pe.wait_ge(s_quant, 4 + g)
                for j in range(3):
                    rows = min(P, FFN - j * P)
                    if g:
                        pe.wait_ge(s_ht, 3 * g - 3 + j + 1)
                    for t in range(4):
                        mm = nc.tensor.transpose(ps[0:rows, 4 + j, t * P:(t + 1) * P],
                                                 hid_q[:, g % 2, t * FFN + j * P:t * FFN + j * P + rows], ident[:])
                    mm.then_inc(s_ht_ps, 1)
                pe.wait_ge(s_ht, 3 * g + 3)
                if g:
                    pe.wait_ge(s_res, 4 + g)
                for t in range(4):
                    for j in range(3):
                        rows = min(P, FFN - j * P)
                        mm = nc.tensor.matmul(ps[:, 7, t * D:(t + 1) * D], hid_t[0:rows, j, t * P:(t + 1) * P],
                                              wd_t[0:rows, j, :], start=(j == 0), stop=(j == 2))
                mm.then_inc(s_down, 1)

            pe.wait_ge(s_w34, 16 * N_W34)
            pe.wait_ge(s_ht, 12)
            nc.tensor.transpose(ps[:, 4, 0:D], wdt[:], ident[:])
            for n in range(2):
                nc.tensor.transpose(ps[:, 4, (n + 1) * D:(n + 2) * D], wbc[:, n], ident[:])
            nc.tensor.transpose(ps[:, 4, 3 * D:3 * D + EXPERTS * HT], b1r[:],
                                ident[0:EXPERTS * HT, 0:EXPERTS * HT]).then_inc(s_dtw_ps, 1)
            for g in range(4):
                turn_pe(2, g)
            pe.wait_ge(s_dtw, 2)
            pe.wait_ge(s_res, 8)
            for c in range(CHUNKS):
                pe.wait_ge(s_xt, 8 + c + 1)
                for n in range(3):
                    if c:
                        pe.wait_ge(s_z, 3 * (c - 1) + n + 1)
                    nc.tensor.matmul(ps[:, 5 + n], ssm_t[:, n], xt[:, c * BANK:(c + 1) * BANK],
                                     start=True, stop=True).then_inc(s_zps, 1)

            def rows(b, n, slot):
                m = NSTATE * b + n
                first = isinstance(m, int) and m < 2
                pick = sel_b[:, bass.ds(n, 1)].to_broadcast([P, P])
                if not first:
                    pe.wait_ge(s_dbx, m - 1)
                for k in range(2):
                    mm = nc.tensor.matmul(ps[:, 2 * slot + k], pick, bcp[:, 0, b * SEQ + k * BANK:b * SEQ + (k + 1) * BANK],
                                          start=True, stop=True)
                mm.then_inc(s_bb, 1)
                if not (isinstance(m, int) and m < 1):
                    pe.wait_ge(s_cs, m)
                for k in range(2):
                    mm = nc.tensor.matmul(ps[:, 4 + k], pick, bcp[:, 1, b * SEQ + k * BANK:b * SEQ + (k + 1) * BANK],
                                          start=True, stop=True)
                mm.then_inc(s_cb, 1)

            def total(b, n, slot):
                m = NSTATE * b + n
                first = isinstance(n, int) and n == 0
                last = isinstance(n, int) and n == NSTATE - 1
                pe.wait_ge(s_hc, m + 1)
                if first:
                    pe.wait_ge(s_skip, b)
                for k in range(2):
                    mm = nc.tensor.matmul(ps[:, 6 + k], ident[:], hc[:, slot, k * BANK:(k + 1) * BANK], start=first, stop=last)
                mm.then_inc(s_y3, 1)

            pe.wait_ge(s_selb, 1)
            pe.wait_ge(s_bp3, 2 * BATCH)
            pe.wait_ge(s_z, 3 * CHUNKS)
            for b in range(BATCH):
                for n in range(4):
                    rows(b, n, n % 2)
                    if n == 1:
                        continue
                total(b, 0, 0)
                total(b, 1, 1)
                with pe.Fori(2, NSTATE // 2) as k:
                    rows(b, 2 * k, 0)
                    rows(b, 2 * k + 1, 1)
                    total(b, 2 * k - 2, 0)
                    total(b, 2 * k - 1, 1)
                total(b, NSTATE - 2, 0)
                total(b, NSTATE - 1, 1)
            pe.wait_ge(s_dbx, BATCH * NSTATE)
            for g in range(4):
                pe.wait_ge(s_skip, g // 2 + 1)
                for j in range(4):
                    t = 4 * g + j
                    mm = nc.tensor.transpose(ps[:, g, j * P:(j + 1) * P], zt[:, t * P:(t + 1) * P], ident[:])
                mm.then_inc(s_yt, 1)

            for g in range(4):
                turn_pe(3, g)
            pe.wait_ge(s_cs, BATCH * NSTATE)
            for t in range(TILES):
                pe.wait_ge(s_xt, 12 + t // 4 + 1)
                mm = nc.tensor.matmul(ps[:, 4, t * EXPERTS:(t + 1) * EXPERTS], xt[:, t * P:(t + 1) * P], wgate[:],
                                      start=True, stop=True)
            mm.then_inc(s_lgps, 1)
            pe.wait_ge(s_comb, 1)
            for t in range(TILES):
                mm = nc.tensor.transpose(ps[0:EXPERTS, t // 4, (t % 4) * P:(t % 4 + 1) * P], comb[:, t, :], ident[:])
            mm.then_inc(s_combt_ps, 1)
            pe.wait_ge(s_combt, 1)
            for t in range(TILES):
                mm = nc.tensor.matmul(ps[:, 4 + t // 4, (t % 4) * D:(t % 4 + 1) * D], comb_t[:, t * P:(t + 1) * P], b2[:],
                                      start=True, stop=True)
                if t % 4 == 3:
                    mm.then_inc(s_b2, 1)
            pe.wait_ge(s_acc, 4)

            def first_product(k, u):
                m = 2 * CHUNKS * k + u
                c, e = u % CHUNKS, u // CHUNKS
                if c == 0:
                    pe.wait_ge(s_w12[e], 32 * (k + 1))
                for h in range(HT):
                    if u:
                        pe.wait_ge(s_gelu, HT * m + h - 3)
                    nc.tensor.matmul(ps[:, h], w1[:, e, h * P:(h + 1) * P], xt[:, c * BANK:(c + 1) * BANK],
                                     start=True, stop=True).then_inc(s_l1, 1)

            def second_product(k, u):
                m = 2 * CHUNKS * k + u
                pe.wait_ge(s_gelu, HT * m + HT)
                if u:
                    pe.wait_ge(s_moe, m if u == 1 else m - 1)
                for j in range(4):
                    for h in range(HT):
                        mm = nc.tensor.matmul(ps[:, 4 + u % 2, j * D:(j + 1) * D], act_t[:, u % 2, h, j * P:(j + 1) * P],
                                              w2[:, u // CHUNKS, h], start=(h == 0), stop=(h == HT - 1))
                mm.then_inc(s_l2, 1)

            with pe.Fori(0, EXPERTS // 2) as k:
                first_product(k, 0)
                for u in range(1, 2 * CHUNKS):
                    first_product(k, u)
                    second_product(k, u - 1)
                second_product(k, 2 * CHUNKS - 1)
                pe.wait_ge(s_moe, 2 * CHUNKS * (k + 1) - 1)


def constants():
    f32 = np.float32
    inv = f32(1.0) / np.power(f32(10000.0), np.arange(0, HD, 2, dtype=f32) / f32(HD)).astype(f32)
    ang = (np.arange(SEQ, dtype=f32)[:, None] * inv[None, :]).astype(f32).astype(np.float64)
    ang = np.concatenate([ang, ang], axis=-1).T
    sign = np.where(np.arange(HD) % 2 == 0, -1.0, 1.0)[:, None]
    order = np.arange(P).reshape(HEADS // QUAD, QUAD, HD).transpose(0, 2, 1).ravel()
    perm = np.zeros((2, P, P), f32)
    perm[0, order, np.arange(P)] = 1
    perm[1, order ^ 1, np.arange(P)] = 1
    sel = np.zeros((P, NSTATE), f32)
    for part in (0, 64, 96):
        sel[part + np.arange(NSTATE), np.arange(NSTATE)] = 1
    tri = np.tril(np.ones((EXPERTS, EXPERTS), f32), -1)
    return {
        "ident": np.eye(P, dtype=f32),
        "perm": perm,
        "sel": sel,
        "tri": np.broadcast_to(tri, (P, EXPERTS, EXPERTS)).copy(),
        "cos": np.tile(np.cos(ang), (HEADS, 1)).astype(f32)[order],
        "sin": np.tile(np.sin(ang) * sign, (HEADS, 1)).astype(f32)[order],
    }


def kernel(**inputs):
    import concourse.bacc as bacc
    from concourse.bass_utils import run_bass_kernel_spmd

    nc = bacc.Bacc("TRN2", target_bir_lowering=False, num_devices=1)
    arrays, aps = {}, {}
    for name, a in {**inputs, **constants()}.items():
        a = np.ascontiguousarray(a)
        arrays["in_" + name] = a
        aps[name] = nc.dram_tensor("in_" + name, a.shape, mybir.dt.from_np(a.dtype), kind="ExternalInput").ap()
    out = nc.dram_tensor("out_x", (BATCH, SEQ, D), F32, kind="ExternalOutput").ap()
    build_kernel(nc, aps, out)
    r = run_bass_kernel_spmd(nc, [arrays], core_ids=[0])
    return r.results[0]["out_x"]
```

```python
from contextlib import ExitStack

import numpy as np

import concourse.bass as bass
from concourse import mybir

F32 = mybir.dt.float32
BF16 = mybir.dt.bfloat16
F32R = mybir.dt.float32r
U32 = mybir.dt.uint32
ALU = mybir.AluOpType
ACT = mybir.ActivationFunctionType
AX = mybir.AxisListType

P = 128
BATCH = 2
SEQ = 1024
TOKENS = BATCH * SEQ
D = 128
TILES = TOKENS // P
BANK = 512
CHUNKS = TOKENS // BANK
EPS = 1e-5

HEADS = 16
HD = D // HEADS
QUAD = 4
PASSES = BATCH * HEADS // QUAD
QC = QUAD * HD
KT = SEQ // P
PARTS = 3
PROD = PARTS * PARTS * HD
ROWS = 96
ATT_SCALE = 1.0 / float(np.sqrt(np.float32(HD)))
VW = 16
STEPS = 2 * KT
MAX_TILES = 2
SETS = 3

MIDS = [0.25, 0.75, 1.25, 1.75, 2.5, 3.5, 5.0]
JUMPS = [0.5, 0.5, 0.5, 0.5, 1.0, 1.0, 2.0]
FFN = 352
RING = 4
QB = 16
NSTATE = 32
EXPERTS = 8
HIDDEN = 512
HT = HIDDEN // P
UNITS = 2 * CHUNKS

WF = 6 * D + FFN
QMAX = 4 * FFN


def build_kernel(nc, i, out):
    ctx = ExitStack()

    def sb(name, shape, dt=F32, stack=ctx):
        return stack.enter_context(nc.sbuf_tensor(name, shape, dt))

    def sem(name):
        return ctx.enter_context(nc.semaphore(name))

    with ctx:
        ps = ctx.enter_context(nc.psum_tensor("ps", [P, 8, BANK], F32))

        x = sb("x", [P, TILES, D])
        xc = sb("xc", [P, TILES, D])
        sq = sb("sq", [P, TILES, D])
        xt = sb("xt", [P, TOKENS])
        ident = sb("ident", [P, P])
        stat = sb("stat", [P, 4, TILES])

        zero = sb("zero", [P, 2])
        expo = sb("expo", [P, TILES])

        wf = sb("wf", [P, WF])
        wfq = sb("wfq", [P, WF])
        wgu_t = sb("wgu_t", [P, 2, FFN])
        wd_t = sb("wd_t", [P, 3, D])

        wdt = sb("wdt", [P, D])
        wbc = sb("wbc", [P, 2, D])
        cols = sb("cols", [P, 4])
        log_a = sb("log_a", [P, NSTATE])
        sel = sb("sel", [P, NSTATE])
        sel_b = sb("sel_b", [P, NSTATE], BF16)
        wgate = sb("wgate", [P, EXPERTS])
        b1r = sb("b1r", [EXPERTS * HT, P])
        b2 = sb("b2", [EXPERTS, D])
        tri = sb("tri", [P, EXPERTS, EXPERTS])
        ssm_t = sb("ssm_t", [P, 3, D])
        b1t = sb("b1t", [P, (EXPERTS + 2) * HT])
        b1_now = sb("b1_now", [P, 2, HT])

        phase = ExitStack()

        def sb(name, shape, dt=F32):
            return phase.enter_context(nc.sbuf_tensor(name, shape, dt))

        w4 = sb("w4", [P, 4, D])
        perm = sb("perm", [P, 2, P])
        cos = sb("cos", [P, SEQ])
        sin = sb("sin", [P, SEQ])
        rot = sb("rot", [P, 2, 3, BANK])
        rest = sb("rest", [P, 2, BANK])
        parts = sb("parts", [P, CHUNKS, PARTS, BANK], BF16)
        stacks = [[sb(f"{w}{n}", [ROWS, 2, QUAD, BANK], BF16) for w in ("qs", "ks")] for n in reversed(range(SETS))][::-1]
        qs, ks = ([pair[n] for pair in stacks] for n in range(2))
        fill = sb("fill", [4 * (ROWS - PROD), 2, 2 * BANK], BF16)
        prob = sb("prob", [P, 8, BANK])
        vq = [sb(f"vq{n}", [P, KT, QUAD, VW]) for n in range(SETS)]
        v = sb("v", [P, PASSES, KT, QC])
        wt = sb("wt", [P, 6, D])
        bqk = sb("bqk", [P, 2])
        bperm = sb("bperm", [P, 2, 2])
        bv_all = sb("bv_all", [P, D])
        bo_all = sb("bo_all", [P, D])
        nmax = sb("nmax", [P, 2, 16])
        nmax_p = sb("nmax_p", [P, 32], BF16)
        nmax_t = sb("nmax_t", [P, 2, 32], BF16)
        o_sb = sb("o_sb", [P, 2, BANK])
        den = sb("den", [P, BATCH, HEADS * SEQ // P])
        rden = sb("rden", [P, BATCH, SEQ])
        num = sb("num", [P, TOKENS])
        phase.close()

        fa = sb("fa", [P, 2, QMAX])
        fx = sb("fx", [P, 2, QMAX])
        fs = sb("fs", [P, 2, QMAX], BF16)
        fg = sb("fg", [P, 7, QMAX], BF16)
        fblk = sb("fblk", [P, 2, 3, QMAX // QB])
        silu = sb("silu", [P, 2, FFN])
        hid = sb("hid", [P, 2, 4 * FFN])
        hid_q = sb("hid_q", [P, 2, 4 * FFN])
        hid_t = sb("hid_t", [P, 3, BANK])
        phase.close()

        a_neg = sb("a_neg", [P, NSTATE])
        dt = sb("dt", [P, TOKENS])
        dtx = sb("dtx", [P, TOKENS])
        zt = sb("zt", [P, TOKENS])
        bc32 = sb("bc32", [P, 2, TOKENS])
        bcp = sb("bcp", [P, 2, TOKENS], BF16)
        abar = sb("abar", [P, RING, SEQ])
        dbx = sb("dbx", [P, RING, SEQ])
        hst = sb("hst", [P, RING, SEQ])
        cbr = sb("cbr", [P, RING, SEQ])
        hc = sb("hc", [P, RING, SEQ])
        phase.close()

        w12 = sb("w12", [P, 2, 2, HIDDEN])
        w12_h = sb("w12_h", [P, 2, 2, HIDDEN], F32R)
        w12_l = sb("w12_l", [P, 2, 2, HIDDEN], F32R)
        xh = sb("xh", [P, TOKENS], F32R)
        xl = sb("xl", [P, TOKENS], F32R)
        act_t = sb("act_t", [P, 2, HT, BANK])
        act_h = sb("act_h", [P, 2, HT, BANK], F32R)
        act_l = sb("act_l", [P, 2, HT, BANK], F32R)
        gate = sb("gate", [P, 2, TOKENS])
        term = sb("term", [P, BANK])
        acc = sb("acc", [P, TOKENS])
        lg = sb("lg", [P, TILES, EXPERTS])
        gt = sb("gt", [P, TILES, EXPERTS, EXPERTS])
        eq = sb("eq", [P, TILES, EXPERTS, EXPERTS])
        rank = sb("rank", [P, TILES, EXPERTS])
        is01 = sb("is01", [P, 2, TILES, EXPERTS])
        top = sb("top", [P, 6, TILES])
        comb = sb("comb", [P, TILES, EXPERTS])
        comb_t = sb("comb_t", [EXPERTS, TOKENS])
        phase.close()

        q_dram = nc.dram_tensor("q_dram", (PASSES, 2, PARTS, QC, BANK), BF16, kind="Internal").ap()
        k_dram = nc.dram_tensor("k_dram", (PASSES, 2, PARTS, QC, BANK), BF16, kind="Internal").ap()
        o_dram = nc.dram_tensor("o_dram", (PASSES, P, SEQ), F32, kind="Internal").ap()
        c_dram = nc.dram_tensor("c_dram", (EXPERTS, TOKENS), F32, kind="Internal").ap()
        r_dram = nc.dram_tensor("r_dram", (BATCH, HEADS, SEQ), F32, kind="Internal").ap()

        s_x = [sem(f"s_x{n}") for n in range(2)]
        s_const = sem("s_const")
        s_centred = sem("s_centred")
        s_squared = sem("s_squared")
        s_var = sem("s_var")
        s_rstd = sem("s_rstd")
        s_normed = sem("s_normed")
        s_turned = sem("s_turned")
        s_xt = sem("s_xt")
        s_v1 = sem("s_v1")
        s_p1 = sem("s_p1")
        s_wt_ps = sem("s_wt_ps")
        s_wt = sem("s_wt")
        s_proj = sem("s_proj")
        s_rope_read = sem("s_rope_read")
        s_rope = sem("s_rope")
        s_part1 = sem("s_part1")
        s_rest = sem("s_rest")
        s_part2 = sem("s_part2")
        s_part3 = sem("s_part3")
        s_parts_out = [sem(f"s_parts_out{n}") for n in range(CHUNKS)]
        s_v_ps = sem("s_v_ps")
        s_v = sem("s_v")
        s_fill = sem("s_fill")
        s_set = sem("s_set")
        s_qk = [sem(f"s_qk{n}") for n in range(SETS)]
        s_score = sem("s_score")
        s_max = sem("s_max")
        s_nmax = sem("s_nmax")
        s_nrow = [sem(f"s_nrow{n}") for n in range(2)]
        s_st = sem("s_st")
        s_exp = sem("s_exp")
        s_pv = sem("s_pv")
        s_o = sem("s_o")
        s_o_out = [sem(f"s_o_out{n}") for n in range(2)]
        s_vq = sem("s_vq")
        s_od = [sem(f"s_od{n}") for n in range(2)]
        s_num = sem("s_num")
        s_rden = sem("s_rden")
        s_ready = sem("s_ready")
        s_att = sem("s_att")
        s_y = sem("s_y")
        s_res = sem("s_res")
        s_out = sem("s_out")
        s_wf = sem("s_wf")
        s_wfz = sem("s_wfz")
        s_blk = sem("s_blk")
        s_ss = sem("s_ss")
        s_qx = sem("s_qx")
        s_qa = sem("s_qa")
        s_quant = sem("s_quant")
        s_wft_ps = sem("s_wft_ps")
        s_wft = sem("s_wft")
        s_gu = sem("s_gu")
        s_silu = sem("s_silu")
        s_hid = sem("s_hid")
        s_ht_ps = sem("s_ht_ps")
        s_ht = sem("s_ht")
        s_down = sem("s_down")
        s_skip = sem("s_skip")
        s_b1_now = sem("s_b1_now")
        s_w12 = [sem(f"s_w12_{n}") for n in range(2)]
        s_w34 = sem("s_w34")
        s_dtw_ps = sem("s_dtw_ps")
        s_dtw = sem("s_dtw")
        s_zps = sem("s_zps")
        s_z = sem("s_z")
        s_e = sem("s_e")
        s_u = sem("s_u")
        s_ln = sem("s_ln")
        s_dt = sem("s_dt")
        s_bp = sem("s_bp")
        s_bp2 = sem("s_bp2")
        s_bp3 = sem("s_bp3")
        s_rest3 = sem("s_rest3")
        s_a = sem("s_a")
        s_abar = sem("s_abar")
        s_bb = sem("s_bb")
        s_cb = sem("s_cb")
        s_dbx = sem("s_dbx")
        s_scan = sem("s_scan")
        s_cs = sem("s_cs")
        s_hc = sem("s_hc")
        s_y3 = sem("s_y3")
        s_yt = sem("s_yt")
        s_selb = sem("s_selb")
        s_lgps = sem("s_lgps")
        s_lg = sem("s_lg")
        s_diff = sem("s_diff")
        s_ediff = sem("s_ediff")
        s_comb = sem("s_comb")
        s_combt_ps = sem("s_combt_ps")
        s_combt = sem("s_combt")
        s_b2 = sem("s_b2")
        s_l1 = sem("s_l1")
        s_gelu = sem("s_gelu")
        s_l2 = sem("s_l2")
        s_moe = sem("s_moe")
        s_acc = sem("s_acc")
        s_mstep = sem("s_mstep")
        s_xh = sem("s_xh")
        s_xl = sem("s_xl")
        s_w_h = sem("s_w_h")
        s_w_l = sem("s_w_l")
        s_act_h = sem("s_act_h")
        s_act_l = sem("s_act_l")
        s_term = sem("s_term")
        s_comb_out = sem("s_comb_out")
        s_gate = [sem(f"s_gate{n}") for n in range(2)]
        s_back = sem("s_back")
        s_final = sem("s_final")

        block = ctx.enter_context(nc.Block())

        count = {"dve": 0, "pool": 0}

        def dve_step(ins):
            count["dve"] += 1
            ins.then_inc(s_v1, 1)
            nc.vector.wait_ge(s_v1, count["dve"])

        def pool_step(ins):
            count["pool"] += 1
            ins.then_inc(s_p1, 1)
            nc.gpsimd.wait_ge(s_p1, count["pool"])

        def bc(ap2, n):
            return ap2.unsqueeze(2).to_broadcast([ap2.shape[0], ap2.shape[1], n])

        def norm_dve_a(k, h):
            a, b = h * TILES // 2, (h + 1) * TILES // 2
            dve_step(nc.vector.tensor_reduce(stat[:, 0, a:b], x[:, a:b, :], AX.X, ALU.add))
            dve_step(nc.vector.tensor_scalar(stat[:, 1, a:b], stat[:, 0, a:b], 1.0 / D, None, ALU.mult))
            if k:
                nc.vector.wait_ge(s_turned, 4 * k)
            nc.vector.tensor_tensor(xc[:, a:b, :], x[:, a:b, :], bc(stat[:, 1, a:b], D),
                                    ALU.subtract).then_inc(s_centred, 1)

        def norm_dve_b(k, h):
            a, b = h * TILES // 2, (h + 1) * TILES // 2
            u = 2 * k + h
            nc.vector.wait_ge(s_squared, u + 1)
            nc.vector.tensor_reduce(stat[:, 2, a:b], sq[:, a:b, :], AX.X, ALU.add).then_inc(s_var, 1)
            nc.vector.wait_ge(s_rstd, u + 1)
            nc.vector.wait_ge(s_centred, u + 1)
            nc.vector.tensor_tensor(xc[:, a:b, :], xc[:, a:b, :], bc(stat[:, 3, a:b], D),
                                    ALU.mult).then_inc(s_normed, 1)

        def norm_act(k, h):
            a, b = h * TILES // 2, (h + 1) * TILES // 2
            u = 2 * k + h
            nc.scalar.wait_ge(s_centred, u + 1)
            if k:
                nc.scalar.wait_ge(s_var, u - 1)
            if k == 2:
                nc.scalar.wait_ge(s_turned, 8)
            nc.scalar.activation(sq[:, a:b, :], xc[:, a:b, :], ACT.Square).then_inc(s_squared, 1)

        def norm_pool(k, h):
            a, b = h * TILES // 2, (h + 1) * TILES // 2
            u = 2 * k + h
            nc.gpsimd.wait_ge(s_var, u + 1)
            if k:
                nc.gpsimd.wait_ge(s_normed, u - 1)
            pool_step(nc.gpsimd.tensor_scalar(stat[:, 3, a:b], stat[:, 2, a:b], 1.0 / D, EPS, ALU.mult, ALU.add))
            nc.gpsimd.tensor_tensor(stat[:, 3, a:b], stat[:, 3, a:b], expo[:, a:b], ALU.pow).then_inc(s_rstd, 1)

        def turn_pe(k, g):
            if k == 1:
                nc.tensor.wait_ge(s_quant, 1 + g // 2 + 1)
            else:
                nc.tensor.wait_ge(s_normed, 2 * k + g // 2 + 1)
            if k:
                nc.tensor.wait_ge(s_xt, 4 * (k - 1) + g + 1)
            for j in range(4):
                mm = nc.tensor.transpose(ps[:, g, j * P:(j + 1) * P], (sq if k == 1 else xc)[:, 4 * g + j, :], ident[:])
            mm.then_inc(s_turned, 1)

        def turn_act(k, g):
            nc.scalar.wait_ge(s_turned, 4 * k + g + 1)
            if k == 1:
                nc.scalar.wait_ge(s_v_ps, 4)
            if k == 2:
                nc.scalar.wait_ge(s_gu, TILES)
            if k == 3:
                nc.scalar.wait_ge(s_skip, BATCH)
            nc.scalar.activation(xt[:, g * BANK:(g + 1) * BANK], ps[:, g, :], ACT.Copy).then_inc(s_xt, 1)

        X_PIECE = (1, 3)
        HID_PIECE = (2, 4, 5, 6)

        def blocks(ap):
            return ap.rearrange("p (b k) -> p b k", k=QB)

        def x_half(t, h):
            return t[:, 8 * h:8 * h + 8, :].rearrange("p t c -> p (t c)")

        def quant_scale(n, src, ready=None):
            w = src.shape[1]
            blk = fblk[:, n % 2, :, 0:w // QB]
            if ready:
                nc.vector.wait_ge(*ready)
            if n >= 2:
                nc.vector.wait_ge(s_quant, n - 1)
            dve_step(nc.vector.tensor_reduce(blk[:, 0], blocks(src), AX.X, ALU.max, apply_absolute_value=True))
            dve_step(nc.vector.tensor_scalar(blk[:, 1], blk[:, 0], 1.0 / 6.0, 1e-12, ALU.mult, ALU.max))
            nc.vector.reciprocal(blk[:, 2], blk[:, 1]).then_inc(s_blk, 1)

        def quant_pool(n, src):
            w = src.shape[1]
            nc.gpsimd.wait_ge(s_blk, n + 1)
            if n >= 2:
                nc.gpsimd.wait_ge(s_quant, n - 1)
            nc.gpsimd.tensor_tensor(blocks(fx[:, n % 2, 0:w]), blocks(src), bc(fblk[:, n % 2, 2, 0:w // QB], QB),
                                    ALU.mult).then_inc(s_qx, 1)
            nc.gpsimd.wait_ge(s_qa, 2 * (n + 1))
            nc.gpsimd.tensor_tensor(blocks(fx[:, n % 2, 0:w]), blocks(fs[:, n % 2, 0:w]),
                                    bc(fblk[:, n % 2, 1, 0:w // QB], QB), ALU.mult).then_inc(s_ss, 1)

        def quant_act(n, w):
            nc.scalar.wait_ge(s_qx, n + 1)
            if n >= 2:
                nc.scalar.wait_ge(s_quant, n - 1)
                nc.scalar.wait_ge(s_ss, n - 1)
            nc.scalar.activation(fa[:, n % 2, 0:w], fx[:, n % 2, 0:w], ACT.Abs).then_inc(s_qa, 1)
            nc.scalar.activation(fs[:, n % 2, 0:w], fx[:, n % 2, 0:w], ACT.Sign).then_inc(s_qa, 1)

        def quant_grid(n, dst, free=None):
            w = dst.shape[1]
            a = fa[:, n % 2, 0:w]
            g = [fg[:, m, 0:w] for m in range(7)]
            nc.vector.wait_ge(s_qa, 2 * (n + 1))
            if n:
                nc.vector.wait_ge(s_quant, n)
            for m in range(7):
                ins = nc.vector.tensor_scalar(g[m], a, MIDS[m], JUMPS[m], ALU.is_gt, ALU.mult)
            dve_step(ins)
            for m in (0, 2, 4):
                ins = nc.vector.tensor_tensor(g[m], g[m], g[m + 1], ALU.add)
            dve_step(ins)
            dve_step(nc.vector.tensor_tensor(g[0], g[0], g[2], ALU.add))
            dve_step(nc.vector.tensor_tensor(g[4], g[4], g[6], ALU.add))
            dve_step(nc.vector.tensor_tensor(g[0], g[0], g[4], ALU.add))
            if free:
                nc.vector.wait_ge(*free)
            nc.vector.wait_ge(s_ss, n + 1)
            nc.vector.tensor_tensor(dst, g[0], fx[:, n % 2, 0:w], ALU.mult).then_inc(s_quant, 1)

        N_CONST = 6 + 4 + 2
        N_W34 = 3 + 16 + 6

        LOADS = 16 * (2 * (PARTS + 1) + 1)

        @block.sync
        def _(sp):
            xv = i["L0_attn_x"].rearrange("b (t p) c -> p (b t) c", p=P)
            for h in range(2):
                sp.dma_start(x[:, 8 * h:8 * h + 8, :], xv[:, 8 * h:8 * h + 8, :]).then_inc(s_x[h], 16)
            sp.dma_start(ident[:], i["ident"]).then_inc(s_const, 16)
            for n, w in enumerate(("Wq", "Wk", "Wv", "Wo")):
                sp.dma_start(w4[:, n, :], i["L0_attn_" + w]).then_inc(s_const, 16)
            sp.dma_start(perm[:], i["perm"].rearrange("n p c -> p n c")).then_inc(s_const, 16)
            for n, b in enumerate(("bq", "bk")):
                sp.dma_start(bqk[:, n:n + 1], i["L0_attn_" + b].rearrange("(p o) -> p o", o=1)).then_inc(s_const, 16)
            sp.dma_start(cos[:], i["cos"]).then_inc(s_const, 16)
            sp.dma_start(sin[:], i["sin"]).then_inc(s_const, 16)
            for b, t in (("bv", bv_all), ("bo", bo_all)):
                sp.dma_start(t[:], i["L0_attn_" + b].rearrange("(o c) -> o c", o=1).to_broadcast([P, D])).then_inc(s_const, 16)

            sp.wait_ge(s_fill, 1)
            for n in range(SETS):
                for k, t in enumerate((qs[n], ks[n])):
                    sp.dma_start(t[PROD:ROWS].rearrange("n f (a h) t -> n (f a) (h t)", h=2), fill[:, k]).then_inc(s_set, 16)

            sp.wait_ge(s_wfz, 1)
            for n, w in enumerate(("gate", "up")):
                src = i["L0_ffn_w_" + w]
                sp.dma_start(wf[:, 3 * n * D:(3 * n + 2) * D].rearrange("p (t c) -> p t c", c=D),
                             src[0:2 * P].rearrange("(t p) c -> p t c", p=P)).then_inc(s_wf, 16)
                sp.dma_start(wf[0:FFN - 2 * P, (3 * n + 2) * D:(3 * n + 3) * D], src[2 * P:FFN]).then_inc(s_wf, 16)
            sp.dma_start(wf[:, 6 * D:WF], i["L0_ffn_w_down"]).then_inc(s_wf, 16)

            col = lambda name: i["L1_attn_" + name].rearrange("(p o) -> p o", o=1)
            sp.dma_start(wdt[:], i["L1_attn_dt_w"]).then_inc(s_w34, 16)
            sp.dma_start(cols[:, 0:1], col("dt_b")).then_inc(s_w34, 16)
            sp.dma_start(cols[:, 3:4], col("D_skip")).then_inc(s_w34, 16)
            for n in range(4):
                rows = slice(NSTATE * n, NSTATE * (n + 1))
                for m, w in enumerate("BC"):
                    sp.dma_start(wbc[rows, m], i[f"L1_attn_{w}_w"]).then_inc(s_w34, 16)
                    sp.dma_start(cols[rows, 1 + m:2 + m], col(w + "_b")).then_inc(s_w34, 16)
            sp.dma_start(log_a[:], i["L1_attn_log_A"]).then_inc(s_w34, 16)
            sp.dma_start(sel[:], i["sel"]).then_inc(s_w34, 16)
            sp.dma_start(wgate[:], i["L1_ffn_gate_w"]).then_inc(s_w34, 16)
            sp.dma_start(b1r[:], i["L1_ffn_b1"].rearrange("e (h p) -> (e h) p", p=P)).then_inc(s_w34, 16)
            sp.dma_start(b2[:], i["L1_ffn_b2"]).then_inc(s_w34, 16)
            sp.dma_start(tri[:], i["tri"]).then_inc(s_w34, 16)

            def store_parts(u):
                c, kind = divmod(u, 2)
                sp.wait_ge(s_part3, u + 1)
                dst = (q_dram, k_dram)[kind]
                for g in range(QUAD):
                    sp.dma_start(dst[4 * (c // 2) + g, c % 2].rearrange("n c t -> c n t"),
                                 parts[QC * g:QC * g + QC, u % CHUNKS]).then_inc(s_parts_out[u % CHUNKS], 16)

            def load(it, p):
                for f in range(2):
                    sp.dma_start(qs[p][0:PROD, f], q_dram[bass.ds(it, 1), f].rearrange(
                        "o n (d h) t -> (o n d) (h t)", h=QUAD).unsqueeze(1).to_broadcast([PARTS * HD, PARTS, QUAD * BANK])).then_inc(s_qk[p], 16)
                    for a in range(PARTS):
                        sp.dma_start(ks[p][HD * PARTS * a:HD * PARTS * (a + 1), f], k_dram[bass.ds(it, 1), f].rearrange(
                            "o n (d h) t -> d (o n) (h t)", h=QUAD)).then_inc(s_qk[p], 16)
                sp.dma_start(qs[p][PROD:PROD + 2], fill[0:16, 0, 0:BANK]).then_inc(s_qk[p], 16)

            def store_maxima(it, p, half):
                sp.wait_ge(s_nmax, 2 * it + half + 1)
                for z in range(4):
                    sp.dma_start(
                        qs[p][PROD:PROD + 2, half].rearrange("n h (q t) -> n (h q) t", t=P)[:, :, 32 * z:32 * z + 32],
                        nmax_t[32 * z:32 * z + 32, half, :]).then_inc(s_nrow[half], 16)

            def store_out(it, half):
                sp.wait_ge(s_o, 2 * it + half + 2)
                sp.dma_start(o_dram[bass.ds(it, 1), :, half * BANK:(half + 1) * BANK].rearrange("o r t -> (o r) t"),
                             o_sb[:, half, :]).then_inc(s_o_out[half], 16)

            for u in range(CHUNKS):
                store_parts(u)
            for n in range(CHUNKS):
                sp.wait_ge(s_parts_out[n], 16 * QUAD)
            sp.wait_ge(s_set, 16 * 2 * SETS)
            for p in range(SETS):
                load(p, p)
            for u in range(CHUNKS, 2 * CHUNKS):
                store_parts(u)
            for n in range(CHUNKS):
                sp.wait_ge(s_parts_out[n], 16 * QUAD * 2)
            store_maxima(0, 0, 0)
            store_maxima(0, 0, 1)

            def one_pass(it, p, more, again=None):
                if more:
                    store_maxima(it + 1, (p + 1) % SETS, 0)
                store_out(it, 0)
                if again is not None:
                    sp.wait_ge(s_pv, STEPS * (it + 1))
                    load(again, p)
                store_out(it, 1)
                if more:
                    store_maxima(it + 1, (p + 1) % SETS, 1)

            def load_out(b):
                sp.wait_ge(s_o_out[0], 16 * (4 * b + 4 + 1))
                sp.wait_ge(s_o_out[1], 16 * (4 * b + 4 + 1))
                rows = o_dram[4 * b:4 * b + 4].rearrange("q (h r) t -> (q h) r t", r=32)
                sp.dma_start(den[:, b], rows[:, HD]).then_inc(s_od[b], 16)
                sp.dma_start(num[:, b * SEQ:(b + 1) * SEQ], rows[:, 0:HD]).then_inc(s_num, 16)
                sp.wait_ge(s_rden, b + 1)
                sp.dma_start(r_dram[b].rearrange("h (c t) -> (h c) t", c=P // HEADS), den[:, b]).then_inc(s_od[b], 16)
                sp.wait_ge(s_od[b], 32)
                sp.dma_start(rden[:, b], r_dram[b].unsqueeze(1).to_broadcast([HEADS, HD, SEQ])).then_inc(s_num, 16)
                sp.wait_ge(s_num, 32 * (b + 1))
                sp.sem_inc(s_ready, 1)

            with sp.Fori(0, PASSES // SETS) as r:
                for p in range(SETS):
                    one_pass(SETS * r + p, p, True, (SETS * r + p + SETS) % PASSES)
            load_out(0)
            one_pass(PASSES - 2, 0, True)
            one_pass(PASSES - 1, 1, False)
            load_out(1)

            def load_expert(e, p):
                sp.dma_start(w12[:, p, 0], i["L1_ffn_w1"][bass.ds(e, 1)].rearrange("o c h -> c (o h)")).then_inc(s_w12[p], 16)
                sp.dma_start(w12[:, p, 1].rearrange("p (t c) -> p t c", c=D),
                             i["L1_ffn_w2"][bass.ds(e, 1)].rearrange("o (t p) c -> p (o t) c", p=P)).then_inc(s_w12[p], 16)

            def load_gate(e, p):
                sp.dma_start(gate[:, p], c_dram[bass.ds(e, 1)].to_broadcast([P, TOKENS])).then_inc(s_gate[p], 16)

            sp.wait_ge(s_skip, BATCH)
            sp.wait_ge(s_yt, 4)
            load_expert(0, 0)
            load_expert(1, 1)
            sp.wait_ge(s_combt, 1)
            sp.dma_start(c_dram, comb_t[:]).then_inc(s_comb_out, 16)
            sp.wait_ge(s_comb_out, 16)
            load_gate(0, 0)
            load_gate(1, 1)
            with sp.Fori(1, EXPERTS // 2) as r:
                for p in range(2):
                    sp.wait_ge(s_moe, 2 + CHUNKS * (2 * r + p - 1))
                    load_expert(2 * r + p, p)
                    load_gate(2 * r + p, p)
            ov = out.rearrange("b (t p) c -> p (b t) c", p=P)
            for c in range(CHUNKS):
                sp.wait_ge(s_final, c + 1)
                sp.dma_start(ov[:, 4 * c:4 * c + 4], x[:, 4 * c:4 * c + 4]).then_inc(s_out, 16)
            sp.wait_ge(s_out, 16 * CHUNKS)

        @block.gpsimd
        def _(pool):
            nc.gpsimd.memset(zero[:], 0.0)
            nc.gpsimd.memset(fill[:, 0], 0.0)
            nc.gpsimd.memset(fill[:, 1], 1.0).then_inc(s_fill, 1)
            pool_step(nc.gpsimd.memset(expo[:], -0.5))
            for h in range(2):
                norm_pool(0, h)
            pool.wait_ge(s_rstd, 2)
            for n in range(SETS):
                ins = nc.gpsimd.memset(vq[n][:], 1.0)
            pool_step(ins)
            def third_part(u):
                b = u % 2
                pool.wait_ge(s_rest, u + 1)
                pool.wait_ge(s_part2, u + 1)
                nc.gpsimd.tensor_tensor(parts[:, u % CHUNKS, 2], rest[:, b], parts[:, u % CHUNKS, 1], ALU.subtract).then_inc(s_part3, 1)

            for u in range(2 * CHUNKS):
                b = u % 2
                pool.wait_ge(s_part1, u + 1)
                if u >= 2:
                    pool.wait_ge(s_part3, u - 1)
                nc.gpsimd.tensor_tensor(rest[:, b], rot[:, b, 2], parts[:, u % CHUNKS, 0], ALU.subtract).then_inc(s_rest, 1)
                if u:
                    third_part(u - 1)
            third_part(2 * CHUNKS - 1)

            def values(it, p):
                nc.gpsimd.tensor_copy(vq[p][:, :, :, 0:HD], v[:, bass.ds(it, 1)].rearrange(
                    "p o k (h d) -> p (o k) h d", d=HD)).then_inc(s_vq, 1)

            pool.wait_ge(s_v, 4)
            for p in range(SETS):
                values(p, p)
            with pool.Fori(1, PASSES // SETS) as r:
                for p in range(SETS):
                    pool.wait_ge(s_pv, STEPS * (SETS * (r - 1) + p + 1))
                    values(SETS * r + p, p)
            for p in range(PASSES % SETS):
                pool.wait_ge(s_pv, STEPS * (SETS * (PASSES // SETS - 1) + p + 1))
                values(PASSES - PASSES % SETS + p, p)

            hidden_slot = lambda g: hid[:, g % 2]
            norm_pool(1, 0)
            pool.wait_ge(s_qk[SETS - 1], LOADS * (PASSES // SETS + 1))
            quant_pool(0, wf[:])
            quant_pool(1, x_half(xc, 0))
            quant_pool(2, hidden_slot(0))
            norm_pool(1, 1)
            quant_pool(3, x_half(xc, 1))
            for g in range(1, 4):
                quant_pool(HID_PIECE[g], hidden_slot(g))

            norm_pool(2, 0)
            norm_pool(2, 1)

            def outflow(b, n, slot):
                m = NSTATE * b + n
                pool.wait_ge(s_scan, m + 1)
                pool.wait_ge(s_cs, m + 1)
                if not (isinstance(m, int) and m < RING):
                    pool.wait_ge(s_y3, m - RING + 1)
                nc.gpsimd.tensor_tensor(hc[:, slot], hst[:, slot], cbr[:, slot], ALU.mult).then_inc(s_hc, 1)

            for b in range(BATCH):
                if b == 0:
                    for n in range(RING):
                        outflow(0, n, n)
                with pool.Fori(1 - b, NSTATE // RING) as k:
                    for n in range(RING):
                        outflow(b, RING * k + n, n)

            norm_pool(3, 0)
            norm_pool(3, 1)
            with pool.Fori(0, EXPERTS // 2) as k:
                for p in range(2):
                    pool.wait_ge(s_w12[p], 32 * (k + 1))
                    nc.gpsimd.tensor_tensor(w12_h[:, p], w12[:, p], zero[:].unsqueeze(2).to_broadcast([P, 2, HIDDEN]),
                                            ALU.subtract).then_inc(s_w_h, 1)
                    pool.wait_ge(s_w_h, 2 * k + p + 1)
                    nc.gpsimd.tensor_tensor(w12_l[:, p], w12[:, p], w12_h[:, p].bitcast(F32), ALU.subtract).then_inc(s_w_l, 1)

        @block.scalar
        def _(act):
            for h in range(2):
                norm_act(0, h)
            act.wait_ge(s_wt_ps, 1)
            nc.scalar.activation(wt[:, 0:4, :], ps[:, 4, :], ACT.Copy).then_inc(s_wt, 1)
            nc.scalar.activation(wt[:, 4:6, :], ps[:, 5, 0:2 * D], ACT.Copy).then_inc(s_wt, 1)
            nc.scalar.activation(bperm[:], ps[:, 5, 2 * D:2 * D + 4].rearrange("p (n k) -> p n k", k=2), ACT.Copy).then_inc(s_wt, 1)
            def second_part(u):
                act.wait_ge(s_rest, u + 1)
                nc.scalar.activation(parts[:, u % CHUNKS, 1], rest[:, u % 2], ACT.Copy).then_inc(s_part2, 1)

            turn_act(0, 0)
            turn_act(0, 1)
            for u in range(2 * CHUNKS):
                b = u % 2
                act.wait_ge(s_rope, u + 1)
                if u >= CHUNKS:
                    act.wait_ge(s_parts_out[u % CHUNKS], 16 * QUAD)
                nc.scalar.activation(parts[:, u % CHUNKS, 0], rot[:, b, 2], ACT.Copy).then_inc(s_part1, 1)
                if u:
                    second_part(u - 1)
                if u == 2:
                    turn_act(0, 2)
                    turn_act(0, 3)
            second_part(2 * CHUNKS - 1)

            def one_pass(it, first, between={}):
                for s in range(STEPS):
                    if s in between:
                        between[s]()
                    for j in range(4):
                        n = 4 * s + j
                        if j == 0 and s >= 2:
                            act.wait_ge(s_pv, STEPS * it + s - 1)
                        act.wait_ge(s_st, 4 * STEPS * it + n + 1)
                        nc.scalar.activation(prob[:, n % 8], ps[:, 4 + (first + n) % 3], ACT.Exp,
                                             scale=ATT_SCALE).then_inc(s_exp, 1)
                    if s == KT:
                        evacuate(it, 0)
                evacuate(it, 1)

            def evacuate(it, half):
                act.wait_ge(s_pv, STEPS * it + KT * (half + 1))
                act.wait_ge(s_o_out[half], 16 * (it + 1))
                nc.scalar.activation(o_sb[:, half], ps[:, 7], ACT.Copy).then_inc(s_o, 1)

            for half in range(2):
                act.sem_inc(s_o_out[half], 16)
            with act.Fori(0, PASSES // SETS) as r:
                for p in range(SETS):
                    one_pass(SETS * r + p, 4 * STEPS * p)
            one_pass(PASSES - 2, 0)

            def turned_weights():
                act.wait_ge(s_wft_ps, 1)
                nc.scalar.activation(wgu_t[:], ps[:, 1:3, 0:FFN], ACT.Copy).then_inc(s_wft, 1)
                nc.scalar.activation(wd_t[:, 0:2], ps[:, 3, 0:2 * D].rearrange("p (t c) -> p t c", c=D), ACT.Copy).then_inc(s_wft, 1)
                nc.scalar.activation(wd_t[0:FFN - 2 * P, 2], ps[0:FFN - 2 * P, 3, 2 * D:3 * D], ACT.Copy).then_inc(s_wft, 1)

            def turned_x(g, bank):
                act.wait_ge(s_turned, 4 + g + 1)
                act.wait_ge(s_v_ps, 4)
                nc.scalar.activation(xt[:, g * BANK:(g + 1) * BANK], ps[:, bank, :], ACT.Copy).then_inc(s_xt, 1)

            def turned_hidden(g):
                for j in range(3):
                    rows = min(P, FFN - j * P)
                    act.wait_ge(s_ht_ps, 3 * g + j + 1)
                    if g:
                        act.wait_ge(s_down, g)
                    nc.scalar.activation(hid_t[0:rows, j], ps[0:rows, 4 + j], ACT.Copy).then_inc(s_ht, 1)

            def silus(t0, t1):
                for t in range(t0, t1):
                    act.wait_ge(s_gu, t + 1)
                    if t >= 2:
                        act.wait_ge(s_hid, t - 1)
                    nc.scalar.activation(silu[:, t % 2], ps[:, 2 * (t % 2), 0:FFN], ACT.Silu).then_inc(s_silu, 1)

            one_pass(PASSES - 1, 4 * STEPS, {
                4: lambda: norm_act(1, 0),
                7: lambda: quant_act(0, WF),
                10: lambda: quant_act(1, TOKENS // 2),
                13: turned_weights})
            turned_x(0, 0)
            turned_x(1, 1)
            silus(0, 4)
            quant_act(2, QMAX)
            norm_act(1, 1)
            silus(4, 6)
            quant_act(3, TOKENS // 2)
            silus(6, 8)
            turned_hidden(0)
            quant_act(4, QMAX)
            turned_x(2, 4)
            turned_x(3, 5)
            silus(8, 14)
            quant_act(5, QMAX)
            silus(14, 16)
            turned_hidden(1)
            quant_act(6, QMAX)
            norm_act(2, 0)
            turned_hidden(2)
            turned_hidden(3)

            act.wait_ge(s_dtw_ps, 1)
            nc.scalar.activation(ssm_t[:], ps[:, 4, 0:3 * D].rearrange("p (t c) -> p t c", c=D), ACT.Copy).then_inc(s_dtw, 1)
            nc.scalar.activation(b1t[:, 0:EXPERTS * HT], ps[:, 4, 3 * D:3 * D + EXPERTS * HT], ACT.Copy).then_inc(s_dtw, 1)
            nc.scalar.activation(sel_b[:], sel[:], ACT.Copy).then_inc(s_selb, 1)
            norm_act(2, 1)
            nc.scalar.activation(a_neg[:], log_a[:], ACT.Exp).then_inc(s_a, 1)
            for g in range(4):
                turn_act(2, g)
            for c in range(CHUNKS):
                w = slice(c * BANK, (c + 1) * BANK)
                for n, dst in enumerate((zt[:, w], bc32[:, 0, w], bc32[:, 1, w])):
                    act.wait_ge(s_zps, 3 * c + n + 1)
                    nc.scalar.activation(dst, ps[:, 5 + n], ACT.Identity, bias=cols[:, n:n + 1]).then_inc(s_z, 1)
            for b in range(BATCH):
                w = slice(b * SEQ, (b + 1) * SEQ)
                act.wait_ge(s_z, 6 * (b + 1))
                nc.scalar.activation(dt[:, w], zt[:, w], ACT.Abs).then_inc(s_e, 1)
                act.wait_ge(s_e, 2 * b + 1)
                nc.scalar.activation(dt[:, w], dt[:, w], ACT.Exp, scale=-1.0).then_inc(s_e, 1)
                for n in range(2):
                    nc.scalar.activation(bcp[:, n, w], bc32[:, n, w], ACT.Copy).then_inc(s_bp, 1)
                act.wait_ge(s_u, b + 1)
                nc.scalar.activation(cbr[:, b], dtx[:, w], ACT.Ln).then_inc(s_ln, 1)
                for n in range(2):
                    act.wait_ge(s_rest3, 2 * b + n + 1)
                    nc.scalar.activation(bcp[64:P, n, w], bc32[64:P, n, w], ACT.Copy).then_inc(s_bp2, 1)

            def factors(b, n, slot):
                m = NSTATE * b + n
                first = isinstance(m, int) and m < RING
                if not first:
                    act.wait_ge(s_scan, m - RING + 1)
                act.wait_ge(s_a, 2)
                nc.scalar.activation(abar[:, slot], dt[:, b * SEQ:(b + 1) * SEQ], ACT.Exp,
                                     scale=a_neg[:, bass.ds(n, 1)]).then_inc(s_abar, 1)
                act.wait_ge(s_cb, m + 1)
                if not first:
                    act.wait_ge(s_hc, m - RING + 1)
                nc.scalar.activation(cbr[:, slot], ps[:, 4:6], ACT.Copy).then_inc(s_cs, 1)

            act.wait_ge(s_a, 2)
            act.wait_ge(s_dt, 2 * BATCH)
            for b in range(BATCH):
                if b == 0:
                    for n in range(RING):
                        factors(0, n, n)
                with act.Fori(1 - b, NSTATE // RING) as k:
                    for n in range(RING):
                        factors(b, RING * k + n, n)

            norm_act(3, 0)
            norm_act(3, 1)
            for g in range(4):
                turn_act(3, g)
                nc.scalar.activation(xh[:, g * BANK:(g + 1) * BANK], ps[:, g], ACT.Copy).then_inc(s_xh, 1)

            def unit(k, u):
                m = UNITS * k + u
                act.wait_ge(s_l2, m + 1)
                if u % CHUNKS == 0:
                    act.wait_ge(s_b1_now, 2 * k + u // CHUNKS + 1)
                for h in range(HT):
                    act.wait_ge(s_l1, HT * m + h + 1)
                    nc.scalar.activation(act_t[:, u % 2, h], ps[:, h], ACT.Gelu,
                                         bias=b1_now[:, u // CHUNKS, h:h + 1]).then_inc(s_gelu, 1)
                    if h % 2:
                        act.wait_ge(s_gelu, HT * (m + 1) + h + 1)
                        nc.scalar.activation(act_h[:, u % 2, h - 1:h + 1], act_t[:, u % 2, h - 1:h + 1],
                                             ACT.Copy).then_inc(s_act_h, 1)

            act.sem_inc(s_gelu, HT)
            unit(0, 0)
            act.wait_ge(s_diff, 1)
            nc.scalar.activation(top[:, 3], top[:, 2], ACT.Exp).then_inc(s_ediff, 1)
            act.wait_ge(s_combt_ps, 1)
            nc.scalar.activation(comb_t[:].rearrange("e (g t) -> e g t", t=BANK), ps[0:EXPERTS, 4:8], ACT.Copy).then_inc(s_combt, 1)
            for c in range(CHUNKS):
                act.wait_ge(s_b2, c + 1)
                nc.scalar.activation(acc[:, c * BANK:(c + 1) * BANK], ps[:, 4 + c], ACT.Copy).then_inc(s_acc, 1)
            with act.Fori(0, EXPERTS // 2 - 1) as k:
                for u in range(1, UNITS):
                    unit(k, u)
                unit(k + 1, 0)
            for u in range(1, UNITS):
                unit(EXPERTS // 2 - 1, u)

        @block.vector
        def _(dve):
            nc.vector.memset(ps[:, 7], 0.0).then_inc(s_o, 1)
            nc.vector.memset(wf[:], 0.0).then_inc(s_wfz, 1)
            dve_step(nc.vector.memset(b1t[:, EXPERTS * HT:], 0.0))
            for h in range(2):
                dve.wait_ge(s_x[h], 16)
                norm_dve_a(0, h)
            for h in range(2):
                norm_dve_b(0, h)
            dve.wait_ge(s_const, 16 * N_CONST)
            dve.wait_ge(s_wt, 3)
            for u in range(2 * CHUNKS):
                c, kind = divmod(u, 2)
                b = u % 2
                t0 = (c % 2) * BANK
                dve.wait_ge(s_proj, u + 1)
                if u >= 2:
                    dve.wait_ge(s_rest, u - 1)
                nc.vector.scalar_tensor_tensor(rot[:, b, 0], ps[:, 4 + 2 * b], bperm[:, 0, kind:kind + 1],
                                               cos[:, t0:t0 + BANK], ALU.add, ALU.mult)
                ins = nc.vector.scalar_tensor_tensor(rot[:, b, 1], ps[:, 5 + 2 * b], bperm[:, 1, kind:kind + 1],
                                                     sin[:, t0:t0 + BANK], ALU.add, ALU.mult)
                ins.then_inc(s_rope_read, 1)
                dve.wait_ge(s_rope_read, u + 1)
                nc.vector.tensor_tensor(rot[:, b, 2], rot[:, b, 0], rot[:, b, 1], ALU.add).then_inc(s_rope, 1)
            for g in range(4):
                b, k0 = divmod(4 * g, KT)
                dve.wait_ge(s_v_ps, g + 1)
                for j in range(4):
                    ins = nc.vector.tensor_tensor(v[:, 4 * b:4 * b + 4, k0 + j, :],
                                                  ps[:, g, j * P:(j + 1) * P].rearrange("p (q c) -> p q c", c=QC),
                                                  bv_all[:].rearrange("p (q c) -> p q c", c=QC), ALU.add)
                ins.then_inc(s_v, 1)

            def maxima(it):
                for half in range(2):
                    for n in range(16):
                        t = 16 * half + n
                        dve.wait_ge(s_score, 32 * it + t + 1)
                        nc.vector.tensor_reduce(nmax[:, half, n:n + 1], ps[:, 2 * (t % 2):2 * (t % 2) + 2, :],
                                                AX.XY, ALU.max, negate=True).then_inc(s_max, 1)
                    w = 2 * (2 * it + half)
                    dve.wait_ge(s_max, 32 * it + 16 * half + 16)
                    nc.vector.tensor_copy(nmax_p[:, 0:16], nmax[:, half]).then_inc(s_mstep, 1)
                    dve.wait_ge(s_mstep, w + 1)
                    nc.vector.tensor_tensor(nmax_p[:, 16:32], nmax[:, half], nmax_p[:, 0:16], ALU.subtract).then_inc(s_mstep, 1)
                    dve.wait_ge(s_mstep, w + 2)
                    dve.wait_ge(s_nrow[half], 64 * it)
                    nc.vector.transpose(nmax_t[:, half, :], nmax_p[:]).then_inc(s_nmax, 1)

            maxima(0)
            with dve.Fori(1, PASSES - 1) as it:
                maxima(it)

            def inverse_denominators(b):
                dve.wait_ge(s_od[b], 16)
                nc.vector.reciprocal(den[:, b], den[:, b]).then_inc(s_rden, 1)

            def attention_out(b):
                w = slice(b * SEQ, (b + 1) * SEQ)
                dve.wait_ge(s_ready, b + 1)
                nc.vector.tensor_tensor(num[:, w], num[:, w], rden[:, b], ALU.mult).then_inc(s_att, 1)
                for g in (2 * b, 2 * b + 1):
                    dve_step(nc.vector.tensor_tensor(x[:, 4 * g:4 * g + 4, :], x[:, 4 * g:4 * g + 4, :],
                                                     bo_all[:].unsqueeze(1).to_broadcast([P, 4, D]), ALU.add))
                    dve.wait_ge(s_y, g + 1)
                    nc.vector.tensor_tensor(x[:, 4 * g:4 * g + 4, :], x[:, 4 * g:4 * g + 4, :],
                                            ps[:, 4 * b + g % 2, :].rearrange("p (t c) -> p t c", c=D), ALU.add).then_inc(s_res, 1)

            inverse_denominators(0)
            maxima(PASSES - 1)

            attention_out(0)
            dve.wait_ge(s_res, 2)
            norm_dve_a(1, 0)
            dve.wait_ge(s_qk[SETS - 1], LOADS * (PASSES // SETS + 1))
            quant_scale(0, wf[:], (s_wf, 16 * 5))
            norm_dve_b(1, 0)
            quant_scale(1, x_half(xc, 0), (s_normed, 3))
            quant_grid(0, wfq[:])
            quant_grid(1, x_half(sq, 0))
            inverse_denominators(1)

            def hidden(g):
                for t in range(4 * g, 4 * g + 4):
                    dve.wait_ge(s_silu, t + 1)
                    if g >= 2:
                        dve.wait_ge(s_qx, HID_PIECE[g - 2] + 1)
                    nc.vector.tensor_tensor(hid[:, g % 2, (t % 4) * FFN:(t % 4 + 1) * FFN], silu[:, t % 2],
                                            ps[:, 2 * (t % 2) + 1, 0:FFN], ALU.mult).then_inc(s_hid, 1)
                quant_scale(HID_PIECE[g], hid[:, g % 2], (s_hid, 4 * g + 4))

            def down(g):
                dve.wait_ge(s_down, g + 1)
                nc.vector.tensor_tensor(x[:, 4 * g:4 * g + 4, :], x[:, 4 * g:4 * g + 4, :],
                                        ps[:, 7].rearrange("p (t c) -> p t c", c=D), ALU.add).then_inc(s_res, 1)

            hidden(0)
            attention_out(1)
            dve.wait_ge(s_res, 4)
            norm_dve_a(1, 1)
            norm_dve_b(1, 1)
            quant_grid(2, hid_q[:, 0])
            quant_scale(3, x_half(xc, 1), (s_normed, 4))
            hidden(1)
            quant_grid(3, x_half(sq, 1))
            down(0)
            quant_grid(4, hid_q[:, 1])
            hidden(2)
            hidden(3)
            quant_grid(5, hid_q[:, 0], (s_ht_ps, 3))
            down(1)
            dve.wait_ge(s_res, 6)
            norm_dve_a(2, 0)
            quant_grid(6, hid_q[:, 1], (s_ht_ps, 6))
            norm_dve_b(2, 0)
            down(2)
            down(3)

            dve.wait_ge(s_res, 8)
            norm_dve_a(2, 1)
            norm_dve_b(2, 1)
            dve.wait_ge(s_a, 1)
            nc.vector.tensor_scalar(a_neg[:], a_neg[:], -1.0, None, ALU.mult).then_inc(s_a, 1)
            for b in range(BATCH):
                w = slice(b * SEQ, (b + 1) * SEQ)
                dve.wait_ge(s_e, 2 * b + 2)
                nc.vector.tensor_scalar(dtx[:, w], dt[:, w], 1.0, None, ALU.add).then_inc(s_u, 1)
                for n in range(2):
                    dve.wait_ge(s_bp, 2 * b + n + 1)
                    nc.vector.tensor_tensor(bc32[64:P, n, w], bc32[64:P, n, w], bcp[64:P, n, w], ALU.subtract).then_inc(s_rest3, 1)
                dve.wait_ge(s_u, b + 1)
                dve_step(nc.vector.scalar_tensor_tensor(dt[:, w], dtx[:, w], 1.0, dt[:, w], ALU.subtract, ALU.subtract))
                dve.wait_ge(s_ln, b + 1)
                dve_step(nc.vector.tensor_tensor(dt[:, w], cbr[:, b], dt[:, w], ALU.subtract))
                nc.vector.scalar_tensor_tensor(dt[:, w], zt[:, w], 0.0, dt[:, w], ALU.max, ALU.add).then_inc(s_dt, 1)
                for n in range(2):
                    dve.wait_ge(s_bp2, 2 * b + n + 1)
                    nc.vector.tensor_tensor(bcp[96:P, n, w], bc32[96:P, n, w], bcp[96:P, n, w], ALU.subtract).then_inc(s_bp3, 1)
                dve.wait_ge(s_dt, 2 * b + 1)
                nc.vector.tensor_tensor(dtx[:, w], dt[:, w], xt[:, w], ALU.mult).then_inc(s_dt, 1)

            def inflow(b, n, slot):
                m = NSTATE * b + n
                dve.wait_ge(s_bb, m + 1)
                if not (isinstance(m, int) and m < RING):
                    dve.wait_ge(s_scan, m - RING + 1)
                nc.vector.tensor_tensor(dbx[:, slot].rearrange("p (k t) -> p k t", k=2),
                                        dtx[:, b * SEQ:(b + 1) * SEQ].rearrange("p (k t) -> p k t", k=2),
                                        ps[:, 2 * (slot % 2):2 * (slot % 2) + 2], ALU.mult).then_inc(s_dbx, 1)

            def scan(b, n, slot):
                m = NSTATE * b + n
                dve.wait_ge(s_dbx, m + 1)
                dve.wait_ge(s_abar, m + 1)
                if not (isinstance(m, int) and m < RING):
                    dve.wait_ge(s_hc, m - RING + 1)
                nc.vector.tensor_tensor_scan(hst[:, slot], abar[:, slot], dbx[:, slot], 0.0, ALU.mult, ALU.add).then_inc(s_scan, 1)

            def skip(b):
                w = slice(b * SEQ, (b + 1) * SEQ)
                dve.wait_ge(s_y3, NSTATE * (b + 1))
                nc.vector.scalar_tensor_tensor(zt[:, w].rearrange("p (k t) -> p k t", k=2),
                                               xt[:, w].rearrange("p (k t) -> p k t", k=2), cols[:, 3:4],
                                               ps[:, 6:8], ALU.mult, ALU.add).then_inc(s_skip, 1)

            dve.wait_ge(s_dt, 2 * BATCH)
            inflow(0, 0, 0)
            for b in range(BATCH):
                for n in range(RING):
                    inflow(b, n + 1, (n + 1) % RING)
                    scan(b, n, n)
                    if b and n == 1:
                        skip(b - 1)
                with dve.Fori(1, NSTATE // RING - 1) as k:
                    for n in range(RING):
                        inflow(b, RING * k + n + 1, (n + 1) % RING)
                        scan(b, RING * k + n, n)
                for n in range(NSTATE - RING, NSTATE):
                    if NSTATE * b + n + 1 < BATCH * NSTATE:
                        inflow(*divmod(NSTATE * b + n + 1, NSTATE), (n + 1) % RING)
                    scan(b, n, n % RING)
            skip(BATCH - 1)
            for g in range(4):
                dve.wait_ge(s_yt, g + 1)
                nc.vector.tensor_tensor(x[:, 4 * g:4 * g + 4, :], x[:, 4 * g:4 * g + 4, :],
                                        ps[:, g].rearrange("p (t c) -> p t c", c=D), ALU.add).then_inc(s_res, 1)

            dve.wait_ge(s_res, 12)
            norm_dve_a(3, 0)
            norm_dve_a(3, 1)
            norm_dve_b(3, 0)
            norm_dve_b(3, 1)
            for c in range(CHUNKS):
                dve.wait_ge(s_xh, c + 1)
                w = slice(c * BANK, (c + 1) * BANK)
                nc.vector.tensor_tensor(xl[:, w], xt[:, w], xh[:, w].bitcast(F32), ALU.subtract).then_inc(s_xl, 1)

            def next_bias(e, p):
                nc.vector.tensor_scalar(b1_now[:, p], b1t[:, bass.ds(HT * e, HT)], 1.0, None, ALU.mult).then_inc(s_b1_now, 1)

            dve.wait_ge(s_dtw, 2)
            next_bias(0, 0)
            next_bias(1, 1)
            dve.wait_ge(s_lgps, 1)
            lg3 = lg[:].rearrange("p t e -> p (t e)")
            dve_step(nc.vector.tensor_copy(lg3, ps[:, 4, 0:TILES * EXPERTS]))
            shape = [P, TILES, EXPERTS, EXPERTS]
            l_e = lg[:].unsqueeze(3).to_broadcast(shape)
            l_j = lg[:].unsqueeze(2).to_broadcast(shape)
            nc.vector.tensor_tensor(gt[:], l_j, l_e, ALU.is_gt)
            dve_step(nc.vector.tensor_tensor(eq[:], l_j, l_e, ALU.is_equal))
            dve_step(nc.vector.tensor_tensor(eq[:], eq[:], tri[:].unsqueeze(1).to_broadcast(shape), ALU.mult))
            dve_step(nc.vector.tensor_tensor(gt[:], gt[:], eq[:], ALU.add))
            dve_step(nc.vector.tensor_reduce(rank[:], gt[:], AX.X, ALU.add))
            nc.vector.tensor_reduce(top[:, 0], lg[:], AX.X, ALU.max)
            nc.vector.tensor_scalar(is01[:, 0], rank[:], 0.0, None, ALU.is_equal)
            dve_step(nc.vector.tensor_scalar(is01[:, 1], rank[:], 1.0, None, ALU.is_equal))
            dve_step(nc.vector.tensor_tensor(rank[:], lg[:], is01[:, 1], ALU.mult))
            dve_step(nc.vector.tensor_reduce(top[:, 1], rank[:], AX.X, ALU.add))
            nc.vector.tensor_tensor(top[:, 2], top[:, 1], top[:, 0], ALU.subtract).then_inc(s_diff, 1)
            dve.wait_ge(s_ediff, 1)
            dve_step(nc.vector.tensor_scalar(top[:, 4], top[:, 3], 1.0, None, ALU.add))
            dve_step(nc.vector.reciprocal(top[:, 4], top[:, 4]))
            dve_step(nc.vector.tensor_tensor(top[:, 5], top[:, 3], top[:, 4], ALU.mult))
            for n in range(2):
                ins = nc.vector.tensor_tensor(is01[:, n], is01[:, n], bc(top[:, 4 + n], EXPERTS), ALU.mult)
            dve_step(ins)
            nc.vector.tensor_tensor(comb[:], is01[:, 0], is01[:, 1], ALU.add).then_inc(s_comb, 1)

            def second_parts(k, u):
                m = UNITS * k + u
                for h in (0, 2):
                    dve.wait_ge(s_act_h, 2 * m + h // 2 + 1)
                    nc.vector.tensor_tensor(act_l[:, u % 2, h:h + 2], act_t[:, u % 2, h:h + 2],
                                            act_h[:, u % 2, h:h + 2].bitcast(F32), ALU.subtract).then_inc(s_act_l, 1)
                if u % CHUNKS == CHUNKS - 1:
                    next_bias(2 * k + 2 + u // CHUNKS, u // CHUNKS)

            def combine(k, u):
                m = UNITS * k + u
                e, c = divmod(u, CHUNKS)
                w = slice(c * BANK, (c + 1) * BANK)
                if c == 0:
                    dve.wait_ge(s_gate[e], 16 * (k + 1))
                dve.wait_ge(s_l2, m + 3)
                dve.wait_ge(s_moe, m + 2)
                nc.vector.tensor_tensor(term[:], ps[:, 4 + u % 2], gate[:, e, w], ALU.mult).then_inc(s_term, 1)
                dve.wait_ge(s_term, m + 1)
                nc.vector.tensor_tensor(acc[:, w], acc[:, w], term[:], ALU.add).then_inc(s_moe, 1)

            def add_experts(c):
                dve.wait_ge(s_back, c + 1)
                nc.vector.tensor_tensor(x[:, 4 * c:4 * c + 4, :], x[:, 4 * c:4 * c + 4, :],
                                        ps[:, 6 + c % 2].rearrange("p (t c) -> p t c", c=D), ALU.add).then_inc(s_final, 1)

            second_parts(0, 0)
            dve.sem_inc(s_moe, 2)
            dve.wait_ge(s_acc, CHUNKS)
            with dve.Fori(0, EXPERTS // 2 - 1) as k:
                for u in range(1, UNITS):
                    second_parts(k, u)
                    combine(k, u - 1)
                second_parts(k + 1, 0)
                combine(k, UNITS - 1)
            last = EXPERTS // 2 - 1
            for u in range(1, UNITS):
                second_parts(last, u)
                combine(last, u - 1)
                if u >= CHUNKS + 2:
                    add_experts(u - CHUNKS - 2)
            combine(last, UNITS - 1)
            for c in range(2, CHUNKS):
                add_experts(c)

        @block.tensor
        def _(pe):
            pe.wait_ge(s_const, 16 * N_CONST)
            for n, (w, order) in enumerate(((0, 0), (0, 1), (1, 0), (1, 1), (2, 2), (3, 2))):
                nc.tensor.matmul(ps[:, 4 + n // 4, (n % 4) * D:(n % 4 + 1) * D], w4[:, w, :],
                                 ident[:] if order == 2 else perm[:, order],
                                 start=True, stop=True, is_transpose=True)
            for n in range(2):
                mm = nc.tensor.matmul(ps[:, 5, 2 * D + 2 * n:2 * D + 2 * n + 2], perm[:, n], bqk[:], start=True, stop=True)
            mm.then_inc(s_wt_ps, 1)
            turn_pe(0, 0)
            turn_pe(0, 1)
            pe.wait_ge(s_wt, 3)
            for u in range(2 * CHUNKS):
                if u == CHUNKS - 1:
                    turn_pe(0, 2)
                    turn_pe(0, 3)
                c, kind = divmod(u, 2)
                pe.wait_ge(s_xt, c + 1)
                if u >= 2:
                    pe.wait_ge(s_rope_read, u - 1)
                for n in range(2):
                    mm = nc.tensor.matmul(ps[:, 4 + 2 * (u % 2) + n], wt[:, 2 * kind + n, :],
                                          xt[:, c * BANK:(c + 1) * BANK], start=True, stop=True)
                mm.then_inc(s_proj, 1)
            for g in range(4):
                pe.wait_ge(s_xt, 4)
                for j in range(4):
                    t = 4 * g + j
                    mm = nc.tensor.matmul(ps[:, g, j * P:(j + 1) * P], xt[:, t * P:(t + 1) * P], wt[:, 4, :],
                                          start=True, stop=True)
                mm.then_inc(s_v_ps, 1)

            def score_half(it, p, t, kk):
                half, h, q = t // 16, t % 16 // 4, t % 4
                if kk == 0 and not (isinstance(it, int) and it == 0 and t < 2):
                    pe.wait_ge(s_max, 32 * it + t - 1)
                mm = nc.tensor.matmul(ps[:, 2 * (t % 2) + kk], qs[p][:, half, h, q * P:(q + 1) * P],
                                      ks[p][:, kk, h, :], start=True, stop=True)
                if kk == 1:
                    mm.then_inc(s_score, 1)

            def one_pass(it, p, first, more, loads=None, between={}):
                for s in range(STEPS):
                    if s in between:
                        between[s]()
                    half, kt = divmod(s, KT)
                    if kt == 0:
                        pe.wait_ge(s_nrow[half], 64 * (it + 1))
                    if more and s == 0:
                        pe.wait_ge(s_qk[(p + 1) % SETS], LOADS * loads)
                    todo = [(MAX_TILES * s + n // 2, n % 2) for n in range(2 * MAX_TILES)] if more else []
                    for j in range(QUAD):
                        n = 4 * s + j
                        if n >= 3:
                            pe.wait_ge(s_exp, 4 * STEPS * it + n - 2)
                        nc.tensor.matmul(ps[:, 4 + (first + n) % 3], ks[p][:, kt // 4, j, kt % 4 * P:(kt % 4 + 1) * P],
                                         qs[p][:, half, j, :], start=True, stop=True).then_inc(s_st, 1)
                        for t, kk in todo[len(todo) * j // 4:len(todo) * (j + 1) // 4]:
                            score_half(it + 1, (p + 1) % SETS, t, kk)
                        if s >= 1 and j == (QUAD - 1 if more else QUAD - 2):
                            products(it, p, s - 1)
                products(it, p, STEPS - 1)

            def products(it, p, s):
                half, kt = divmod(s, KT)
                if s == 0:
                    pe.wait_ge(s_vq, it + 1)
                if kt == 0:
                    pe.wait_ge(s_o, 2 * it + half + 1)
                pe.wait_ge(s_exp, 4 * STEPS * it + 4 * s + 4)
                for j in range(QUAD):
                    mm = nc.tensor.matmul(ps[32 * j:32 * j + VW, 7], vq[p][:, kt, j, :], prob[:, (4 * s + j) % 8],
                                          start=(kt == 0), stop=(kt == KT - 1))
                mm.then_inc(s_pv, 1)

            pe.wait_ge(s_qk[0], LOADS)
            pe.wait_ge(s_v, 4)
            for t in range(32):
                score_half(0, 0, t, 0)
                score_half(0, 0, t, 1)
            with pe.Fori(0, PASSES // SETS) as r:
                for p in range(SETS):
                    one_pass(SETS * r + p, p, 4 * STEPS * p, True, r + 1 + (p + 1) // SETS)
            one_pass(PASSES - 2, 0, 0, True, PASSES // SETS + 1)

            def project_out(b):
                pe.wait_ge(s_att, b + 1)
                if b:
                    pe.wait_ge(s_exp, 4 * STEPS * PASSES)
                for g in (2 * b, 2 * b + 1):
                    for j in range(4):
                        t = 4 * g + j
                        mm = nc.tensor.matmul(ps[:, 4 * b + g % 2, j * P:(j + 1) * P], num[:, t * P:(t + 1) * P], wt[:, 5, :],
                                              start=True, stop=True)
                    mm.then_inc(s_y, 1)

            def turn_weights():
                pe.wait_ge(s_quant, 1)
                pe.wait_ge(s_res, 2)
                for n in range(2):
                    for j in range(3):
                        rows = min(P, FFN - j * P)
                        nc.tensor.transpose(ps[:, 1 + n, j * P:j * P + rows], wfq[0:rows, (3 * n + j) * D:(3 * n + j + 1) * D],
                                            ident[0:rows, 0:rows])
                for j in range(3):
                    rows = min(P, FFN - j * P)
                    mm = nc.tensor.transpose(ps[0:rows, 3, j * D:(j + 1) * D], wfq[:, 6 * D + j * P:6 * D + j * P + rows], ident[:])
                mm.then_inc(s_wft_ps, 1)

            def turn_x(g, bank):
                for j in range(4):
                    mm = nc.tensor.transpose(ps[:, bank, j * P:(j + 1) * P], sq[:, 4 * g + j, :], ident[:])
                mm.then_inc(s_turned, 1)

            def gate_up(g):
                for t in range(4 * g, 4 * g + 4):
                    pe.wait_ge(s_xt, 4 + (2 if g < 2 else g + 1))
                    if t >= 2:
                        pe.wait_ge(s_hid, t - 1)
                    for n in range(2):
                        mm = nc.tensor.matmul(ps[:, 2 * (t % 2) + n, 0:FFN], xt[:, t * P:(t + 1) * P], wgu_t[:, n, :],
                                              start=True, stop=True)
                    mm.then_inc(s_gu, 1)

            def turn_hidden(g):
                pe.wait_ge(s_quant, HID_PIECE[g] + 1)
                for j in range(3):
                    rows = min(P, FFN - j * P)
                    if g:
                        pe.wait_ge(s_ht, 3 * g - 3 + j + 1)
                    for t in range(4):
                        mm = nc.tensor.transpose(ps[0:rows, 4 + j, t * P:(t + 1) * P],
                                                 hid_q[:, g % 2, t * FFN + j * P:t * FFN + j * P + rows], ident[:])
                    mm.then_inc(s_ht_ps, 1)

            def down(g):
                pe.wait_ge(s_ht, 3 * g + 3)
                if g:
                    pe.wait_ge(s_res, 4 + g)
                else:
                    pe.wait_ge(s_o, 2 * PASSES + 1)
                for t in range(4):
                    for j in range(3):
                        rows = min(P, FFN - j * P)
                        mm = nc.tensor.matmul(ps[:, 7, t * D:(t + 1) * D], hid_t[0:rows, j, t * P:(t + 1) * P],
                                              wd_t[0:rows, j, :], start=(j == 0), stop=(j == 2))
                mm.then_inc(s_down, 1)

            one_pass(PASSES - 1, 1, 4 * STEPS, False, between={1: lambda: project_out(0), 13: turn_weights})
            pe.wait_ge(s_quant, 2)
            turn_x(0, 0)
            pe.wait_ge(s_wft, 3)
            turn_x(1, 1)
            gate_up(0)
            project_out(1)
            gate_up(1)
            pe.wait_ge(s_res, 4)
            turn_hidden(0)
            down(0)
            pe.wait_ge(s_quant, 4)
            turn_x(2, 4)
            turn_x(3, 5)
            gate_up(2)
            gate_up(3)
            turn_hidden(1)
            down(1)
            turn_hidden(2)
            down(2)
            turn_hidden(3)
            down(3)

            pe.wait_ge(s_w34, 16 * N_W34)
            pe.wait_ge(s_ht, 12)
            nc.tensor.transpose(ps[:, 4, 0:D], wdt[:], ident[:])
            for n in range(2):
                nc.tensor.transpose(ps[:, 4, (n + 1) * D:(n + 2) * D], wbc[:, n], ident[:])
            nc.tensor.transpose(ps[:, 4, 3 * D:3 * D + EXPERTS * HT], b1r[:],
                                ident[0:EXPERTS * HT, 0:EXPERTS * HT]).then_inc(s_dtw_ps, 1)
            for g in range(4):
                turn_pe(2, g)
            pe.wait_ge(s_dtw, 2)
            pe.wait_ge(s_res, 8)
            for c in range(CHUNKS):
                pe.wait_ge(s_xt, 8 + c + 1)
                for n in range(3):
                    if c:
                        pe.wait_ge(s_z, 3 * (c - 1) + n + 1)
                    nc.tensor.matmul(ps[:, 5 + n], ssm_t[:, n], xt[:, c * BANK:(c + 1) * BANK],
                                     start=True, stop=True).then_inc(s_zps, 1)

            def rows(b, n, slot):
                m = NSTATE * b + n
                first = isinstance(m, int) and m < 2
                pick = sel_b[:, bass.ds(n, 1)].to_broadcast([P, P])
                if not first:
                    pe.wait_ge(s_dbx, m - 1)
                for k in range(2):
                    mm = nc.tensor.matmul(ps[:, 2 * (slot % 2) + k], pick, bcp[:, 0, b * SEQ + k * BANK:b * SEQ + (k + 1) * BANK],
                                          start=True, stop=True)
                mm.then_inc(s_bb, 1)
                if not (isinstance(m, int) and m < 1):
                    pe.wait_ge(s_cs, m)
                for k in range(2):
                    mm = nc.tensor.matmul(ps[:, 4 + k], pick, bcp[:, 1, b * SEQ + k * BANK:b * SEQ + (k + 1) * BANK],
                                          start=True, stop=True)
                mm.then_inc(s_cb, 1)

            def total(b, n, slot):
                m = NSTATE * b + n
                first = isinstance(n, int) and n == 0
                last = isinstance(n, int) and n == NSTATE - 1
                pe.wait_ge(s_hc, m + 1)
                if first and b:
                    pe.wait_ge(s_skip, b)
                for k in range(2):
                    mm = nc.tensor.matmul(ps[:, 6 + k], ident[:], hc[:, slot, k * BANK:(k + 1) * BANK], start=first, stop=last)
                mm.then_inc(s_y3, 1)

            pe.wait_ge(s_selb, 1)
            pe.wait_ge(s_bp3, 2 * BATCH)
            pe.wait_ge(s_z, 3 * CHUNKS)
            LAG = RING - 1
            for b in range(BATCH):
                for n in range(RING):
                    rows(b, n, n)
                    if b and n < LAG:
                        total(b - 1, NSTATE - LAG + n, (n + 1) % RING)
                total(b, 0, 0)
                with pe.Fori(1, NSTATE // RING) as k:
                    for n in range(RING):
                        rows(b, RING * k + n, n)
                        total(b, RING * k + n - LAG, (n + 1) % RING)
            for n in range(LAG):
                total(BATCH - 1, NSTATE - LAG + n, (n + 1) % RING)
            pe.wait_ge(s_dbx, BATCH * NSTATE)
            for g in range(4):
                pe.wait_ge(s_skip, g // 2 + 1)
                for j in range(4):
                    t = 4 * g + j
                    mm = nc.tensor.transpose(ps[:, g, j * P:(j + 1) * P], zt[:, t * P:(t + 1) * P], ident[:])
                mm.then_inc(s_yt, 1)

            for g in range(4):
                turn_pe(3, g)
            pe.wait_ge(s_cs, BATCH * NSTATE)
            for t in range(TILES):
                pe.wait_ge(s_xt, 12 + t // 4 + 1)
                mm = nc.tensor.matmul(ps[:, 4, t * EXPERTS:(t + 1) * EXPERTS], xt[:, t * P:(t + 1) * P], wgate[:],
                                      start=True, stop=True)
            mm.then_inc(s_lgps, 1)

            def split_product(dst, w_h, w_l, r_h, r_l, start, stop):
                nc.tensor.matmul(dst, w_l, r_h, start=start, stop=False)
                nc.tensor.matmul(dst, w_h, r_l, start=False, stop=False)
                return nc.tensor.matmul(dst, w_h, r_h, start=False, stop=stop)

            def first_product(k, u):
                m = UNITS * k + u
                e, c = divmod(u, CHUNKS)
                w = slice(c * BANK, (c + 1) * BANK)
                if c == 0:
                    pe.wait_ge(s_w_l, 2 * k + e + 1)
                for h in range(HT):
                    pe.wait_ge(s_gelu, HT * m + h + 1)
                    cols = slice(h * P, (h + 1) * P)
                    split_product(ps[:, h], w12_h[:, e, 0, cols], w12_l[:, e, 0, cols], xh[:, w], xl[:, w],
                                  True, True).then_inc(s_l1, 1)

            def second_product(k, u):
                m = UNITS * k + u
                e = u // CHUNKS
                pe.wait_ge(s_moe, m + 1)
                for h in range(HT):
                    if h % 2 == 0:
                        pe.wait_ge(s_act_l, 2 * m + h // 2 + 1)
                    cols = slice(h * D, (h + 1) * D)
                    mm = split_product(ps[:, 4 + u % 2], w12_h[:, e, 1, cols], w12_l[:, e, 1, cols],
                                       act_h[:, u % 2, h], act_l[:, u % 2, h], h == 0, h == HT - 1)
                mm.then_inc(s_l2, 1)

            def turn_back(c):
                pe.wait_ge(s_moe, 2 + UNITS * (EXPERTS // 2) - CHUNKS + c + 1)
                if c >= 2:
                    pe.wait_ge(s_final, c - 1)
                for j in range(4):
                    mm = nc.tensor.transpose(ps[:, 6 + c % 2, j * P:(j + 1) * P], acc[:, c * BANK + j * P:c * BANK + (j + 1) * P], ident[:])
                mm.then_inc(s_back, 1)

            pe.sem_inc(s_l2, 2)
            pe.wait_ge(s_xh, CHUNKS)
            pe.wait_ge(s_xl, CHUNKS)
            first_product(0, 0)
            pe.wait_ge(s_comb, 1)
            for t in range(TILES):
                mm = nc.tensor.transpose(ps[0:EXPERTS, 4 + t // 4, (t % 4) * P:(t % 4 + 1) * P], comb[:, t, :], ident[:])
            mm.then_inc(s_combt_ps, 1)
            pe.wait_ge(s_combt, 1)
            for c in range(CHUNKS):
                nc.tensor.matmul(ps[:, 4 + c], b2[:], comb_t[:, c * BANK:(c + 1) * BANK], start=True, stop=True).then_inc(s_b2, 1)
            pe.wait_ge(s_acc, CHUNKS)
            with pe.Fori(0, EXPERTS // 2 - 1) as k:
                for u in range(1, UNITS):
                    first_product(k, u)
                    second_product(k, u - 1)
                first_product(k + 1, 0)
                second_product(k, UNITS - 1)
            last = EXPERTS // 2 - 1
            for u in range(1, UNITS):
                first_product(last, u)
                second_product(last, u - 1)
                if u >= CHUNKS + 2:
                    turn_back(u - CHUNKS - 2)
            second_product(last, UNITS - 1)
            for c in range(2, CHUNKS):
                turn_back(c)


def constants():
    f32 = np.float32
    inv = f32(1.0) / np.power(f32(10000.0), np.arange(0, HD, 2, dtype=f32) / f32(HD)).astype(f32)
    ang = (np.arange(SEQ, dtype=f32)[:, None] * inv[None, :]).astype(f32).astype(np.float64)
    ang = np.concatenate([ang, ang], axis=-1).T
    sign = np.where(np.arange(HD) % 2 == 0, -1.0, 1.0)[:, None]
    order = np.arange(P).reshape(HEADS // QUAD, QUAD, HD).transpose(0, 2, 1).ravel()
    perm = np.zeros((2, P, P), f32)
    perm[0, order, np.arange(P)] = 1
    perm[1, order ^ 1, np.arange(P)] = 1
    sel = np.zeros((P, NSTATE), f32)
    for part in (0, 64, 96):
        sel[part + np.arange(NSTATE), np.arange(NSTATE)] = 1
    tri = np.tril(np.ones((EXPERTS, EXPERTS), f32), -1)
    return {
        "ident": np.eye(P, dtype=f32),
        "perm": perm,
        "sel": sel,
        "tri": np.broadcast_to(tri, (P, EXPERTS, EXPERTS)).copy(),
        "cos": np.tile(np.cos(ang), (HEADS, 1)).astype(f32)[order],
        "sin": np.tile(np.sin(ang) * sign, (HEADS, 1)).astype(f32)[order],
    }


def kernel(**inputs):
    import concourse.bacc as bacc
    from concourse.bass_utils import run_bass_kernel_spmd

    nc = bacc.Bacc("TRN2", target_bir_lowering=False, num_devices=1)
    arrays, aps = {}, {}
    for name, a in {**inputs, **constants()}.items():
        a = np.ascontiguousarray(a)
        arrays["in_" + name] = a
        aps[name] = nc.dram_tensor("in_" + name, a.shape, mybir.dt.from_np(a.dtype), kind="ExternalInput").ap()
    out = nc.dram_tensor("out_x", (BATCH, SEQ, D), F32, kind="ExternalOutput").ap()
    build_kernel(nc, aps, out)
    r = run_bass_kernel_spmd(nc, [arrays], core_ids=[0])
    return r.results[0]["out_x"]
```

```python
from contextlib import ExitStack

import numpy as np

import concourse.bass as bass
from concourse import mybir

F32 = mybir.dt.float32
BF16 = mybir.dt.bfloat16
F32R = mybir.dt.float32r
ALU = mybir.AluOpType
ACT = mybir.ActivationFunctionType
AX = mybir.AxisListType

P = 128
BATCH = 2
SEQ = 1024
TOKENS = BATCH * SEQ
D = 128
TILES = TOKENS // P
BANK = 512
CHUNKS = TOKENS // BANK
EPS = 1e-5

HEADS = 16
HD = D // HEADS
QUAD = 4
PASSES = BATCH * HEADS // QUAD
QC = QUAD * HD
KT = SEQ // P
PARTS = 3
PROD = PARTS * PARTS * HD
ROWS = 96
ATT_SCALE = 1.0 / float(np.sqrt(np.float32(HD)))
VW = 16
STEPS = 2 * KT
MAX_TILES = 2
SETS = 3

MIDS = [0.25, 0.75, 1.25, 1.75, 2.5, 3.5, 5.0]
HELPED = 3
JUMPS = [0.5, 0.5, 0.5, 0.5, 1.0, 1.0, 2.0]
FFN = 352
PEEL = 8
RING = 4
QB = 16
NSTATE = 32
EXPERTS = 8
HIDDEN = 512
HT = HIDDEN // P
UNITS = 2 * CHUNKS

WF = 6 * D + FFN
QMAX = 4 * FFN


def build_kernel(nc, i, out):
    ctx = ExitStack()

    def sb(name, shape, dt=F32):
        return ctx.enter_context(nc.sbuf_tensor(name, shape, dt))

    def sem(name):
        return ctx.enter_context(nc.semaphore(name))

    with ctx:
        ps = ctx.enter_context(nc.psum_tensor("ps", [P, 8, BANK], F32))

        x = sb("x", [P, TILES, D])
        xc = sb("xc", [P, TILES, D])
        sq = sb("sq", [P, TILES, D])
        xt = sb("xt", [P, TOKENS])
        ident = sb("ident", [P, P])
        stat = sb("stat", [P, 4, TILES])

        zero = sb("zero", [P, 2])
        borders = sb("borders", [P, 2])
        expo = sb("expo", [P, TILES])

        wf = sb("wf", [P, WF])
        wfq = sb("wfq", [P, WF])
        wgu_t = sb("wgu_t", [P, 2, FFN])
        wd_t = sb("wd_t", [P, 3, D])

        wdt = sb("wdt", [P, D])
        wbc = sb("wbc", [P, 2, D])
        cols = sb("cols", [P, 4])
        log_a = sb("log_a", [P, NSTATE])
        sel = sb("sel", [P, NSTATE])
        sel_b = sb("sel_b", [P, NSTATE], BF16)
        wgate = sb("wgate", [P, EXPERTS])
        b1r = sb("b1r", [EXPERTS * HT, P])
        b2 = sb("b2", [EXPERTS, D])
        tri = sb("tri", [P, EXPERTS, EXPERTS])
        ssm_t = sb("ssm_t", [P, 3, D])
        b1t = sb("b1t", [P, (EXPERTS + 2) * HT])
        b1_now = sb("b1_now", [P, 2, HT])

        phase = ExitStack()

        def sb(name, shape, dt=F32):
            return phase.enter_context(nc.sbuf_tensor(name, shape, dt))

        w4 = sb("w4", [P, 4, D])
        perm = sb("perm", [P, 2, P])
        cos = sb("cos", [P, SEQ])
        sin = sb("sin", [P, SEQ])
        rot = sb("rot", [P, 2, 3, BANK])
        rest = sb("rest", [P, 2, BANK])
        parts = sb("parts", [P, CHUNKS, PARTS, BANK], BF16)
        fill = sb("fill", [4 * (ROWS - PROD), 2, 2 * BANK], BF16)
        stacks = [[sb(f"{w}{n}", [ROWS, 2, QUAD, BANK], BF16) for w in ("qs", "ks")] for n in reversed(range(SETS))][::-1]
        qs, ks = ([pair[n] for pair in stacks] for n in range(2))
        prob = sb("prob", [P, 8, BANK])
        vq = [sb(f"vq{n}", [P, KT, QUAD, VW]) for n in range(SETS)]
        v = sb("v", [P, PASSES, KT, QC])
        wt = sb("wt", [P, 6, D])
        bqk = sb("bqk", [P, 2])
        bperm = sb("bperm", [P, 2, 2])
        bv_all = sb("bv_all", [P, D])
        bo_all = sb("bo_all", [P, D])
        nmax = sb("nmax", [P, 2, 16])
        nmax_p = sb("nmax_p", [P, 32], BF16)
        nmax_t = sb("nmax_t", [P, 2, 32], BF16)
        o_sb = sb("o_sb", [P, 2, BANK])
        den = sb("den", [P, BATCH, HEADS * SEQ // P])
        rden = sb("rden", [P, BATCH, SEQ])
        num = sb("num", [P, TOKENS])
        phase.close()

        fa = sb("fa", [P, 2, QMAX])
        fx = sb("fx", [P, 2, QMAX])
        fs = sb("fs", [P, 2, QMAX], BF16)
        fg = sb("fg", [P, 4, QMAX], BF16)
        fg_high = sb("fg_high", [P, 2, 3, QMAX], BF16)
        fblk = sb("fblk", [P, 2, 3, QMAX // QB])
        silu = sb("silu", [P, 2, FFN])
        hid = sb("hid", [P, 2, 4 * FFN])
        hid_q = sb("hid_q", [P, 2, 4 * FFN])
        hid_t = sb("hid_t", [P, 3, BANK])
        phase.close()

        abar = sb("abar", [P, RING, SEQ])
        dbx = sb("dbx", [P, RING, SEQ])
        hst = sb("hst", [P, RING, SEQ])
        cbr = sb("cbr", [P, RING, SEQ])
        hc = sb("hc", [P, RING, SEQ])
        ln_u = sb("ln_u", [P, SEQ])
        a_neg = sb("a_neg", [P, NSTATE])
        dt = sb("dt", [P, TOKENS])
        dtx = sb("dtx", [P, TOKENS])
        zt = sb("zt", [P, TOKENS])
        bc32 = sb("bc32", [P, 2, TOKENS])
        bcp = sb("bcp", [P, 2, TOKENS], BF16)
        phase.close()

        w12 = [t[:, 0:2 * HIDDEN].rearrange("p (m c) -> p m c", c=HIDDEN) for t in (wf, wfq)]
        w12_h = sb("w12_h", [P, 2, 2, HIDDEN], F32R)
        w12_l = sb("w12_l", [P, 2, 2, HIDDEN], F32R)
        xh = sb("xh", [P, TOKENS], F32R)
        xl = sb("xl", [P, TOKENS], F32R)
        act_t = sb("act_t", [P, 2, HT, BANK])
        act_h = sb("act_h", [P, 2, HT, BANK], F32R)
        act_l = sb("act_l", [P, 2, HT, BANK], F32R)
        gate = sb("gate", [P, 2, TOKENS])
        term = sb("term", [P, BANK])
        acc = sb("acc", [P, TOKENS])
        lg = sb("lg", [P, TILES, EXPERTS])
        gt = sb("gt", [P, TILES, EXPERTS, EXPERTS])
        eq = sb("eq", [P, TILES, EXPERTS, EXPERTS])
        rank = sb("rank", [P, TILES, EXPERTS])
        is01 = sb("is01", [P, 2, TILES, EXPERTS])
        top = sb("top", [P, 6, TILES])
        comb = sb("comb", [P, TILES, EXPERTS])
        comb_t = sb("comb_t", [EXPERTS, TOKENS])
        phase.close()

        q_dram = nc.dram_tensor("q_dram", (PASSES, 2, PARTS, QC, BANK), BF16, kind="Internal").ap()
        k_dram = nc.dram_tensor("k_dram", (PASSES, 2, PARTS, QC, BANK), BF16, kind="Internal").ap()
        o_dram = nc.dram_tensor("o_dram", (PASSES, P, SEQ), F32, kind="Internal").ap()
        c_dram = nc.dram_tensor("c_dram", (EXPERTS, TOKENS), F32, kind="Internal").ap()
        r_dram = nc.dram_tensor("r_dram", (BATCH, HEADS, SEQ), F32, kind="Internal").ap()

        s_x = [sem(f"s_x{n}") for n in range(2)]
        s_const = sem("s_const")
        s_centred = sem("s_centred")
        s_squared = sem("s_squared")
        s_var = sem("s_var")
        s_rstd = sem("s_rstd")
        s_normed = sem("s_normed")
        s_turned = sem("s_turned")
        s_xt = sem("s_xt")
        s_v1 = sem("s_v1")
        s_p1 = sem("s_p1")
        s_wt_ps = sem("s_wt_ps")
        s_wt = sem("s_wt")
        s_proj = sem("s_proj")
        s_rope_read = sem("s_rope_read")
        s_rope = sem("s_rope")
        s_part1 = sem("s_part1")
        s_rest = sem("s_rest")
        s_part2 = sem("s_part2")
        s_part3 = sem("s_part3")
        s_parts_out = [sem(f"s_parts_out{n}") for n in range(CHUNKS)]
        s_v_ps = sem("s_v_ps")
        s_v = sem("s_v")
        s_fill = sem("s_fill")
        s_set = sem("s_set")
        s_qk = [sem(f"s_qk{n}") for n in range(SETS)]
        s_score = sem("s_score")
        s_max = sem("s_max")
        s_nmax = sem("s_nmax")
        s_nrow = [sem(f"s_nrow{n}") for n in range(2)]
        s_st = sem("s_st")
        s_exp = sem("s_exp")
        s_pv = sem("s_pv")
        s_o = sem("s_o")
        s_o_out = [sem(f"s_o_out{n}") for n in range(2)]
        s_vq = sem("s_vq")
        s_od = [sem(f"s_od{n}") for n in range(2)]
        s_num = sem("s_num")
        s_rden = sem("s_rden")
        s_ready = sem("s_ready")
        s_att = sem("s_att")
        s_y = sem("s_y")
        s_res = sem("s_res")
        s_out = sem("s_out")
        s_wf = sem("s_wf")
        s_wfz = sem("s_wfz")
        s_high_act = sem("s_high_act")
        s_high_pool = sem("s_high_pool")
        s_border = sem("s_border")
        s_blk = sem("s_blk")
        s_ss = sem("s_ss")
        s_qx = sem("s_qx")
        s_qa = sem("s_qa")
        s_quant = sem("s_quant")
        s_wft_ps = sem("s_wft_ps")
        s_wft = sem("s_wft")
        s_gu = sem("s_gu")
        s_silu = sem("s_silu")
        s_hid = sem("s_hid")
        s_ht_ps = sem("s_ht_ps")
        s_ht = sem("s_ht")
        s_down = sem("s_down")
        s_skip = sem("s_skip")
        s_b1_now = sem("s_b1_now")
        s_w12 = [sem(f"s_w12_{n}") for n in range(2)]
        s_w34 = sem("s_w34")
        s_dtw_ps = sem("s_dtw_ps")
        s_dtw = sem("s_dtw")
        s_zps = sem("s_zps")
        s_z = sem("s_z")
        s_e = sem("s_e")
        s_u = sem("s_u")
        s_ln = sem("s_ln")
        s_dt = sem("s_dt")
        s_bp = sem("s_bp")
        s_bp2 = sem("s_bp2")
        s_bp3 = [sem(f"s_bp3_{n}") for n in range(2)]
        s_rest3 = [sem(f"s_rest3_{n}") for n in range(2)]
        s_bc = sem("s_bc")
        s_a = sem("s_a")
        s_abar = sem("s_abar")
        s_bb = sem("s_bb")
        s_cb = sem("s_cb")
        s_dbx = sem("s_dbx")
        s_scan = sem("s_scan")
        s_cs = sem("s_cs")
        s_hc = sem("s_hc")
        s_y3 = sem("s_y3")
        s_yt = sem("s_yt")
        s_selb = sem("s_selb")
        s_lgps = sem("s_lgps")
        s_diff = sem("s_diff")
        s_ediff = sem("s_ediff")
        s_comb = sem("s_comb")
        s_combt_ps = sem("s_combt_ps")
        s_combt = sem("s_combt")
        s_b2 = sem("s_b2")
        s_l1 = sem("s_l1")
        s_gelu = sem("s_gelu")
        s_l2 = sem("s_l2")
        s_moe = sem("s_moe")
        s_acc = sem("s_acc")
        s_mstep = sem("s_mstep")
        s_xh = sem("s_xh")
        s_xl = sem("s_xl")
        s_w_h = sem("s_w_h")
        s_w_l = sem("s_w_l")
        s_act_h = sem("s_act_h")
        s_act_l = sem("s_act_l")
        s_term = sem("s_term")
        s_comb_out = sem("s_comb_out")
        s_gate = [sem(f"s_gate{n}") for n in range(2)]
        s_back = sem("s_back")
        s_final = sem("s_final")

        block = ctx.enter_context(nc.Block())

        count = {"dve": 0, "pool": 0}

        def dve_step(ins):
            count["dve"] += 1
            ins.then_inc(s_v1, 1)
            nc.vector.wait_ge(s_v1, count["dve"])

        def pool_step(ins):
            count["pool"] += 1
            ins.then_inc(s_p1, 1)
            nc.gpsimd.wait_ge(s_p1, count["pool"])

        def bc(ap2, n):
            return ap2.unsqueeze(2).to_broadcast([ap2.shape[0], ap2.shape[1], n])

        def norm_dve_a(k, h):
            a, b = h * TILES // 2, (h + 1) * TILES // 2
            dve_step(nc.vector.tensor_reduce(stat[:, 0, a:b], x[:, a:b, :], AX.X, ALU.add))
            dve_step(nc.vector.tensor_scalar(stat[:, 1, a:b], stat[:, 0, a:b], 1.0 / D, None, ALU.mult))
            if k:
                nc.vector.wait_ge(s_turned, 4 * k)
            nc.vector.tensor_tensor(xc[:, a:b, :], x[:, a:b, :], bc(stat[:, 1, a:b], D),
                                    ALU.subtract).then_inc(s_centred, 1)

        def norm_dve_var(k, h):
            a, b = h * TILES // 2, (h + 1) * TILES // 2
            nc.vector.wait_ge(s_squared, 2 * k + h + 1)
            nc.vector.tensor_reduce(stat[:, 2, a:b], sq[:, a:b, :], AX.X, ALU.add).then_inc(s_var, 1)

        def norm_dve_scale(k, h):
            a, b = h * TILES // 2, (h + 1) * TILES // 2
            u = 2 * k + h
            nc.vector.wait_ge(s_rstd, u + 1)
            nc.vector.wait_ge(s_centred, u + 1)
            nc.vector.tensor_tensor(xc[:, a:b, :], xc[:, a:b, :], bc(stat[:, 3, a:b], D),
                                    ALU.mult).then_inc(s_normed, 1)

        def norm_dve_b(k, h):
            norm_dve_var(k, h)
            norm_dve_scale(k, h)

        def norm_act(k, h):
            a, b = h * TILES // 2, (h + 1) * TILES // 2
            u = 2 * k + h
            nc.scalar.wait_ge(s_centred, u + 1)
            if k:
                nc.scalar.wait_ge(s_var, u - 1)
            if k == 2:
                nc.scalar.wait_ge(s_turned, 8)
            nc.scalar.activation(sq[:, a:b, :], xc[:, a:b, :], ACT.Square).then_inc(s_squared, 1)

        def norm_pool(k, h):
            a, b = h * TILES // 2, (h + 1) * TILES // 2
            u = 2 * k + h
            nc.gpsimd.wait_ge(s_var, u + 1)
            if k:
                nc.gpsimd.wait_ge(s_normed, u - 1)
            pool_step(nc.gpsimd.tensor_scalar(stat[:, 3, a:b], stat[:, 2, a:b], 1.0 / D, EPS, ALU.mult, ALU.add))
            nc.gpsimd.tensor_tensor(stat[:, 3, a:b], stat[:, 3, a:b], expo[:, a:b], ALU.pow).then_inc(s_rstd, 1)

        def turn_pe(k, g, bank=None):
            bank = g if bank is None else bank
            nc.tensor.wait_ge(s_normed, 2 * k + g // 2 + 1)
            if k:
                nc.tensor.wait_ge(s_xt, 4 * (k - 1) + g + 1)
            for j in range(4):
                mm = nc.tensor.transpose(ps[:, bank, j * P:(j + 1) * P], xc[:, 4 * g + j, :], ident[:])
            mm.then_inc(s_turned, 1)

        def turn_act(k, g, bank=None):
            bank = g if bank is None else bank
            nc.scalar.wait_ge(s_turned, 4 * k + g + 1)
            if k == 2:
                nc.scalar.wait_ge(s_gu, TILES)
            if k == 3:
                nc.scalar.wait_ge(s_skip, BATCH)
            nc.scalar.activation(xt[:, g * BANK:(g + 1) * BANK], ps[:, bank, :], ACT.Copy).then_inc(s_xt, 1)

        X_PIECE = (1, 3)
        HID_PIECE = (2, 4, 5, 6)

        def blocks(ap):
            return ap.rearrange("p (b k) -> p b k", k=QB)

        def x_half(t, h):
            return t[:, 8 * h:8 * h + 8, :].rearrange("p t c -> p (t c)")

        def quant_scale(n, src, ready=None):
            w = src.shape[1]
            blk = fblk[:, n % 2, :, 0:w // QB]
            if ready:
                nc.vector.wait_ge(*ready)
            if n >= 2:
                nc.vector.wait_ge(s_quant, n - 1)
            dve_step(nc.vector.tensor_reduce(blk[:, 0], blocks(src), AX.X, ALU.max, apply_absolute_value=True))
            dve_step(nc.vector.tensor_scalar(blk[:, 1], blk[:, 0], 1.0 / 6.0, 1e-12, ALU.mult, ALU.max))
            nc.vector.reciprocal(blk[:, 2], blk[:, 1]).then_inc(s_blk, 1)

        def quant_pool(n, src):
            w = src.shape[1]
            nc.gpsimd.wait_ge(s_blk, n + 1)
            if n >= 2:
                nc.gpsimd.wait_ge(s_quant, n - 1)
            nc.gpsimd.tensor_tensor(blocks(fx[:, n % 2, 0:w]), blocks(src), bc(fblk[:, n % 2, 2, 0:w // QB], QB),
                                    ALU.mult).then_inc(s_qx, 1)
            nc.gpsimd.wait_ge(s_qa, 2 * (n + 1))
            if n >= HELPED:
                nc.gpsimd.wait_ge(s_qx, n + 1)
                nc.gpsimd.tensor_scalar(fg_high[:, n % 2, 0, 0:w], fa[:, n % 2, 0:w], MIDS[4], JUMPS[4], ALU.is_gt,
                                        ALU.mult).then_inc(s_high_pool, 1)
                nc.gpsimd.wait_ge(s_high_pool, n - HELPED + 1)
            nc.gpsimd.tensor_tensor(blocks(fx[:, n % 2, 0:w]), blocks(fs[:, n % 2, 0:w]),
                                    bc(fblk[:, n % 2, 1, 0:w // QB], QB), ALU.mult).then_inc(s_ss, 1)

        def quant_act(n, w):
            nc.scalar.wait_ge(s_qx, n + 1)
            if n >= 2:
                nc.scalar.wait_ge(s_quant, n - 1)
                nc.scalar.wait_ge(s_ss, n - 1)
            nc.scalar.activation(fa[:, n % 2, 0:w], fx[:, n % 2, 0:w], ACT.Abs).then_inc(s_qa, 1)
            nc.scalar.activation(fs[:, n % 2, 0:w], fx[:, n % 2, 0:w], ACT.Sign).then_inc(s_qa, 1)

        def borders_act(n, w):
            nc.scalar.wait_ge(s_qa, 2 * (n + 1))
            for m in range(2):
                high = fg_high[:, n % 2, 1 + m, 0:w]
                nc.scalar.activation(high, fa[:, n % 2, 0:w], ACT.Sign, bias=borders[:, m:m + 1]).then_inc(s_border, 1)
                nc.scalar.wait_ge(s_border, 2 * (n - HELPED) + m + 1)
                nc.scalar.activation(high, high, ACT.Relu, scale=JUMPS[5 + m]).then_inc(s_high_act, 1)

        def quant_grid(n, dst, free=None, between=None, before_last=None):
            w = dst.shape[1]
            a = fa[:, n % 2, 0:w]
            g = [fg[:, m, 0:w] for m in range(4)] + [fg_high[:, n % 2, m, 0:w] for m in range(3)]
            nc.vector.wait_ge(s_qa, 2 * (n + 1))
            if n:
                nc.vector.wait_ge(s_quant, n)
            for m in range(7 if n < HELPED else 4):
                ins = nc.vector.tensor_scalar(g[m], a, MIDS[m], JUMPS[m], ALU.is_gt, ALU.mult)
            dve_step(ins)
            if between:
                between()
            if n >= HELPED:
                nc.vector.wait_ge(s_high_act, 2 * (n - HELPED + 1))
            for m in (0, 2, 5):
                ins = nc.vector.tensor_tensor(g[m], g[m], g[m + 1], ALU.add)
            dve_step(ins)
            dve_step(nc.vector.tensor_tensor(g[0], g[0], g[2], ALU.add))
            dve_step(nc.vector.tensor_tensor(g[0], g[0], g[5], ALU.add))
            if n >= HELPED:
                nc.vector.wait_ge(s_high_pool, n - HELPED + 1)
            dve_step(nc.vector.tensor_tensor(g[0], g[0], g[4], ALU.add))
            if before_last:
                before_last()
            if free:
                nc.vector.wait_ge(*free)
            nc.vector.wait_ge(s_ss, n + 1)
            nc.vector.tensor_tensor(dst, g[0], fx[:, n % 2, 0:w], ALU.mult).then_inc(s_quant, 1)

        N_CONST = 6 + 4 + 2
        N_W34 = 3 + 16 + 6

        LOADS = 16 * (2 * (PARTS + 1) + 1)

        @block.sync
        def _(sp):
            xv = i["L0_attn_x"].rearrange("b (t p) c -> p (b t) c", p=P)
            for h in range(2):
                sp.dma_start(x[:, 8 * h:8 * h + 8, :], xv[:, 8 * h:8 * h + 8, :]).then_inc(s_x[h], 16)
            sp.dma_start(ident[:], i["ident"]).then_inc(s_const, 16)
            for n, w in enumerate(("Wq", "Wk", "Wv", "Wo")):
                sp.dma_start(w4[:, n, :], i["L0_attn_" + w]).then_inc(s_const, 16)
            sp.dma_start(perm[:], i["perm"].rearrange("n p c -> p n c")).then_inc(s_const, 16)
            for n, b in enumerate(("bq", "bk")):
                sp.dma_start(bqk[:, n:n + 1], i["L0_attn_" + b].rearrange("(p o) -> p o", o=1)).then_inc(s_const, 16)
            sp.dma_start(cos[:], i["cos"]).then_inc(s_const, 16)
            sp.dma_start(sin[:], i["sin"]).then_inc(s_const, 16)
            for b, t in (("bv", bv_all), ("bo", bo_all)):
                sp.dma_start(t[:], i["L0_attn_" + b].rearrange("(o c) -> o c", o=1).to_broadcast([P, D])).then_inc(s_const, 16)

            sp.wait_ge(s_fill, 1)
            for n in range(SETS):
                for k, t in enumerate((qs[n], ks[n])):
                    sp.dma_start(t[PROD:ROWS].rearrange("n f (a h) t -> n (f a) (h t)", h=2), fill[:, k]).then_inc(s_set, 16)

            sp.wait_ge(s_wfz, 1)
            for n, w in enumerate(("gate", "up")):
                src = i["L0_ffn_w_" + w]
                sp.dma_start(wf[:, 3 * n * D:(3 * n + 2) * D].rearrange("p (t c) -> p t c", c=D),
                             src[0:2 * P].rearrange("(t p) c -> p t c", p=P)).then_inc(s_wf, 16)
                sp.dma_start(wf[0:FFN - 2 * P, (3 * n + 2) * D:(3 * n + 3) * D], src[2 * P:FFN]).then_inc(s_wf, 16)
            sp.dma_start(wf[:, 6 * D:WF], i["L0_ffn_w_down"]).then_inc(s_wf, 16)

            col = lambda name: i["L1_attn_" + name].rearrange("(p o) -> p o", o=1)
            sp.dma_start(wdt[:], i["L1_attn_dt_w"]).then_inc(s_w34, 16)
            sp.dma_start(cols[:, 0:1], col("dt_b")).then_inc(s_w34, 16)
            sp.dma_start(cols[:, 3:4], col("D_skip")).then_inc(s_w34, 16)
            for n in range(4):
                rows = slice(NSTATE * n, NSTATE * (n + 1))
                for m, w in enumerate("BC"):
                    sp.dma_start(wbc[rows, m], i[f"L1_attn_{w}_w"]).then_inc(s_w34, 16)
                    sp.dma_start(cols[rows, 1 + m:2 + m], col(w + "_b")).then_inc(s_w34, 16)
            sp.dma_start(log_a[:], i["L1_attn_log_A"]).then_inc(s_w34, 16)
            sp.dma_start(sel[:], i["sel"]).then_inc(s_w34, 16)
            sp.dma_start(wgate[:], i["L1_ffn_gate_w"]).then_inc(s_w34, 16)
            sp.dma_start(b1r[:], i["L1_ffn_b1"].rearrange("e (h p) -> (e h) p", p=P)).then_inc(s_w34, 16)
            sp.dma_start(b2[:], i["L1_ffn_b2"]).then_inc(s_w34, 16)
            sp.dma_start(tri[:], i["tri"]).then_inc(s_w34, 16)

            def store_parts(u):
                c, kind = divmod(u, 2)
                sp.wait_ge(s_part3, u + 1)
                dst = (q_dram, k_dram)[kind]
                for g in range(QUAD):
                    sp.dma_start(dst[4 * (c // 2) + g, c % 2].rearrange("n c t -> c n t"),
                                 parts[QC * g:QC * g + QC, u % CHUNKS]).then_inc(s_parts_out[u % CHUNKS], 16)

            def load(it, p):
                for f in range(2):
                    sp.dma_start(qs[p][0:PROD, f], q_dram[bass.ds(it, 1), f].rearrange(
                        "o n (d h) t -> (o n d) (h t)", h=QUAD).unsqueeze(1).to_broadcast([PARTS * HD, PARTS, QUAD * BANK])).then_inc(s_qk[p], 16)
                    for a in range(PARTS):
                        sp.dma_start(ks[p][HD * PARTS * a:HD * PARTS * (a + 1), f], k_dram[bass.ds(it, 1), f].rearrange(
                            "o n (d h) t -> d (o n) (h t)", h=QUAD)).then_inc(s_qk[p], 16)
                sp.dma_start(qs[p][PROD:PROD + 2], fill[0:16, 0, 0:BANK]).then_inc(s_qk[p], 16)

            def store_maxima(it, p, half):
                sp.wait_ge(s_nmax, 2 * it + half + 1)
                for z in range(4):
                    sp.dma_start(
                        qs[p][PROD:PROD + 2, half].rearrange("n h (q t) -> n (h q) t", t=P)[:, :, 32 * z:32 * z + 32],
                        nmax_t[32 * z:32 * z + 32, half, :]).then_inc(s_nrow[half], 16)

            def store_out(it, half):
                sp.wait_ge(s_o, 2 * it + half + 2)
                sp.dma_start(o_dram[bass.ds(it, 1), :, half * BANK:(half + 1) * BANK].rearrange("o r t -> (o r) t"),
                             o_sb[:, half, :]).then_inc(s_o_out[half], 16)

            for u in range(CHUNKS):
                store_parts(u)
            for n in range(CHUNKS):
                sp.wait_ge(s_parts_out[n], 16 * QUAD)
            sp.wait_ge(s_set, 16 * 2 * SETS)
            for p in range(SETS):
                load(p, p)
            for u in range(CHUNKS, 2 * CHUNKS):
                store_parts(u)
            for n in range(CHUNKS):
                sp.wait_ge(s_parts_out[n], 16 * QUAD * 2)
            store_maxima(0, 0, 0)
            store_maxima(0, 0, 1)

            def one_pass(it, p, more, again=None):
                if more:
                    store_maxima(it + 1, (p + 1) % SETS, 0)
                store_out(it, 0)
                if again is not None:
                    sp.wait_ge(s_pv, STEPS * (it + 1))
                    load(again, p)
                store_out(it, 1)
                if more:
                    store_maxima(it + 1, (p + 1) % SETS, 1)

            def load_out(b):
                sp.wait_ge(s_o_out[0], 16 * (4 * b + 4 + 1))
                sp.wait_ge(s_o_out[1], 16 * (4 * b + 4 + 1))
                rows = o_dram[4 * b:4 * b + 4].rearrange("q (h r) t -> (q h) r t", r=32)
                sp.dma_start(den[:, b], rows[:, HD]).then_inc(s_od[b], 16)
                sp.dma_start(num[:, b * SEQ:(b + 1) * SEQ], rows[:, 0:HD]).then_inc(s_num, 16)
                sp.wait_ge(s_rden, b + 1)
                sp.dma_start(r_dram[b].rearrange("h (c t) -> (h c) t", c=P // HEADS), den[:, b]).then_inc(s_od[b], 16)
                sp.wait_ge(s_od[b], 32)
                sp.dma_start(rden[:, b], r_dram[b].unsqueeze(1).to_broadcast([HEADS, HD, SEQ])).then_inc(s_num, 16)
                sp.wait_ge(s_num, 32 * (b + 1))
                sp.sem_inc(s_ready, 1)

            with sp.Fori(0, PASSES // SETS) as r:
                for p in range(SETS):
                    one_pass(SETS * r + p, p, True, (SETS * r + p + SETS) % PASSES)
            load_out(0)
            one_pass(PASSES - 2, 0, True)
            one_pass(PASSES - 1, 1, False)
            load_out(1)

            def load_expert(e, p):
                sp.dma_start(w12[p][:, 0], i["L1_ffn_w1"][bass.ds(e, 1)].rearrange("o c h -> c (o h)")).then_inc(s_w12[p], 16)
                sp.dma_start(w12[p][:, 1].rearrange("p (t c) -> p t c", c=D),
                             i["L1_ffn_w2"][bass.ds(e, 1)].rearrange("o (t p) c -> p (o t) c", p=P)).then_inc(s_w12[p], 16)

            def load_gate(e, p):
                sp.dma_start(gate[:, p], c_dram[bass.ds(e, 1)].to_broadcast([P, TOKENS])).then_inc(s_gate[p], 16)

            sp.wait_ge(s_wft_ps, 1)
            load_expert(0, 0)
            load_expert(1, 1)
            sp.wait_ge(s_combt, 2)
            sp.dma_start(c_dram, comb_t[:]).then_inc(s_comb_out, 16)
            sp.wait_ge(s_comb_out, 16)
            load_gate(0, 0)
            load_gate(1, 1)
            with sp.Fori(1, EXPERTS // 2) as r:
                for p in range(2):
                    sp.wait_ge(s_moe, 2 + CHUNKS * (2 * r + p - 1))
                    load_expert(2 * r + p, p)
                    load_gate(2 * r + p, p)
            ov = out.rearrange("b (t p) c -> p (b t) c", p=P)
            for c in range(CHUNKS):
                sp.wait_ge(s_final, c + 1)
                sp.dma_start(ov[:, 4 * c:4 * c + 4], x[:, 4 * c:4 * c + 4]).then_inc(s_out, 16)
            sp.wait_ge(s_out, 16 * CHUNKS)

        @block.gpsimd
        def _(pool):
            nc.gpsimd.memset(zero[:], 0.0)
            for n in range(2):
                nc.gpsimd.memset(borders[:, n:n + 1], -MIDS[5 + n])
            nc.gpsimd.memset(fill[:, 0], 0.0)
            nc.gpsimd.memset(fill[:, 1], 1.0).then_inc(s_fill, 1)
            pool_step(nc.gpsimd.memset(expo[:], -0.5))
            for h in range(2):
                norm_pool(0, h)
            pool.wait_ge(s_rstd, 2)
            for n in range(SETS):
                ins = nc.gpsimd.memset(vq[n][:], 1.0)
            pool_step(ins)
            def third_part(u):
                b = u % 2
                pool.wait_ge(s_rest, u + 1)
                pool.wait_ge(s_part2, u + 1)
                nc.gpsimd.tensor_tensor(parts[:, u % CHUNKS, 2], rest[:, b], parts[:, u % CHUNKS, 1], ALU.subtract).then_inc(s_part3, 1)

            for u in range(2 * CHUNKS):
                b = u % 2
                pool.wait_ge(s_part1, u + 1)
                if u >= 2:
                    pool.wait_ge(s_part3, u - 1)
                nc.gpsimd.tensor_tensor(rest[:, b], rot[:, b, 2], parts[:, u % CHUNKS, 0], ALU.subtract).then_inc(s_rest, 1)
                if u:
                    third_part(u - 1)
            third_part(2 * CHUNKS - 1)

            def values(it, p):
                nc.gpsimd.tensor_copy(vq[p][:, :, :, 0:HD], v[:, bass.ds(it, 1)].rearrange(
                    "p o k (h d) -> p (o k) h d", d=HD)).then_inc(s_vq, 1)

            pool.wait_ge(s_v, 4)
            for p in range(SETS):
                values(p, p)
            with pool.Fori(1, PASSES // SETS) as r:
                for p in range(SETS):
                    pool.wait_ge(s_pv, STEPS * (SETS * (r - 1) + p + 1))
                    values(SETS * r + p, p)
            for p in range(PASSES % SETS):
                pool.wait_ge(s_pv, STEPS * (SETS * (PASSES // SETS - 1) + p + 1))
                values(PASSES - PASSES % SETS + p, p)

            hidden_slot = lambda g: hid[:, g % 2]
            norm_pool(1, 0)
            pool.wait_ge(s_qk[SETS - 1], LOADS * (PASSES // SETS + 1))
            quant_pool(0, wf[:])
            quant_pool(1, x_half(xc, 0))
            quant_pool(2, hidden_slot(0))
            norm_pool(1, 1)
            quant_pool(3, x_half(xc, 1))
            for g in range(1, 4):
                quant_pool(HID_PIECE[g], hidden_slot(g))

            norm_pool(2, 0)
            norm_pool(2, 1)

            def c_rest(b, before):
                w = slice(b * SEQ, (b + 1) * SEQ)
                pool.wait_ge(*before)
                pool.wait_ge(s_bc, 4 * (b + 1))
                pool.wait_ge(s_bp, 2 * b + 2)
                nc.gpsimd.tensor_tensor(bc32[64:P, 1, w], bc32[64:P, 1, w], bcp[64:P, 1, w], ALU.subtract).then_inc(s_rest3[1], 1)
                pool.wait_ge(s_rest3[1], b + 1)

            def c_last(b):
                w = slice(b * SEQ, (b + 1) * SEQ)
                pool.wait_ge(s_bp2, 2 * b + 2)
                nc.gpsimd.tensor_tensor(bcp[96:P, 1, w], bc32[96:P, 1, w], bcp[96:P, 1, w], ALU.subtract).then_inc(s_bp3[1], 1)
                pool.wait_ge(s_bp3[1], b + 1)

            c_rest(0, (s_rstd, 6))
            c_last(0)

            def outflow(b, n, slot):
                m = NSTATE * b + n
                pool.wait_ge(s_scan, m + 1)
                pool.wait_ge(s_cs, m + 1)
                if not (isinstance(m, int) and m < RING):
                    pool.wait_ge(s_y3, m - RING + 1)
                nc.gpsimd.tensor_tensor(hc[:, slot], hst[:, slot], cbr[:, slot], ALU.mult).then_inc(s_hc, 1)

            for b in range(BATCH):
                if b == 0:
                    for n in range(PEEL):
                        outflow(0, n, n % RING)
                        if n == 4:
                            c_rest(1, (s_hc, n + 1))
                    pool.wait_ge(s_hc, PEEL)
                    c_last(1)
                with pool.Fori(0 if b else PEEL // RING, NSTATE // RING) as k:
                    for n in range(RING):
                        outflow(b, RING * k + n, n)

            def split_weights(e, p):
                pool.wait_ge(s_w12[p], 16 * (e + 2 - p))
                nc.gpsimd.tensor_tensor(w12_h[:, p], w12[p], zero[:].unsqueeze(2).to_broadcast([P, 2, HIDDEN]),
                                        ALU.subtract).then_inc(s_w_h, 1)
                pool.wait_ge(s_w_h, e + 1)
                nc.gpsimd.tensor_tensor(w12_l[:, p], w12[p], w12_h[:, p].bitcast(F32), ALU.subtract).then_inc(s_w_l, 1)

            pool.wait_ge(s_hc, BATCH * NSTATE)
            pool.wait_ge(s_skip, BATCH)
            split_weights(0, 0)
            pool.wait_ge(s_w_l, 1)
            norm_pool(3, 0)
            norm_pool(3, 1)
            pool.wait_ge(s_rstd, 8)
            split_weights(1, 1)
            with pool.Fori(1, EXPERTS // 2) as k:
                for p in range(2):
                    split_weights(2 * k + p, p)

        @block.scalar
        def _(act):
            for h in range(2):
                norm_act(0, h)
            act.wait_ge(s_wt_ps, 1)
            nc.scalar.activation(wt[:, 0:4, :], ps[:, 4, :], ACT.Copy).then_inc(s_wt, 1)
            nc.scalar.activation(wt[:, 4:6, :], ps[:, 5, 0:2 * D], ACT.Copy).then_inc(s_wt, 1)
            nc.scalar.activation(bperm[:], ps[:, 5, 2 * D:2 * D + 4].rearrange("p (n k) -> p n k", k=2), ACT.Copy).then_inc(s_wt, 1)
            def second_part(u):
                act.wait_ge(s_rest, u + 1)
                nc.scalar.activation(parts[:, u % CHUNKS, 1], rest[:, u % 2], ACT.Copy).then_inc(s_part2, 1)

            turn_act(0, 0)
            turn_act(0, 1)
            for u in range(2 * CHUNKS):
                b = u % 2
                act.wait_ge(s_rope, u + 1)
                if u >= CHUNKS:
                    act.wait_ge(s_parts_out[u % CHUNKS], 16 * QUAD)
                nc.scalar.activation(parts[:, u % CHUNKS, 0], rot[:, b, 2], ACT.Copy).then_inc(s_part1, 1)
                if u:
                    second_part(u - 1)
                if u == 2:
                    turn_act(0, 2)
                    turn_act(0, 3)
            second_part(2 * CHUNKS - 1)

            def one_pass(it, first, between={}):
                for s in range(STEPS):
                    if s in between:
                        between[s]()
                    for j in range(4):
                        n = 4 * s + j
                        if j == 0 and s >= 2:
                            act.wait_ge(s_pv, STEPS * it + s - 1)
                        act.wait_ge(s_st, 4 * STEPS * it + n + 1)
                        nc.scalar.activation(prob[:, n % 8], ps[:, 4 + (first + n) % 3], ACT.Exp,
                                             scale=ATT_SCALE).then_inc(s_exp, 1)
                    if s == KT:
                        evacuate(it, 0)
                evacuate(it, 1)

            def evacuate(it, half):
                act.wait_ge(s_pv, STEPS * it + KT * (half + 1))
                act.wait_ge(s_o_out[half], 16 * (it + 1))
                nc.scalar.activation(o_sb[:, half], ps[:, 7], ACT.Copy).then_inc(s_o, 1)

            for half in range(2):
                act.sem_inc(s_o_out[half], 16)
            with act.Fori(0, PASSES // SETS) as r:
                for p in range(SETS):
                    one_pass(SETS * r + p, 4 * STEPS * p)
            one_pass(PASSES - 2, 0)

            def turned_weights():
                act.wait_ge(s_wft_ps, 1)
                nc.scalar.activation(wgu_t[:], ps[:, 1:3, 0:FFN], ACT.Copy).then_inc(s_wft, 1)
                nc.scalar.activation(wd_t[:, 0:2], ps[:, 3, 0:2 * D].rearrange("p (t c) -> p t c", c=D), ACT.Copy).then_inc(s_wft, 1)
                nc.scalar.activation(wd_t[0:FFN - 2 * P, 2], ps[0:FFN - 2 * P, 3, 2 * D:3 * D], ACT.Copy).then_inc(s_wft, 1)

            def turned_x(g, bank):
                act.wait_ge(s_turned, 4 + g + 1)
                act.wait_ge(s_v_ps, 4)
                nc.scalar.activation(xt[:, g * BANK:(g + 1) * BANK], ps[:, bank, :], ACT.Copy).then_inc(s_xt, 1)

            def turned_hidden(g):
                for j in range(3):
                    rows = min(P, FFN - j * P)
                    act.wait_ge(s_ht_ps, 3 * g + j + 1)
                    if g:
                        act.wait_ge(s_down, g)
                    nc.scalar.activation(hid_t[0:rows, j], ps[0:rows, 4 + j], ACT.Copy).then_inc(s_ht, 1)

            def silus(t0, t1):
                for t in range(t0, t1):
                    act.wait_ge(s_gu, t + 1)
                    if t >= 2:
                        act.wait_ge(s_hid, t - 1)
                    nc.scalar.activation(silu[:, t % 2], ps[:, 2 * (t % 2), 0:FFN], ACT.Silu).then_inc(s_silu, 1)

            one_pass(PASSES - 1, 4 * STEPS, {
                4: lambda: norm_act(1, 0),
                7: lambda: quant_act(0, WF),
                10: lambda: quant_act(1, TOKENS // 2),
                13: turned_weights})
            turned_x(0, 0)
            turned_x(1, 1)
            silus(0, 4)
            quant_act(2, QMAX)
            norm_act(1, 1)
            silus(4, 8)
            quant_act(3, TOKENS // 2)
            borders_act(3, TOKENS // 2)
            turned_hidden(0)
            quant_act(4, QMAX)
            borders_act(4, QMAX)
            turned_x(2, 4)
            turned_x(3, 5)
            silus(8, 16)
            quant_act(5, QMAX)
            borders_act(5, QMAX)
            turned_hidden(1)
            quant_act(6, QMAX)
            borders_act(6, QMAX)
            norm_act(2, 0)
            turned_hidden(2)

            act.wait_ge(s_dtw_ps, 1)
            nc.scalar.activation(ssm_t[:], ps[:, 0, 0:3 * D].rearrange("p (t c) -> p t c", c=D), ACT.Copy).then_inc(s_dtw, 1)
            nc.scalar.activation(b1t[:, 0:EXPERTS * HT], ps[:, 0, 3 * D:3 * D + EXPERTS * HT], ACT.Copy).then_inc(s_dtw, 1)
            nc.scalar.activation(sel_b[:], sel[:], ACT.Copy).then_inc(s_selb, 1)
            turn_act(2, 0)
            turn_act(2, 1)
            turned_hidden(3)

            def z_projected(c):
                w = slice(c * BANK, (c + 1) * BANK)
                act.wait_ge(s_zps, 3 * c + 1)
                nc.scalar.activation(zt[:, w], ps[:, 3], ACT.Identity, bias=cols[:, 0:1]).then_inc(s_z, 1)

            def softplus_exp(b):
                w = slice(b * SEQ, (b + 1) * SEQ)
                act.wait_ge(s_z, 2 * (b + 1))
                nc.scalar.activation(dt[:, w], zt[:, w], ACT.Abs).then_inc(s_e, 1)
                act.wait_ge(s_e, 2 * b + 1)
                nc.scalar.activation(dt[:, w], dt[:, w], ACT.Exp, scale=-1.0).then_inc(s_e, 1)

            def first_parts(b):
                w = slice(b * SEQ, (b + 1) * SEQ)
                act.wait_ge(s_bc, 4 * (b + 1))
                for n in range(2):
                    nc.scalar.activation(bcp[:, n, w], bc32[:, n, w], ACT.Copy).then_inc(s_bp, 1)

            def softplus_ln(b):
                w = slice(b * SEQ, (b + 1) * SEQ)
                act.wait_ge(s_u, b + 1)
                if b:
                    act.wait_ge(s_dt, 2 * b)
                nc.scalar.activation(ln_u[:], dtx[:, w], ACT.Ln).then_inc(s_ln, 1)

            def second_parts(b):
                w = slice(b * SEQ, (b + 1) * SEQ)
                for n in range(2):
                    act.wait_ge(s_rest3[n], b + 1)
                    nc.scalar.activation(bcp[64:P, n, w], bc32[64:P, n, w], ACT.Copy).then_inc(s_bp2, 1)

            z_projected(0)
            z_projected(1)
            norm_act(2, 1)
            nc.scalar.activation(a_neg[:], log_a[:], ACT.Exp).then_inc(s_a, 1)
            softplus_exp(0)
            first_parts(0)
            softplus_ln(0)
            turn_act(2, 2, 5)
            turn_act(2, 3, 6)
            second_parts(0)
            z_projected(2)
            z_projected(3)

            def factors(b, n, slot):
                m = NSTATE * b + n
                first = isinstance(m, int) and m < RING
                if not first:
                    act.wait_ge(s_scan, m - RING + 1)
                act.wait_ge(s_a, 2)
                nc.scalar.activation(abar[:, slot], dt[:, b * SEQ:(b + 1) * SEQ], ACT.Exp,
                                     scale=a_neg[:, bass.ds(n, 1)]).then_inc(s_abar, 1)
                act.wait_ge(s_cb, m + 1)
                if not first:
                    act.wait_ge(s_hc, m - RING + 1)
                nc.scalar.activation(cbr[:, slot], ps[:, 4:6], ACT.Copy).then_inc(s_cs, 1)

            act.wait_ge(s_a, 2)
            for b in range(BATCH):
                act.wait_ge(s_dt, 2 * b + 1)
                if b == 0:
                    for n in range(PEEL):
                        factors(0, n, n % RING)
                        if n in (1, 3, 4, 6):
                            {1: softplus_exp, 3: first_parts, 4: softplus_ln, 6: second_parts}[n](1)
                with act.Fori(0 if b else PEEL // RING, NSTATE // RING) as k:
                    for n in range(RING):
                        factors(b, RING * k + n, n)

            def turn_and_round(g):
                turn_act(3, g)
                nc.scalar.activation(xh[:, g * BANK:(g + 1) * BANK], ps[:, g], ACT.Copy).then_inc(s_xh, 1)

            act.sem_inc(s_gelu, HT)
            norm_act(3, 0)
            norm_act(3, 1)
            turn_and_round(0)
            turn_and_round(1)

            def unit(k, u):
                m = UNITS * k + u
                act.wait_ge(s_l2, m + 1)
                if u % CHUNKS == 0:
                    act.wait_ge(s_b1_now, 2 * k + u // CHUNKS + 1)
                for h in range(HT):
                    act.wait_ge(s_l1, HT * m + h + 1)
                    nc.scalar.activation(act_t[:, u % 2, h], ps[:, h], ACT.Gelu,
                                         bias=b1_now[:, u // CHUNKS, h:h + 1]).then_inc(s_gelu, 1)
                    if h % 2:
                        act.wait_ge(s_gelu, HT * (m + 1) + h + 1)
                        nc.scalar.activation(act_h[:, u % 2, h - 1:h + 1], act_t[:, u % 2, h - 1:h + 1],
                                             ACT.Copy).then_inc(s_act_h, 1)

            turn_and_round(2)
            turn_and_round(3)
            unit(0, 0)
            act.wait_ge(s_diff, 1)
            nc.scalar.activation(top[:, 3], top[:, 2], ACT.Exp).then_inc(s_ediff, 1)
            unit(0, 1)
            for n in range(2):
                act.wait_ge(s_combt_ps, n + 1)
                nc.scalar.activation(comb_t[:, n * SEQ:(n + 1) * SEQ].rearrange("e (g t) -> e g t", t=BANK), ps[0:EXPERTS, 4:6],
                                     ACT.Copy).then_inc(s_combt, 1)
            for c in range(CHUNKS):
                act.wait_ge(s_b2, c + 1)
                nc.scalar.activation(acc[:, c * BANK:(c + 1) * BANK], ps[:, 4 + c % 2], ACT.Copy).then_inc(s_acc, 1)
            for u in range(2, UNITS):
                unit(0, u)
            unit(1, 0)
            with act.Fori(1, EXPERTS // 2 - 1) as k:
                for u in range(1, UNITS):
                    unit(k, u)
                unit(k + 1, 0)
            for u in range(1, UNITS):
                unit(EXPERTS // 2 - 1, u)

        @block.vector
        def _(dve):
            nc.vector.memset(ps[:, 7], 0.0).then_inc(s_o, 1)
            nc.vector.memset(wf[:], 0.0).then_inc(s_wfz, 1)
            dve_step(nc.vector.memset(b1t[:, EXPERTS * HT:], 0.0))
            for h in range(2):
                dve.wait_ge(s_x[h], 16)
                norm_dve_a(0, h)
            for h in range(2):
                norm_dve_b(0, h)
            dve.wait_ge(s_const, 16 * N_CONST)
            dve.wait_ge(s_wt, 3)
            for u in range(2 * CHUNKS):
                c, kind = divmod(u, 2)
                b = u % 2
                t0 = (c % 2) * BANK
                dve.wait_ge(s_proj, u + 1)
                if u >= 2:
                    dve.wait_ge(s_rest, u - 1)
                nc.vector.scalar_tensor_tensor(rot[:, b, 0], ps[:, 4 + 2 * b], bperm[:, 0, kind:kind + 1],
                                               cos[:, t0:t0 + BANK], ALU.add, ALU.mult)
                ins = nc.vector.scalar_tensor_tensor(rot[:, b, 1], ps[:, 5 + 2 * b], bperm[:, 1, kind:kind + 1],
                                                     sin[:, t0:t0 + BANK], ALU.add, ALU.mult)
                ins.then_inc(s_rope_read, 1)
                dve.wait_ge(s_rope_read, u + 1)
                nc.vector.tensor_tensor(rot[:, b, 2], rot[:, b, 0], rot[:, b, 1], ALU.add).then_inc(s_rope, 1)
            for g in range(4):
                b, k0 = divmod(4 * g, KT)
                dve.wait_ge(s_v_ps, g + 1)
                for j in range(4):
                    ins = nc.vector.tensor_tensor(v[:, 4 * b:4 * b + 4, k0 + j, :],
                                                  ps[:, g, j * P:(j + 1) * P].rearrange("p (q c) -> p q c", c=QC),
                                                  bv_all[:].rearrange("p (q c) -> p q c", c=QC), ALU.add)
                ins.then_inc(s_v, 1)

            def maxima(it):
                for half in range(2):
                    for n in range(16):
                        t = 16 * half + n
                        dve.wait_ge(s_score, 32 * it + t + 1)
                        nc.vector.tensor_reduce(nmax[:, half, n:n + 1], ps[:, 2 * (t % 2):2 * (t % 2) + 2, :],
                                                AX.XY, ALU.max, negate=True).then_inc(s_max, 1)
                    w = 2 * (2 * it + half)
                    dve.wait_ge(s_max, 32 * it + 16 * half + 16)
                    nc.vector.tensor_copy(nmax_p[:, 0:16], nmax[:, half]).then_inc(s_mstep, 1)
                    dve.wait_ge(s_mstep, w + 1)
                    nc.vector.tensor_tensor(nmax_p[:, 16:32], nmax[:, half], nmax_p[:, 0:16], ALU.subtract).then_inc(s_mstep, 1)
                    dve.wait_ge(s_mstep, w + 2)
                    dve.wait_ge(s_nrow[half], 64 * it)
                    nc.vector.transpose(nmax_t[:, half, :], nmax_p[:]).then_inc(s_nmax, 1)

            maxima(0)
            with dve.Fori(1, PASSES - 1) as it:
                maxima(it)

            def inverse_denominators(b):
                dve.wait_ge(s_od[b], 16)
                nc.vector.reciprocal(den[:, b], den[:, b]).then_inc(s_rden, 1)

            def attention_out(b):
                w = slice(b * SEQ, (b + 1) * SEQ)
                dve.wait_ge(s_ready, b + 1)
                nc.vector.tensor_tensor(num[:, w], num[:, w], rden[:, b], ALU.mult).then_inc(s_att, 1)
                for g in (2 * b, 2 * b + 1):
                    dve_step(nc.vector.tensor_tensor(x[:, 4 * g:4 * g + 4, :], x[:, 4 * g:4 * g + 4, :],
                                                     bo_all[:].unsqueeze(1).to_broadcast([P, 4, D]), ALU.add))
                    dve.wait_ge(s_y, g + 1)
                    nc.vector.tensor_tensor(x[:, 4 * g:4 * g + 4, :], x[:, 4 * g:4 * g + 4, :],
                                            ps[:, 4 * b + g % 2, :].rearrange("p (t c) -> p t c", c=D), ALU.add).then_inc(s_res, 1)

            inverse_denominators(0)
            maxima(PASSES - 1)

            attention_out(0)
            dve.wait_ge(s_res, 2)
            norm_dve_a(1, 0)
            dve.wait_ge(s_qk[SETS - 1], LOADS * (PASSES // SETS + 1))
            quant_scale(0, wf[:], (s_wf, 16 * 5))
            norm_dve_b(1, 0)
            quant_scale(1, x_half(xc, 0), (s_normed, 3))
            quant_grid(0, wfq[:])
            quant_grid(1, x_half(sq, 0))
            inverse_denominators(1)

            def hidden(g):
                for t in range(4 * g, 4 * g + 4):
                    dve.wait_ge(s_silu, t + 1)
                    if g >= 2:
                        dve.wait_ge(s_qx, HID_PIECE[g - 2] + 1)
                    nc.vector.tensor_tensor(hid[:, g % 2, (t % 4) * FFN:(t % 4 + 1) * FFN], silu[:, t % 2],
                                            ps[:, 2 * (t % 2) + 1, 0:FFN], ALU.mult).then_inc(s_hid, 1)
                quant_scale(HID_PIECE[g], hid[:, g % 2], (s_hid, 4 * g + 4))

            def down(g):
                dve.wait_ge(s_down, g + 1)
                nc.vector.tensor_tensor(x[:, 4 * g:4 * g + 4, :], x[:, 4 * g:4 * g + 4, :],
                                        ps[:, 7].rearrange("p (t c) -> p t c", c=D), ALU.add).then_inc(s_res, 1)

            hidden(0)
            attention_out(1)
            dve.wait_ge(s_res, 4)
            norm_dve_a(1, 1)
            norm_dve_var(1, 1)
            quant_grid(2, hid_q[:, 0])
            norm_dve_scale(1, 1)
            quant_scale(3, x_half(xc, 1), (s_normed, 4))
            hidden(1)
            quant_grid(3, x_half(sq, 1))
            down(0)
            quant_grid(4, hid_q[:, 1])
            hidden(2)
            hidden(3)
            quant_grid(5, hid_q[:, 0], (s_ht_ps, 3))
            down(1)
            dve.wait_ge(s_res, 6)
            norm_dve_a(2, 0)
            quant_grid(6, hid_q[:, 1], (s_ht_ps, 6), lambda: norm_dve_var(2, 0), lambda: norm_dve_scale(2, 0))
            down(2)

            def bc_projected(c):
                w = slice(c * BANK, (c + 1) * BANK)
                for n in range(2):
                    dve.wait_ge(s_zps, 3 * c + n + 2)
                    nc.vector.tensor_scalar(bc32[:, n, w], ps[:, 2 - n], cols[:, 1 + n:2 + n], None, ALU.add).then_inc(s_bc, 1)

            def softplus_u(b):
                w = slice(b * SEQ, (b + 1) * SEQ)
                dve.wait_ge(s_e, 2 * b + 2)
                nc.vector.tensor_scalar(dtx[:, w], dt[:, w], 1.0, None, ALU.add).then_inc(s_u, 1)
                dve.wait_ge(s_bp, 2 * b + 1)
                nc.vector.tensor_tensor(bc32[64:P, 0, w], bc32[64:P, 0, w], bcp[64:P, 0, w], ALU.subtract).then_inc(s_rest3[0], 1)

            def softplus_lost(b):
                w = slice(b * SEQ, (b + 1) * SEQ)
                dve.wait_ge(s_u, b + 1)
                dve_step(nc.vector.scalar_tensor_tensor(dt[:, w], dtx[:, w], 1.0, dt[:, w], ALU.subtract, ALU.subtract))

            def softplus_dt(b):
                w = slice(b * SEQ, (b + 1) * SEQ)
                dve.wait_ge(s_ln, b + 1)
                dve_step(nc.vector.tensor_tensor(dt[:, w], ln_u[:], dt[:, w], ALU.subtract))
                nc.vector.scalar_tensor_tensor(dt[:, w], zt[:, w], 0.0, dt[:, w], ALU.max, ALU.add).then_inc(s_dt, 1)

            def inflow_factor(b):
                w = slice(b * SEQ, (b + 1) * SEQ)
                dve.wait_ge(s_dt, 2 * b + 1)
                nc.vector.tensor_tensor(dtx[:, w], dt[:, w], xt[:, w], ALU.mult).then_inc(s_dt, 1)
                dve.wait_ge(s_bp2, 2 * b + 1)
                nc.vector.tensor_tensor(bcp[96:P, 0, w], bc32[96:P, 0, w], bcp[96:P, 0, w], ALU.subtract).then_inc(s_bp3[0], 1)

            down(3)
            bc_projected(0)
            dve.wait_ge(s_res, 8)
            norm_dve_a(2, 1)
            bc_projected(1)
            norm_dve_b(2, 1)
            dve.wait_ge(s_a, 1)
            nc.vector.tensor_scalar(a_neg[:], a_neg[:], -1.0, None, ALU.mult).then_inc(s_a, 1)
            dve.wait_ge(s_bc, 4)
            softplus_u(0)
            softplus_lost(0)
            softplus_dt(0)
            inflow_factor(0)
            bc_projected(2)
            bc_projected(3)

            def inflow(b, n, slot):
                m = NSTATE * b + n
                dve.wait_ge(s_bb, m + 1)
                if not (isinstance(m, int) and m < RING):
                    dve.wait_ge(s_scan, m - RING + 1)
                nc.vector.tensor_tensor(dbx[:, slot].rearrange("p (k t) -> p k t", k=2),
                                        dtx[:, b * SEQ:(b + 1) * SEQ].rearrange("p (k t) -> p k t", k=2),
                                        ps[:, 2 * (slot % 2):2 * (slot % 2) + 2], ALU.mult).then_inc(s_dbx, 1)

            def scan(b, n, slot):
                m = NSTATE * b + n
                dve.wait_ge(s_dbx, m + 1)
                dve.wait_ge(s_abar, m + 1)
                if not (isinstance(m, int) and m < RING):
                    dve.wait_ge(s_hc, m - RING + 1)
                nc.vector.tensor_tensor_scan(hst[:, slot], abar[:, slot], dbx[:, slot], 0.0, ALU.mult, ALU.add).then_inc(s_scan, 1)

            def skip(b):
                w = slice(b * SEQ, (b + 1) * SEQ)
                dve.wait_ge(s_y3, NSTATE * (b + 1))
                nc.vector.scalar_tensor_tensor(zt[:, w].rearrange("p (k t) -> p k t", k=2),
                                               xt[:, w].rearrange("p (k t) -> p k t", k=2), cols[:, 3:4],
                                               ps[:, 6:8], ALU.mult, ALU.add).then_inc(s_skip, 1)

            def add_scanned(b):
                for g in (2 * b, 2 * b + 1):
                    dve.wait_ge(s_yt, g + 1)
                    nc.vector.tensor_tensor(x[:, 4 * g:4 * g + 4, :], x[:, 4 * g:4 * g + 4, :],
                                            ps[:, g].rearrange("p (t c) -> p t c", c=D), ALU.add).then_inc(s_res, 1)
                dve.wait_ge(s_res, 8 + 2 * (b + 1))

            dve.wait_ge(s_dt, 2)
            inflow(0, 0, 0)
            for b in range(BATCH):
                for n in range(PEEL):
                    inflow(b, n + 1, (n + 1) % RING)
                    scan(b, n, n % RING)
                    if b and n == 1:
                        skip(b - 1)
                    if b == 0 and n in (2, 4, 5, 7):
                        {2: softplus_u, 4: softplus_lost, 5: softplus_dt, 7: inflow_factor}[n](1)
                dve.wait_ge(s_dt, 2 * BATCH)
                with dve.Fori(PEEL // RING, NSTATE // RING - 1) as k:
                    for n in range(RING):
                        inflow(b, RING * k + n + 1, (n + 1) % RING)
                        scan(b, RING * k + n, n)
                for n in range(NSTATE - RING, NSTATE):
                    if NSTATE * b + n + 1 < BATCH * NSTATE:
                        inflow(*divmod(NSTATE * b + n + 1, NSTATE), (n + 1) % RING)
                    scan(b, n, n % RING)
            add_scanned(0)
            norm_dve_a(3, 0)
            skip(BATCH - 1)
            norm_dve_var(3, 0)
            add_scanned(1)
            def lower_x(c):
                w = slice(c * BANK, (c + 1) * BANK)
                dve.wait_ge(s_xh, c + 1)
                nc.vector.tensor_tensor(xl[:, w], xt[:, w], xh[:, w].bitcast(F32), ALU.subtract).then_inc(s_xl, 1)

            norm_dve_a(3, 1)
            norm_dve_scale(3, 0)
            norm_dve_b(3, 1)
            lower_x(0)
            lower_x(1)
            def next_bias(e, p):
                nc.vector.tensor_scalar(b1_now[:, p], b1t[:, bass.ds(HT * e, HT)], 1.0, None, ALU.mult).then_inc(s_b1_now, 1)

            dve.sem_inc(s_moe, 2)
            dve.wait_ge(s_dtw, 2)
            next_bias(0, 0)
            next_bias(1, 1)

            def second_parts(k, u):
                m = UNITS * k + u
                for h in (0, 2):
                    dve.wait_ge(s_act_h, 2 * m + h // 2 + 1)
                    nc.vector.tensor_tensor(act_l[:, u % 2, h:h + 2], act_t[:, u % 2, h:h + 2],
                                            act_h[:, u % 2, h:h + 2].bitcast(F32), ALU.subtract).then_inc(s_act_l, 1)
                if u % CHUNKS == CHUNKS - 1:
                    next_bias(2 * k + 2 + u // CHUNKS, u // CHUNKS)

            lower_x(2)
            lower_x(3)
            dve.wait_ge(s_lgps, 1)
            lg3 = lg[:].rearrange("p t e -> p (t e)")
            dve_step(nc.vector.tensor_copy(lg3, ps[:, 4, 0:TILES * EXPERTS]))
            shape = [P, TILES, EXPERTS, EXPERTS]
            l_e = lg[:].unsqueeze(3).to_broadcast(shape)
            l_j = lg[:].unsqueeze(2).to_broadcast(shape)
            nc.vector.tensor_tensor(gt[:], l_j, l_e, ALU.is_gt)
            dve_step(nc.vector.tensor_tensor(eq[:], l_j, l_e, ALU.is_equal))
            dve_step(nc.vector.tensor_tensor(eq[:], eq[:], tri[:].unsqueeze(1).to_broadcast(shape), ALU.mult))
            dve_step(nc.vector.tensor_tensor(gt[:], gt[:], eq[:], ALU.add))
            dve_step(nc.vector.tensor_reduce(rank[:], gt[:], AX.X, ALU.add))
            nc.vector.tensor_reduce(top[:, 0], lg[:], AX.X, ALU.max)
            nc.vector.tensor_scalar(is01[:, 0], rank[:], 0.0, None, ALU.is_equal)
            dve_step(nc.vector.tensor_scalar(is01[:, 1], rank[:], 1.0, None, ALU.is_equal))
            dve_step(nc.vector.tensor_tensor(rank[:], lg[:], is01[:, 1], ALU.mult))
            dve_step(nc.vector.tensor_reduce(top[:, 1], rank[:], AX.X, ALU.add))
            nc.vector.tensor_tensor(top[:, 2], top[:, 1], top[:, 0], ALU.subtract).then_inc(s_diff, 1)
            second_parts(0, 0)
            dve.wait_ge(s_ediff, 1)
            dve_step(nc.vector.tensor_scalar(top[:, 4], top[:, 3], 1.0, None, ALU.add))
            dve_step(nc.vector.reciprocal(top[:, 4], top[:, 4]))
            dve_step(nc.vector.tensor_tensor(top[:, 5], top[:, 3], top[:, 4], ALU.mult))
            for n in range(2):
                ins = nc.vector.tensor_tensor(is01[:, n], is01[:, n], bc(top[:, 4 + n], EXPERTS), ALU.mult)
            dve_step(ins)
            nc.vector.tensor_tensor(comb[:], is01[:, 0], is01[:, 1], ALU.add).then_inc(s_comb, 1)

            def combine(k, u):
                m = UNITS * k + u
                e, c = divmod(u, CHUNKS)
                w = slice(c * BANK, (c + 1) * BANK)
                if c == 0:
                    dve.wait_ge(s_gate[e], 16 * (k + 1))
                dve.wait_ge(s_l2, m + 3)
                dve.wait_ge(s_moe, m + 2)
                nc.vector.tensor_tensor(term[:], ps[:, 6 + u % 2], gate[:, e, w], ALU.mult).then_inc(s_term, 1)
                dve.wait_ge(s_term, m + 1)
                nc.vector.tensor_tensor(acc[:, w], acc[:, w], term[:], ALU.add).then_inc(s_moe, 1)

            def add_experts(c):
                dve.wait_ge(s_back, c + 1)
                nc.vector.tensor_tensor(x[:, 4 * c:4 * c + 4, :], x[:, 4 * c:4 * c + 4, :],
                                        ps[:, 4 + c % 2].rearrange("p (t c) -> p t c", c=D), ALU.add).then_inc(s_final, 1)

            second_parts(0, 1)
            dve.wait_ge(s_acc, CHUNKS)
            combine(0, 0)
            for u in range(2, UNITS):
                second_parts(0, u)
                combine(0, u - 1)
            second_parts(1, 0)
            combine(0, UNITS - 1)
            with dve.Fori(1, EXPERTS // 2 - 1) as k:
                for u in range(1, UNITS):
                    second_parts(k, u)
                    combine(k, u - 1)
                second_parts(k + 1, 0)
                combine(k, UNITS - 1)
            last = EXPERTS // 2 - 1
            for u in range(1, UNITS):
                second_parts(last, u)
                combine(last, u - 1)
                if u >= CHUNKS + 2:
                    add_experts(u - CHUNKS - 2)
            combine(last, UNITS - 1)
            for c in range(2, CHUNKS):
                add_experts(c)

        @block.tensor
        def _(pe):
            pe.wait_ge(s_const, 16 * N_CONST)
            for n, (w, order) in enumerate(((0, 0), (0, 1), (1, 0), (1, 1), (2, 2), (3, 2))):
                nc.tensor.matmul(ps[:, 4 + n // 4, (n % 4) * D:(n % 4 + 1) * D], w4[:, w, :],
                                 ident[:] if order == 2 else perm[:, order],
                                 start=True, stop=True, is_transpose=True)
            for n in range(2):
                mm = nc.tensor.matmul(ps[:, 5, 2 * D + 2 * n:2 * D + 2 * n + 2], perm[:, n], bqk[:], start=True, stop=True)
            mm.then_inc(s_wt_ps, 1)
            turn_pe(0, 0)
            turn_pe(0, 1)
            pe.wait_ge(s_wt, 3)
            for u in range(2 * CHUNKS):
                if u == CHUNKS - 1:
                    turn_pe(0, 2)
                    turn_pe(0, 3)
                c, kind = divmod(u, 2)
                pe.wait_ge(s_xt, c + 1)
                if u >= 2:
                    pe.wait_ge(s_rope_read, u - 1)
                for n in range(2):
                    mm = nc.tensor.matmul(ps[:, 4 + 2 * (u % 2) + n], wt[:, 2 * kind + n, :],
                                          xt[:, c * BANK:(c + 1) * BANK], start=True, stop=True)
                mm.then_inc(s_proj, 1)
            for g in range(4):
                pe.wait_ge(s_xt, 4)
                for j in range(4):
                    t = 4 * g + j
                    mm = nc.tensor.matmul(ps[:, g, j * P:(j + 1) * P], xt[:, t * P:(t + 1) * P], wt[:, 4, :],
                                          start=True, stop=True)
                mm.then_inc(s_v_ps, 1)

            def score_half(it, p, t, kk):
                half, h, q = t // 16, t % 16 // 4, t % 4
                if kk == 0 and not (isinstance(it, int) and it == 0 and t < 2):
                    pe.wait_ge(s_max, 32 * it + t - 1)
                mm = nc.tensor.matmul(ps[:, 2 * (t % 2) + kk], qs[p][:, half, h, q * P:(q + 1) * P],
                                      ks[p][:, kk, h, :], start=True, stop=True)
                if kk == 1:
                    mm.then_inc(s_score, 1)

            def one_pass(it, p, first, more, loads=None, between={}):
                for s in range(STEPS):
                    if s in between:
                        between[s]()
                    half, kt = divmod(s, KT)
                    if kt == 0:
                        pe.wait_ge(s_nrow[half], 64 * (it + 1))
                    if more and s == 0:
                        pe.wait_ge(s_qk[(p + 1) % SETS], LOADS * loads)
                    todo = [(MAX_TILES * s + n // 2, n % 2) for n in range(2 * MAX_TILES)] if more else []
                    for j in range(QUAD):
                        n = 4 * s + j
                        if n >= 3:
                            pe.wait_ge(s_exp, 4 * STEPS * it + n - 2)
                        nc.tensor.matmul(ps[:, 4 + (first + n) % 3], ks[p][:, kt // 4, j, kt % 4 * P:(kt % 4 + 1) * P],
                                         qs[p][:, half, j, :], start=True, stop=True).then_inc(s_st, 1)
                        for t, kk in todo[len(todo) * j // 4:len(todo) * (j + 1) // 4]:
                            score_half(it + 1, (p + 1) % SETS, t, kk)
                        if s >= 1 and j == (QUAD - 1 if more else QUAD - 2):
                            products(it, p, s - 1)
                products(it, p, STEPS - 1)

            def products(it, p, s):
                half, kt = divmod(s, KT)
                if s == 0:
                    pe.wait_ge(s_vq, it + 1)
                if kt == 0:
                    pe.wait_ge(s_o, 2 * it + half + 1)
                pe.wait_ge(s_exp, 4 * STEPS * it + 4 * s + 4)
                for j in range(QUAD):
                    mm = nc.tensor.matmul(ps[32 * j:32 * j + VW, 7], vq[p][:, kt, j, :], prob[:, (4 * s + j) % 8],
                                          start=(kt == 0), stop=(kt == KT - 1))
                mm.then_inc(s_pv, 1)

            pe.wait_ge(s_qk[0], LOADS)
            pe.wait_ge(s_v, 4)
            for t in range(32):
                score_half(0, 0, t, 0)
                score_half(0, 0, t, 1)
            with pe.Fori(0, PASSES // SETS) as r:
                for p in range(SETS):
                    one_pass(SETS * r + p, p, 4 * STEPS * p, True, r + 1 + (p + 1) // SETS)
            one_pass(PASSES - 2, 0, 0, True, PASSES // SETS + 1)

            def project_out(b):
                pe.wait_ge(s_att, b + 1)
                if b:
                    pe.wait_ge(s_exp, 4 * STEPS * PASSES)
                for g in (2 * b, 2 * b + 1):
                    for j in range(4):
                        t = 4 * g + j
                        mm = nc.tensor.matmul(ps[:, 4 * b + g % 2, j * P:(j + 1) * P], num[:, t * P:(t + 1) * P], wt[:, 5, :],
                                              start=True, stop=True)
                    mm.then_inc(s_y, 1)

            def turn_weights():
                pe.wait_ge(s_quant, 1)
                pe.wait_ge(s_res, 2)
                for n in range(2):
                    for j in range(3):
                        rows = min(P, FFN - j * P)
                        nc.tensor.transpose(ps[:, 1 + n, j * P:j * P + rows], wfq[0:rows, (3 * n + j) * D:(3 * n + j + 1) * D],
                                            ident[0:rows, 0:rows])
                for j in range(3):
                    rows = min(P, FFN - j * P)
                    mm = nc.tensor.transpose(ps[0:rows, 3, j * D:(j + 1) * D], wfq[:, 6 * D + j * P:6 * D + j * P + rows], ident[:])
                mm.then_inc(s_wft_ps, 1)

            def turn_x(g, bank):
                for j in range(4):
                    mm = nc.tensor.transpose(ps[:, bank, j * P:(j + 1) * P], sq[:, 4 * g + j, :], ident[:])
                mm.then_inc(s_turned, 1)

            def gate_up(g):
                for t in range(4 * g, 4 * g + 4):
                    pe.wait_ge(s_xt, 4 + (2 if g < 2 else g + 1))
                    if t >= 2:
                        pe.wait_ge(s_hid, t - 1)
                    for n in range(2):
                        mm = nc.tensor.matmul(ps[:, 2 * (t % 2) + n, 0:FFN], xt[:, t * P:(t + 1) * P], wgu_t[:, n, :],
                                              start=True, stop=True)
                    mm.then_inc(s_gu, 1)

            def turn_hidden(g):
                pe.wait_ge(s_quant, HID_PIECE[g] + 1)
                for j in range(3):
                    rows = min(P, FFN - j * P)
                    if g:
                        pe.wait_ge(s_ht, 3 * g - 3 + j + 1)
                    for t in range(4):
                        mm = nc.tensor.transpose(ps[0:rows, 4 + j, t * P:(t + 1) * P],
                                                 hid_q[:, g % 2, t * FFN + j * P:t * FFN + j * P + rows], ident[:])
                    mm.then_inc(s_ht_ps, 1)

            def down(g):
                pe.wait_ge(s_ht, 3 * g + 3)
                if g:
                    pe.wait_ge(s_res, 4 + g)
                else:
                    pe.wait_ge(s_o, 2 * PASSES + 1)
                for t in range(4):
                    for j in range(3):
                        rows = min(P, FFN - j * P)
                        mm = nc.tensor.matmul(ps[:, 7, t * D:(t + 1) * D], hid_t[0:rows, j, t * P:(t + 1) * P],
                                              wd_t[0:rows, j, :], start=(j == 0), stop=(j == 2))
                mm.then_inc(s_down, 1)

            one_pass(PASSES - 1, 1, 4 * STEPS, False, between={1: lambda: project_out(0), 13: turn_weights})
            pe.wait_ge(s_quant, 2)
            turn_x(0, 0)
            pe.wait_ge(s_wft, 3)
            turn_x(1, 1)
            gate_up(0)
            project_out(1)
            gate_up(1)
            pe.wait_ge(s_res, 4)
            turn_hidden(0)
            down(0)
            pe.wait_ge(s_quant, 4)
            turn_x(2, 4)
            turn_x(3, 5)
            gate_up(2)
            gate_up(3)
            turn_hidden(1)
            down(1)

            pe.wait_ge(s_w34, 16 * N_W34)
            pe.wait_ge(s_hid, TILES)
            nc.tensor.transpose(ps[:, 0, 0:D], wdt[:], ident[:])
            for n in range(2):
                nc.tensor.transpose(ps[:, 0, (n + 1) * D:(n + 2) * D], wbc[:, n], ident[:])
            nc.tensor.transpose(ps[:, 0, 3 * D:3 * D + EXPERTS * HT], b1r[:],
                                ident[0:EXPERTS * HT, 0:EXPERTS * HT]).then_inc(s_dtw_ps, 1)

            turn_hidden(2)
            down(2)
            pe.wait_ge(s_dtw, 2)
            turn_pe(2, 0)
            turn_pe(2, 1)
            turn_hidden(3)

            def project(c):
                pe.wait_ge(s_xt, 8 + max(c, 1) + 1)
                for n in range(3):
                    if c:
                        if n:
                            pe.wait_ge(s_bc, 2 * (c - 1) + n)
                        else:
                            pe.wait_ge(s_z, c)
                    nc.tensor.matmul(ps[:, 3 - n], ssm_t[:, n], xt[:, c * BANK:(c + 1) * BANK],
                                     start=True, stop=True).then_inc(s_zps, 1)

            down(3)
            project(0)
            project(1)

            pe.wait_ge(s_ht, 12)
            turn_pe(2, 2, 5)
            turn_pe(2, 3, 6)
            project(2)
            project(3)

            def rows(b, n, slot):
                m = NSTATE * b + n
                first = isinstance(m, int) and m < 2
                pick = sel_b[:, bass.ds(n, 1)].to_broadcast([P, P])
                if not first:
                    pe.wait_ge(s_dbx, m - 1)
                for k in range(2):
                    mm = nc.tensor.matmul(ps[:, 2 * (slot % 2) + k], pick, bcp[:, 0, b * SEQ + k * BANK:b * SEQ + (k + 1) * BANK],
                                          start=True, stop=True)
                mm.then_inc(s_bb, 1)
                if not (isinstance(m, int) and m < 1):
                    pe.wait_ge(s_cs, m)
                for k in range(2):
                    mm = nc.tensor.matmul(ps[:, 4 + k], pick, bcp[:, 1, b * SEQ + k * BANK:b * SEQ + (k + 1) * BANK],
                                          start=True, stop=True)
                mm.then_inc(s_cb, 1)

            def total(b, n, slot):
                m = NSTATE * b + n
                first = isinstance(n, int) and n == 0
                last = isinstance(n, int) and n == NSTATE - 1
                pe.wait_ge(s_hc, m + 1)
                if first and b:
                    pe.wait_ge(s_skip, b)
                for k in range(2):
                    mm = nc.tensor.matmul(ps[:, 6 + k], ident[:], hc[:, slot, k * BANK:(k + 1) * BANK], start=first, stop=last)
                mm.then_inc(s_y3, 1)

            pe.wait_ge(s_selb, 1)
            pe.wait_ge(s_xt, 12)
            pe.wait_ge(s_z, CHUNKS)
            pe.wait_ge(s_bc, 2 * CHUNKS)
            def turn_y(b):
                pe.wait_ge(s_skip, b + 1)
                for g in (2 * b, 2 * b + 1):
                    for j in range(4):
                        t = 4 * g + j
                        mm = nc.tensor.transpose(ps[:, g, j * P:(j + 1) * P], zt[:, t * P:(t + 1) * P], ident[:])
                    mm.then_inc(s_yt, 1)

            LAG = RING - 1
            for b in range(BATCH):
                for n in range(2):
                    pe.wait_ge(s_bp3[n], b + 1)
                for n in range(RING):
                    rows(b, n, n)
                    if b and n < LAG:
                        total(b - 1, NSTATE - LAG + n, (n + 1) % RING)
                total(b, 0, 0)
                with pe.Fori(1, NSTATE // RING) as k:
                    for n in range(RING):
                        rows(b, RING * k + n, n)
                        total(b, RING * k + n - LAG, (n + 1) % RING)
            pe.wait_ge(s_dbx, BATCH * NSTATE)
            turn_y(0)
            for n in range(LAG):
                total(BATCH - 1, NSTATE - LAG + n, (n + 1) % RING)
            turn_y(1)
            pe.wait_ge(s_res, 12)
            turn_pe(3, 0)
            turn_pe(3, 1)

            def split_product(dst, w_h, w_l, r_h, r_l, start, stop):
                nc.tensor.matmul(dst, w_l, r_h, start=start, stop=False)
                nc.tensor.matmul(dst, w_h, r_l, start=False, stop=False)
                return nc.tensor.matmul(dst, w_h, r_h, start=False, stop=stop)

            def first_product(k, u):
                m = UNITS * k + u
                e, c = divmod(u, CHUNKS)
                w = slice(c * BANK, (c + 1) * BANK)
                if c == 0:
                    pe.wait_ge(s_w_l, 2 * k + e + 1)
                for h in range(HT):
                    pe.wait_ge(s_gelu, HT * m + h + 1)
                    cols = slice(h * P, (h + 1) * P)
                    split_product(ps[:, h], w12_h[:, e, 0, cols], w12_l[:, e, 0, cols], xh[:, w], xl[:, w],
                                  True, True).then_inc(s_l1, 1)

            def second_product(k, u):
                m = UNITS * k + u
                e = u // CHUNKS
                pe.wait_ge(s_moe, m + 1)
                for h in range(HT):
                    if h % 2 == 0:
                        pe.wait_ge(s_act_l, 2 * m + h // 2 + 1)
                    cols = slice(h * D, (h + 1) * D)
                    mm = split_product(ps[:, 6 + u % 2], w12_h[:, e, 1, cols], w12_l[:, e, 1, cols],
                                       act_h[:, u % 2, h], act_l[:, u % 2, h], h == 0, h == HT - 1)
                mm.then_inc(s_l2, 1)

            def turn_back(c):
                pe.wait_ge(s_moe, 2 + UNITS * (EXPERTS // 2) - CHUNKS + c + 1)
                if c >= 2:
                    pe.wait_ge(s_final, c - 1)
                for j in range(4):
                    mm = nc.tensor.transpose(ps[:, 4 + c % 2, j * P:(j + 1) * P], acc[:, c * BANK + j * P:c * BANK + (j + 1) * P], ident[:])
                mm.then_inc(s_back, 1)

            pe.sem_inc(s_l2, 2)
            turn_pe(3, 2)
            turn_pe(3, 3)
            pe.wait_ge(s_cs, BATCH * NSTATE)
            for t in range(TILES):
                pe.wait_ge(s_xt, 12 + t // 4 + 1)
                mm = nc.tensor.matmul(ps[:, 4, t * EXPERTS:(t + 1) * EXPERTS], xt[:, t * P:(t + 1) * P], wgate[:],
                                      start=True, stop=True)
            mm.then_inc(s_lgps, 1)
            pe.wait_ge(s_xh, CHUNKS)
            pe.wait_ge(s_xl, 2)
            first_product(0, 0)
            first_product(0, 1)
            second_product(0, 0)
            pe.wait_ge(s_comb, 1)
            for n in range(2):
                if n:
                    pe.wait_ge(s_combt, n)
                for t in range(8 * n, 8 * n + 8):
                    mm = nc.tensor.transpose(ps[0:EXPERTS, 4 + t // 4 % 2, (t % 4) * P:(t % 4 + 1) * P], comb[:, t, :], ident[:])
                mm.then_inc(s_combt_ps, 1)
            pe.wait_ge(s_combt, 2)
            for c in range(CHUNKS):
                if c >= 2:
                    pe.wait_ge(s_acc, c - 1)
                nc.tensor.matmul(ps[:, 4 + c % 2], b2[:], comb_t[:, c * BANK:(c + 1) * BANK], start=True, stop=True).then_inc(s_b2, 1)
            pe.wait_ge(s_xl, CHUNKS)
            for u in range(2, UNITS):
                first_product(0, u)
                second_product(0, u - 1)
            first_product(1, 0)
            second_product(0, UNITS - 1)
            with pe.Fori(1, EXPERTS // 2 - 1) as k:
                for u in range(1, UNITS):
                    first_product(k, u)
                    second_product(k, u - 1)
                first_product(k + 1, 0)
                second_product(k, UNITS - 1)
            last = EXPERTS // 2 - 1
            for u in range(1, UNITS):
                first_product(last, u)
                second_product(last, u - 1)
                if u >= CHUNKS + 2:
                    turn_back(u - CHUNKS - 2)
            second_product(last, UNITS - 1)
            for c in range(2, CHUNKS):
                turn_back(c)


def constants():
    f32 = np.float32
    inv = f32(1.0) / np.power(f32(10000.0), np.arange(0, HD, 2, dtype=f32) / f32(HD)).astype(f32)
    ang = (np.arange(SEQ, dtype=f32)[:, None] * inv[None, :]).astype(f32).astype(np.float64)
    ang = np.concatenate([ang, ang], axis=-1).T
    sign = np.where(np.arange(HD) % 2 == 0, -1.0, 1.0)[:, None]
    order = np.arange(P).reshape(HEADS // QUAD, QUAD, HD).transpose(0, 2, 1).ravel()
    perm = np.zeros((2, P, P), f32)
    perm[0, order, np.arange(P)] = 1
    perm[1, order ^ 1, np.arange(P)] = 1
    sel = np.zeros((P, NSTATE), f32)
    for part in (0, 64, 96):
        sel[part + np.arange(NSTATE), np.arange(NSTATE)] = 1
    tri = np.tril(np.ones((EXPERTS, EXPERTS), f32), -1)
    return {
        "ident": np.eye(P, dtype=f32),
        "perm": perm,
        "sel": sel,
        "tri": np.broadcast_to(tri, (P, EXPERTS, EXPERTS)).copy(),
        "cos": np.tile(np.cos(ang), (HEADS, 1)).astype(f32)[order],
        "sin": np.tile(np.sin(ang) * sign, (HEADS, 1)).astype(f32)[order],
    }


def kernel(**inputs):
    import concourse.bacc as bacc
    from concourse.bass_utils import run_bass_kernel_spmd

    nc = bacc.Bacc("TRN2", target_bir_lowering=False, num_devices=1)
    arrays, aps = {}, {}
    for name, a in {**inputs, **constants()}.items():
        a = np.ascontiguousarray(a)
        arrays["in_" + name] = a
        aps[name] = nc.dram_tensor("in_" + name, a.shape, mybir.dt.from_np(a.dtype), kind="ExternalInput").ap()
    out = nc.dram_tensor("out_x", (BATCH, SEQ, D), F32, kind="ExternalOutput").ap()
    build_kernel(nc, aps, out)
    r = run_bass_kernel_spmd(nc, [arrays], core_ids=[0])
    return r.results[0]["out_x"]
```
